# Optimizing a Trainium2 kernel written in Bass

```python
import numpy as np
import jax
import jax.numpy as jnp

def _softmax(x, axis=-1):
    return jax.nn.softmax(x, axis=axis)

def _gelu(x):
    return jax.nn.gelu(x, approximate=True)

def _silu(x):
    return jax.nn.silu(x)

def _sigmoid(x):
    return jax.nn.sigmoid(x)

def _layernorm(x, axis=-1, eps=1e-05):
    m = jnp.mean(x, axis=axis, keepdims=True)
    v = jnp.var(x, axis=axis, keepdims=True)
    return (x - m) / jnp.sqrt(v + eps)

def _scatter_add(tgt, idx, src, axis=0):
    return tgt.at[idx].add(src)

def _segment_sum(src, seg, n):
    return jax.ops.segment_sum(src, seg, n)
kernel_name = 'mk_vit_tower_d1_tok_img1024_r4_37fb39'

def setup_inputs(seed: int=0):
    np.random.seed(seed)
    _w = jnp.asarray

    def _rec_inputs():
        import jax
        import jax.numpy as jnp
        _rk = jax.random.key(seed)
        x = -0.00016672 + 0.999947 * jax.random.normal(jax.random.fold_in(_rk, 1), (64, 3, 96, 96), jnp.float32)
        return x
    x = _rec_inputs()

    def _L0_tok_setup():
        import jax, jax.numpy as jnp
        import numpy as np
        B, C, H, W = (64, 3, 96, 96)
        P = 16
        NP = H // P * (W // P)
        PD = C * P * P
        ED = 256
        NCLS = 1

        def _layernorm(x, g, b, eps=1e-05):
            mu = jnp.mean(x, axis=-1, keepdims=True)
            var = jnp.mean(jnp.square(x - mu), axis=-1, keepdims=True)
            return (x - mu) * jax.lax.rsqrt(var + eps) * g + b
        key = jax.random.key(seed)
        ks = jax.random.split(key, 8)
        x = jax.random.normal(ks[0], (B, C, H, W), dtype=jnp.float32)
        ln1_g = jnp.ones((PD,), jnp.float32)
        ln1_b = jnp.zeros((PD,), jnp.float32)
        W_proj = jax.random.normal(ks[1], (PD, ED), jnp.float32) / np.sqrt(PD)
        b_proj = jnp.zeros((ED,), jnp.float32)
        ln2_g = jnp.ones((ED,), jnp.float32)
        ln2_b = jnp.zeros((ED,), jnp.float32)
        cls_token = jax.random.normal(ks[2], (1, NCLS, ED), jnp.float32)
        pos_emb = jax.random.normal(ks[3], (1, NP + NCLS, ED), jnp.float32)
        return {'x': x, 'ln1_g': ln1_g, 'ln1_b': ln1_b, 'W_proj': W_proj, 'b_proj': b_proj, 'ln2_g': ln2_g, 'ln2_b': ln2_b, 'cls_token': cls_token, 'pos_emb': pos_emb}
    _L0_tok_all = _L0_tok_setup()
    _L0_tok_in = {k: v for k, v in _L0_tok_all.items() if k in ('ln1_g', 'ln1_b', 'W_proj', 'b_proj', 'ln2_g', 'ln2_b', 'cls_token', 'pos_emb')}
    del _L0_tok_all

    def _L0_attn_setup():
        import jax, jax.numpy as jnp
        import numpy as np
        NUM_HEAD = 16
        D_Q = 128
        D_KV = 128
        ROPE_BASE = 10000.0

        def _cos_sin(seq_len, dim):
            pos = jnp.arange(seq_len, dtype=jnp.float32)[:, None]
            ids = jnp.arange(dim // 2, dtype=jnp.float32)
            theta = ROPE_BASE ** (-2.0 * ids) / (dim // 2)
            r = pos * theta[None, :]
            return (jnp.cos(r), jnp.sin(r))

        def _rope(x, cos, sin):
            b, s, d = x.shape
            xv = x.reshape(b, s, d // 2, 2)
            x0, x1 = (xv[..., 0], xv[..., 1])
            out = jnp.stack([x0 * cos - x1 * sin, x1 * cos + x0 * sin], axis=-1)
            return out.reshape(b, s, d)
        key = jax.random.key(seed)
        ks = jax.random.split(key, 10)
        d_model, d_q, d_kv = (256, D_Q, D_KV)
        b, s = (2, 512)
        w = lambda k, i, o: jax.random.normal(k, (i, o), dtype=jnp.float32) * 0.02
        return {'x': jax.random.normal(ks[0], (b, s, d_model), dtype=jnp.float32), 'Wd_q_w': w(ks[1], d_model, d_q), 'Wd_q_b': jnp.zeros((d_q,), jnp.float32), 'Wu_q_w': w(ks[2], d_q, d_model), 'Wu_q_b': jnp.zeros((d_model,), jnp.float32), 'Wq_r_w': w(ks[3], d_q, d_model), 'Wq_r_b': jnp.zeros((d_model,), jnp.float32), 'Wk_r_w': w(ks[4], d_model, d_model), 'Wk_r_b': jnp.zeros((d_model,), jnp.float32), 'Wd_kv_w': w(ks[5], d_model, d_kv), 'Wd_kv_b': jnp.zeros((d_kv,), jnp.float32), 'Wu_k_w': w(ks[6], d_kv, d_model), 'Wu_k_b': jnp.zeros((d_model,), jnp.float32), 'Wu_v_w': w(ks[7], d_kv, d_model), 'Wu_v_b': jnp.zeros((d_model,), jnp.float32), 'Wo_w': w(ks[8], d_model, d_model), 'Wo_b': jnp.zeros((d_model,), jnp.float32)}
    _L0_attn_all = _L0_attn_setup()
    _L0_attn_in = {k: v for k, v in _L0_attn_all.items() if k in ('Wd_q_w', 'Wd_q_b', 'Wu_q_w', 'Wu_q_b', 'Wq_r_w', 'Wq_r_b', 'Wk_r_w', 'Wk_r_b', 'Wd_kv_w', 'Wd_kv_b', 'Wu_k_w', 'Wu_k_b', 'Wu_v_w', 'Wu_v_b', 'Wo_w', 'Wo_b')}
    del _L0_attn_all

    def _L0_ffn_setup():
        import jax, jax.numpy as jnp
        import numpy as np
        E, K = (8, 2)
        B, S, H, F = (2, 512, 256, 1024)
        EPS = 1e-12

        def _expert_ffn(xf, Wi_e, bi_e, Wg_e, bg_e, Wo_e, bo_e, g_e, b_e):
            h = jax.nn.gelu(xf @ Wi_e + bi_e, approximate=False) * jax.nn.sigmoid(xf @ Wg_e + bg_e)
            r = xf + (h @ Wo_e + bo_e)
            mu = jnp.mean(r, axis=-1, keepdims=True)
            var = jnp.mean(jnp.square(r - mu), axis=-1, keepdims=True)
            return (r - mu) * jax.lax.rsqrt(var + EPS) * g_e + b_e
        key = jax.random.key(seed)
        ks = jax.random.split(key, 8)
        s = 0.02
        return {'x': jax.random.normal(ks[0], (B, S, H), jnp.float32), 'Wr': jax.random.normal(ks[1], (H, E), jnp.float32) * s, 'br': jnp.zeros((E,), jnp.float32), 'Wi': jax.random.normal(ks[2], (E, H, F), jnp.float32) * s, 'bi': jnp.zeros((E, F), jnp.float32), 'Wg': jax.random.normal(ks[3], (E, H, F), jnp.float32) * s, 'bg': jnp.zeros((E, F), jnp.float32), 'Wo': jax.random.normal(ks[4], (E, F, H), jnp.float32) * s, 'bo': jnp.zeros((E, H), jnp.float32), 'gamma': jnp.ones((E, H), jnp.float32), 'beta': jnp.zeros((E, H), jnp.float32)}
    _L0_ffn_all = _L0_ffn_setup()
    _L0_ffn_in = {k: v for k, v in _L0_ffn_all.items() if k in ('Wr', 'br', 'Wi', 'bi', 'Wg', 'bg', 'Wo', 'bo', 'gamma', 'beta')}
    del _L0_ffn_all
    return {'x': x, 'L0_tok_ln1_g': _L0_tok_in['ln1_g'], 'L0_tok_ln1_b': _L0_tok_in['ln1_b'], 'L0_tok_W_proj': _L0_tok_in['W_proj'], 'L0_tok_b_proj': _L0_tok_in['b_proj'], 'L0_tok_ln2_g': _L0_tok_in['ln2_g'], 'L0_tok_ln2_b': _L0_tok_in['ln2_b'], 'L0_tok_cls_token': _L0_tok_in['cls_token'], 'L0_tok_pos_emb': _L0_tok_in['pos_emb'], 'L0_attn_Wd_q_w': _L0_attn_in['Wd_q_w'], 'L0_attn_Wd_q_b': _L0_attn_in['Wd_q_b'], 'L0_attn_Wu_q_w': _L0_attn_in['Wu_q_w'], 'L0_attn_Wu_q_b': _L0_attn_in['Wu_q_b'], 'L0_attn_Wq_r_w': _L0_attn_in['Wq_r_w'], 'L0_attn_Wq_r_b': _L0_attn_in['Wq_r_b'], 'L0_attn_Wk_r_w': _L0_attn_in['Wk_r_w'], 'L0_attn_Wk_r_b': _L0_attn_in['Wk_r_b'], 'L0_attn_Wd_kv_w': _L0_attn_in['Wd_kv_w'], 'L0_attn_Wd_kv_b': _L0_attn_in['Wd_kv_b'], 'L0_attn_Wu_k_w': _L0_attn_in['Wu_k_w'], 'L0_attn_Wu_k_b': _L0_attn_in['Wu_k_b'], 'L0_attn_Wu_v_w': _L0_attn_in['Wu_v_w'], 'L0_attn_Wu_v_b': _L0_attn_in['Wu_v_b'], 'L0_attn_Wo_w': _L0_attn_in['Wo_w'], 'L0_attn_Wo_b': _L0_attn_in['Wo_b'], 'L0_ffn_Wr': _L0_ffn_in['Wr'], 'L0_ffn_br': _L0_ffn_in['br'], 'L0_ffn_Wi': _L0_ffn_in['Wi'], 'L0_ffn_bi': _L0_ffn_in['bi'], 'L0_ffn_Wg': _L0_ffn_in['Wg'], 'L0_ffn_bg': _L0_ffn_in['bg'], 'L0_ffn_Wo': _L0_ffn_in['Wo'], 'L0_ffn_bo': _L0_ffn_in['bo'], 'L0_ffn_gamma': _L0_ffn_in['gamma'], 'L0_ffn_beta': _L0_ffn_in['beta']}

def reference(x, L0_tok_ln1_g, L0_tok_ln1_b, L0_tok_W_proj, L0_tok_b_proj, L0_tok_ln2_g, L0_tok_ln2_b, L0_tok_cls_token, L0_tok_pos_emb, L0_attn_Wd_q_w, L0_attn_Wd_q_b, L0_attn_Wu_q_w, L0_attn_Wu_q_b, L0_attn_Wq_r_w, L0_attn_Wq_r_b, L0_attn_Wk_r_w, L0_attn_Wk_r_b, L0_attn_Wd_kv_w, L0_attn_Wd_kv_b, L0_attn_Wu_k_w, L0_attn_Wu_k_b, L0_attn_Wu_v_w, L0_attn_Wu_v_b, L0_attn_Wo_w, L0_attn_Wo_b, L0_ffn_Wr, L0_ffn_br, L0_ffn_Wi, L0_ffn_bi, L0_ffn_Wg, L0_ffn_bg, L0_ffn_Wo, L0_ffn_bo, L0_ffn_gamma, L0_ffn_beta):
    import jax
    import jax.numpy as jnp

    def _L0_tok_ref(x, ln1_g, ln1_b, W_proj, b_proj, ln2_g, ln2_b, cls_token, pos_emb):
        import jax, jax.numpy as jnp
        import numpy as np
        B, C, H, W = (64, 3, 96, 96)
        P = 16
        NP = H // P * (W // P)
        PD = C * P * P
        ED = 256
        NCLS = 1

        def _layernorm(x, g, b, eps=1e-05):
            mu = jnp.mean(x, axis=-1, keepdims=True)
            var = jnp.mean(jnp.square(x - mu), axis=-1, keepdims=True)
            return (x - mu) * jax.lax.rsqrt(var + eps) * g + b
        b = x.shape[0]
        h, w = (H // P, W // P)
        patches = x.reshape(b, C, h, P, w, P)
        patches = patches.transpose(0, 2, 4, 3, 5, 1).reshape(b, h * w, P * P * C)
        z = _layernorm(patches, ln1_g, ln1_b)
        z = jnp.einsum('bnp,pe->bne', z, W_proj) + b_proj
        z = _layernorm(z, ln2_g, ln2_b)
        cls = jnp.broadcast_to(cls_token, (b, NCLS, ED))
        z = jnp.concatenate([cls, z], axis=1)
        z = z + pos_emb
        return z

    def _L0_attn_ref(x, Wd_q_w, Wd_q_b, Wu_q_w, Wu_q_b, Wq_r_w, Wq_r_b, Wk_r_w, Wk_r_b, Wd_kv_w, Wd_kv_b, Wu_k_w, Wu_k_b, Wu_v_w, Wu_v_b, Wo_w, Wo_b):
        import jax, jax.numpy as jnp
        import numpy as np
        NUM_HEAD = 16
        D_Q = 128
        D_KV = 128
        ROPE_BASE = 10000.0

        def _cos_sin(seq_len, dim):
            pos = jnp.arange(seq_len, dtype=jnp.float32)[:, None]
            ids = jnp.arange(dim // 2, dtype=jnp.float32)
            theta = ROPE_BASE ** (-2.0 * ids) / (dim // 2)
            r = pos * theta[None, :]
            return (jnp.cos(r), jnp.sin(r))

        def _rope(x, cos, sin):
            b, s, d = x.shape
            xv = x.reshape(b, s, d // 2, 2)
            x0, x1 = (xv[..., 0], xv[..., 1])
            out = jnp.stack([x0 * cos - x1 * sin, x1 * cos + x0 * sin], axis=-1)
            return out.reshape(b, s, d)
        b, s, d_model = x.shape
        h = NUM_HEAD
        hd = d_model // h
        scale = jnp.sqrt(jnp.float32(h + D_KV + D_Q))

        def heads(t):
            return t.reshape(b, s, h, hd).transpose(0, 2, 1, 3)
        cos, sin = _cos_sin(s, d_model)
        ct_q = x @ Wd_q_w + Wd_q_b
        qt_c = heads(ct_q @ Wu_q_w + Wu_q_b)
        qt_r = heads(_rope(ct_q @ Wq_r_w + Wq_r_b, cos, sin))
        query = qt_c + qt_r
        ct_kv = x @ Wd_kv_w + Wd_kv_b
        kt_c = heads(ct_kv @ Wu_k_w + Wu_k_b)
        kt_r = heads(_rope(x @ Wk_r_w + Wk_r_b, cos, sin))
        key = kt_c + kt_r
        value = heads(ct_kv @ Wu_v_w + Wu_v_b)
        attn = jnp.einsum('bhqd,bhkd->bhqk', query, key) / scale
        attn = jax.nn.softmax(attn, axis=-1)
        out = jnp.einsum('bhqk,bhkd->bhqd', attn, value)
        out = out.transpose(0, 2, 1, 3).reshape(b, s, d_model)
        return out @ Wo_w + Wo_b

    def _L0_ffn_ref(x, Wr, br, Wi, bi, Wg, bg, Wo, bo, gamma, beta):
        import jax, jax.numpy as jnp
        import numpy as np
        E, K = (8, 2)
        B, S, H, F = (2, 512, 256, 1024)
        EPS = 1e-12

        def _expert_ffn(xf, Wi_e, bi_e, Wg_e, bg_e, Wo_e, bo_e, g_e, b_e):
            h = jax.nn.gelu(xf @ Wi_e + bi_e, approximate=False) * jax.nn.sigmoid(xf @ Wg_e + bg_e)
            r = xf + (h @ Wo_e + bo_e)
            mu = jnp.mean(r, axis=-1, keepdims=True)
            var = jnp.mean(jnp.square(r - mu), axis=-1, keepdims=True)
            return (r - mu) * jax.lax.rsqrt(var + EPS) * g_e + b_e
        b, s, h = x.shape
        T = b * s
        xf = x.reshape(T, h)
        probs = jax.nn.softmax(xf @ Wr + br, axis=-1)
        topw, topi = jax.lax.top_k(probs, K)
        topw = topw / jnp.sum(topw, axis=-1, keepdims=True)
        c = jnp.zeros((T, E), x.dtype).at[jnp.arange(T)[:, None], topi].set(topw)
        y = jax.vmap(_expert_ffn, in_axes=(None, 0, 0, 0, 0, 0, 0, 0, 0))(xf, Wi, bi, Wg, bg, Wo, bo, gamma, beta)
        out = jnp.einsum('te,eth->th', c, y)
        return out.reshape(b, s, h)
    h = _L0_tok_ref(x, L0_tok_ln1_g, L0_tok_ln1_b, L0_tok_W_proj, L0_tok_b_proj, L0_tok_ln2_g, L0_tok_ln2_b, L0_tok_cls_token, L0_tok_pos_emb)
    h = h + _L0_attn_ref(_layernorm(h, axis=-1), L0_attn_Wd_q_w, L0_attn_Wd_q_b, L0_attn_Wu_q_w, L0_attn_Wu_q_b, L0_attn_Wq_r_w, L0_attn_Wq_r_b, L0_attn_Wk_r_w, L0_attn_Wk_r_b, L0_attn_Wd_kv_w, L0_attn_Wd_kv_b, L0_attn_Wu_k_w, L0_attn_Wu_k_b, L0_attn_Wu_v_w, L0_attn_Wu_v_b, L0_attn_Wo_w, L0_attn_Wo_b)
    h = h + _L0_ffn_ref(_layernorm(h, axis=-1), L0_ffn_Wr, L0_ffn_br, L0_ffn_Wi, L0_ffn_bi, L0_ffn_Wg, L0_ffn_bg, L0_ffn_Wo, L0_ffn_bo, L0_ffn_gamma, L0_ffn_beta)
    return h

_drawn_inputs = setup_inputs


def setup_inputs(seed=0):
    import zlib

    import numpy as np

    out = dict(_drawn_inputs(seed))
    spreads = {'L0_tok_ln1_g': (1.0, 0.2),
     'L0_tok_ln1_b': (0.0, 0.1),
     'L0_tok_b_proj': (0.0, 0.1),
     'L0_tok_ln2_g': (1.0, 0.2),
     'L0_tok_ln2_b': (0.0, 0.1),
     'L0_attn_Wd_q_b': (0.0, 0.8),
     'L0_attn_Wu_q_b': (0.0, 0.8),
     'L0_attn_Wq_r_b': (0.0, 0.8),
     'L0_attn_Wk_r_b': (0.0, 0.8),
     'L0_attn_Wd_kv_b': (0.0, 0.8),
     'L0_attn_Wu_k_b': (0.0, 0.8),
     'L0_attn_Wu_v_b': (0.0, 0.323),
     'L0_attn_Wo_b': (0.0, 0.1),
     'L0_ffn_br': (0.0, 0.1),
     'L0_ffn_bi': (0.0, 0.8),
     'L0_ffn_bg': (0.0, 0.8),
     'L0_ffn_bo': (0.0, 0.27),
     'L0_ffn_gamma': (1.0, 0.2),
     'L0_ffn_beta': (0.0, 0.28)}
    factors = {'L0_attn_Wd_q_w': 8.0,
     'L0_attn_Wu_q_w': 8.0,
     'L0_attn_Wq_r_w': 8.0,
     'L0_attn_Wk_r_w': 8.0,
     'L0_attn_Wd_kv_w': 8.0,
     'L0_attn_Wu_k_w': 8.0,
     'L0_attn_Wu_v_w': 8.0,
     'L0_ffn_Wi': 3.453,
     'L0_ffn_Wg': 8.0,
     'L0_ffn_Wo': 3.199}
    for name, (base, spread) in spreads.items():
        noise = np.random.default_rng([zlib.crc32(name.encode()), seed]).standard_normal(out[name].shape)
        drawn = base * np.exp(spread * noise) if base else spread * noise
        out[name] = jnp.asarray(drawn.astype(out[name].dtype))
    for name, factor in factors.items():
        out[name] = (out[name] * factor).astype(out[name].dtype)
    return out
```

```python
import concourse.bass as bass
from concourse import mybir
from contextlib import ExitStack

IMAGES, PATCHES, TOKENS, DIM = 64, 36, 37, 256
PATCH_DIM = 768
ALL_TOKENS = IMAGES * TOKENS
PER_GROUP = 3
GROUPS = -(-IMAGES // PER_GROUP)
ROWS = PER_GROUP * TOKENS
HEADS, HEAD_DIM = 16, 16
LATENT = 128
EXPERTS, TOP, FFN = 8, 2, 1024
SLOT = 128
SLOTS = (ALL_TOKENS * TOP + EXPERTS * (SLOT - 1)) // SLOT
CHUNKS = 8
CHUNK = ALL_TOKENS // CHUNKS
CHUNK_IMAGES = CHUNK // TOKENS
SCORE_SCALE = float(1.0 / (HEADS + 2 * LATENT) ** 0.5)
HEAD_SPAN = TOKENS * (HEADS // 2)
ROUND = 4
C_IDENT, C_BEFORE, C_ONES, C_HEAD, C_IMAGE, C_PATCH, C_RANK, C_VALID, C_THRESH, C_SLOTNO, C_SIGN = range(11)


def constant_columns():
    widths = [128, ROWS, ROWS, 8, 3, 2, GROUPS * 8, GROUPS, 8 * 19, SLOTS * 8, SLOTS * 8]
    start, out = 0, []
    for w in widths:
        out.append((start, start + w))
        start += w
    return out, start


def images_of(g):
    return IMAGES - PER_GROUP * (GROUPS - 1) if isinstance(g, int) and g == GROUPS - 1 else PER_GROUP


def build(nc, patches, consts, w_proj, rows_pack, row_tables, pos, wd, wq, wk, wv_o, cols_pack, rope, w_router,
          wi, wg, wo, expert_bias, expert_rows, out, scr_h, slots_in, slots_out, bias_parts, stage_limit=9):
    f32, f32r, i32 = mybir.dt.float32, mybir.dt.float32r, mybir.dt.int32
    ALU, ACT, AX = mybir.AluOpType, mybir.ActivationFunctionType, mybir.AxisListType
    ds = bass.ds
    cols, const_width = constant_columns()

    whole = ExitStack()
    with whole:
        def sb(name, shape, dt=f32, ctx=whole):
            return ctx.enter_context(nc.sbuf_tensor(name, shape, dt))

        def pb(name, shape, ctx, dt=f32):
            return ctx.enter_context(nc.psum_tensor(name, shape, dt))

        def sem(name):
            return whole.enter_context(nc.semaphore(name))

        const = sb("const", [128, const_width])

        def cst(which, p=128):
            a, b = cols[which]
            return const[0:p, a:b]

        ident = cst(C_IDENT)
        choice_weight = sb("choice_weight", [ROWS, TOP, GROUPS])
        choice_row = sb("choice_row", [ROWS, TOP, GROUPS], i32)
        slot_expert = sb("slot_expert", [1, SLOTS], i32)
        slot_buffer = sb("slot_buffer", [1, SLOTS], i32)
        tiles_done = sb("tiles_done", [1, EXPERTS], i32)

        early = ExitStack()
        def eb(name, shape, dt=f32):
            return sb(name, shape, dt, early)
        resid = eb("resid", [ROWS, GROUPS * DIM])
        x1T = eb("x1T", [128, 2, ALL_TOKENS])
        qT = eb("qT", [128, 2, ALL_TOKENS])
        kT = eb("kT", [128, 2, ALL_TOKENS])
        latT = eb("latT", [128, ALL_TOKENS])
        wd_sb = eb("wd_sb", [128, 2, 2 * LATENT])
        wq_sb = eb("wq_sb", [128, 3 * DIM])
        wk_sb = eb("wk_sb", [128, 5, DIM])
        wvo_sb = eb("wvo_sb", [128, 3, DIM])
        wr_sb = eb("wr_sb", [128, 2, EXPERTS])
        colb = eb("colb", [128, 14])
        rope_sb = eb("rope_sb", [128, 2, 2, TOKENS])
        rowb = eb("rowb", [ROWS, 6 * DIM + EXPERTS])
        ln2_g, ln2_b, cls_row, b_proj, b_v, b_o = (rowb[:, i * DIM:(i + 1) * DIM] for i in range(6))
        b_router = rowb[:, 6 * DIM:6 * DIM + EXPERTS]
        pos_sb = eb("pos_sb", [ROWS, DIM])
        ln4_stats = eb("ln4_stats", [ROWS, GROUPS, 6])

        one = ExitStack()
        def ob(name, shape, dt=f32):
            return sb(name, shape, dt, one)
        wproj_sb = ob("wproj_sb", [128, 6, DIM])
        ln1_rows = ob("ln1_rows", [ROWS, 2, PATCH_DIM])
        x_in = ob("x_in", [ROWS, 2, PATCH_DIM])
        x_norm = ob("x_norm", [ROWS, 2, PATCH_DIM])
        x_aff = ob("x_aff", [ROWS, 2, PATCH_DIM])
        x_affT = ob("x_affT", [128, 2, 6, ROWS])
        z_sb = ob("z_sb", [ROWS, 2, DIM])
        z_norm = ob("z_norm", [ROWS, 2, DIM])
        x1 = ob("x1", [ROWS, 2, DIM])
        add_rows = ob("add_rows", [ROWS, DIM])
        mul_rows = ob("mul_rows", [ROWS, DIM])
        tmp_rows = ob("tmp_rows", [ROWS, DIM])
        ln1_st = ob("ln1_st", [ROWS, 2, 2, 6])
        ln2_st = ob("ln2_st", [ROWS, 2, 6])
        ln3_st = ob("ln3_st", [ROWS, 2, 6])
        ln_mv = ob("ln_mv", [ROWS, 2, 3, 2])
        ln_ve = ob("ln_ve", [ROWS, 2, 3])
        ln_sd = ob("ln_sd", [ROWS, 2, 3])
        ln_r0 = ob("ln_r0", [ROWS, 2, 3])
        ln_t = ob("ln_t", [ROWS, 2, 3, 3])
        ln_rs = ob("ln_rs", [ROWS, 2, 3])
        one.close()
        two = ExitStack()
        ctq = sb("ctq", [128, 2, CHUNK], f32, two)
        rot = sb("rot", [128, 2, 3, CHUNK], f32, two)
        two.close()
        three = ExitStack()
        def tb(name, shape, dt=f32):
            return sb(name, shape, dt, three)
        k_blocks = tb("k_blocks", [128, 2, 2, PER_GROUP * HEAD_SPAN])
        q_pad = tb("q_pad", [128, 2, 2, PER_GROUP * (ROWS + TOKENS)])
        lat_g = tb("lat_g", [128, 2, ROWS])
        shifted = tb("shifted", [ROWS, 2, HEADS * TOKENS])
        probs = tb("probs", [ROWS, 2, HEADS * TOKENS])
        p_wide = tb("p_wide", [ROWS, 2, HEADS * ROWS])
        pT = tb("pT", [ROWS, 2, HEADS * ROWS])
        v_one = tb("v_one", [ROWS, 2, HEADS, HEAD_DIM + 1])
        top = tb("top", [ROWS, 2, HEADS])
        inv_sum = tb("inv_sum", [ROWS, 2, HEADS])
        att = tb("att", [ROWS, 2, DIM])
        attT = tb("attT", [128, 2, 2, ROWS])
        att_b = tb("att_b", [ROWS, 2, DIM])
        three.close()
        four = ExitStack()
        def fb(name, shape, dt=f32):
            return sb(name, shape, dt, four)
        x2 = fb("x2", [ROWS, GROUPS, DIM])
        x2T = fb("x2T", [128, 2, 2, ROWS])
        mv4 = fb("mv4", [ROWS, GROUPS, 2])
        sc4 = fb("sc4", [ROWS, 8, GROUPS])
        NE = GROUPS * EXPERTS
        lg = fb("lg", [ROWS, 16, NE])
        small = fb("small", [ROWS, 12, GROUPS])
        cnt = fb("cnt", [ROWS, 8, EXPERTS])
        over = fb("over", [ROWS, EXPERTS * 19])
        smap = fb("smap", [1, 2, SLOTS * 8])
        smap_sum = fb("smap_sum", [1, 2, SLOTS])
        bias_raw = fb("bias_raw", [128, 128])
        bias_hl = fb("bias_hl", [128, 2, 128], f32r)
        zero_rows = fb("zero_rows", [128, 1024])
        four.close()
        early.close()
        late = ExitStack()
        def lb(name, shape, dt=f32):
            return sb(name, shape, dt, late)
        stage = lb("stage", [128, 2, 2048])
        WSZ = 2048
        wi_hl = [lb(f"wi_{p}", [128, 2 * WSZ], f32r) for p in ("hi", "lo")]
        wg_hl = [lb(f"wg_{p}", [128, 2 * WSZ], f32r) for p in ("hi", "lo")]
        wo_hl = [lb(f"wo_{p}", [128, 2 * WSZ], f32r) for p in ("hi", "lo")]
        bias_sb = lb("bias_sb", [2, 2 * WSZ], f32r)
        ones2 = lb("ones2", [2, 128], f32r)
        exp_rows = lb("exp_rows", [128, 3 * EXPERTS * DIM])
        xs = lb("xs", [128, 4, DIM])
        xsT = [lb(f"xsT_{p}", [128, 2, 2, 128], f32r) for p in ("hi", "lo")]
        act_u = lb("act_u", [128, 2, 512])
        act_g = lb("act_g", [128, 2, 512])
        hid = lb("hid", [128, 2, 512])
        hidT = [lb(f"hidT_{p}", [128, 2, 8, 128], f32r) for p in ("hi", "lo")]
        y_res = lb("y_res", [128, 2, 3, DIM])
        y_out = lb("y_out", [128, 2, DIM])
        y_st = lb("y_st", [128, 6])
        y_mv = lb("y_mv", [128, 2])
        y_sc = lb("y_sc", [128, 12])
        y_int = lb("y_int", [128, 2], i32)
        late.close()
        last = ExitStack()
        got = sb("got", [ROWS, 4, TOP, DIM], f32, last)
        res_in = sb("res_in", [ROWS, 4, DIM], f32, last)
        sum_a = sb("sum_a", [ROWS, 4, DIM], f32, last)
        sum_b = sb("sum_b", [ROWS, 4, DIM], f32, last)
        last.close()

        bank = [pb(f"bank{i}", [128, 512], whole) for i in range(8)]

        S = {n: sem(n) for n in (
            "const_loaded wproj_loaded rows_loaded weights_loaded x_loaded0 x_loaded1 setup_done setup_c "
            "ln1_c ln2_c ln3_c ln_c std_ready x_norm_ready x_aff_c xT_ps x_affT_ready z_ps z_norm_ready resid_c "
            "x1_ready x1T_ps x1T_ready "
            "lat_ps lat_ready rope_ps rope_c "
            "attn_zero keys_ready queries_ready scores_ps v_ps v_ready max_c exp_ready p_wide_ready "
            "pT_ps pT_act pT_dve pv_ps att_c attT_ps attT_ready proj_ps resid_done "
            "ln4_c x2_ready x2T_ps x2T_ready logits_ps sd4_ready route_c route_ps route_in exp4_ready "
            "bias_loaded bias_c bias_stored zero_ready zeroed hres_stored "
            "scattered plan_ready "
            "stage_loaded0 stage_loaded1 stage_used weights_ready bias_ready exp_rows_loaded ones_ready "
            "xs_loaded0 xs_loaded1 xs_loaded2 xs_loaded3 xs_done xsT_ps xs_hi xs_lo ug_ps gelu_c hid_ready hidT_ps hid_hi hid_lo y_ps y_c y_out_ready y_stored0 y_stored1 "
            "got_y0 got_y1 got_y2 got_y3 res_loaded0 res_loaded1 res_loaded2 res_loaded3 sum_c out_stored0 out_stored1 out_stored2 out_stored3").split()}

        block = whole.enter_context(nc.Block())

        def need(eng, name, n):
            if isinstance(n, int) and n <= 0:
                return
            eng.wait_ge(S[name], n)

        def need_first(eng, name, n):
            if isinstance(n, int) and n <= 0:
                return
            eng.wait_ge(S[name], n)
            eng.nop(nofuse=True)

        def sweep(eng, head, tail, total, body):
            for s in range(min(head, total)):
                body(s, s % 2, s // 2)
            if tail > head:
                with eng.Fori(head // 2, tail // 2) as half:
                    body(half * 2, 0, half)
                    body(half * 2 + 1, 1, half)
            for s in range(tail, total):
                body(s, s % 2, s // 2)

        def live(g):
            return not isinstance(g, int) or 0 <= g < GROUPS

        def rows_of(g):
            return images_of(g) * TOKENS

        P1 = dict(head=6, tail=20, total=GROUPS + 5)
        P3 = dict(head=4, tail=20, total=GROUPS + 3)
        P2 = dict(head=2, tail=8, total=CHUNKS)
        def x_loaded_after(g, pair):
            return pair * (16 * PER_GROUP) + 16 * images_of(g)

        @block.sync
        def _(sp):
            def load_x(g, par):
                need(sp, "x_norm_ready", g - 1)
                for i in range(images_of(g)):
                    sp.dma_start(x_in[TOKENS * i + 1:TOKENS * (i + 1), par, :],
                                 patches[ds((g * PER_GROUP + i) * PATCHES, PATCHES), :]).then_inc(S[f"x_loaded{par}"], 16)

            sp.wait_ge(S["setup_done"], 1)
            load_x(0, 0)
            sp.dma_start(const[:, :], consts).then_inc(S["const_loaded"], 16)
            sp.dma_start(ln1_rows[:, :, :], row_tables.partition_broadcast(ROWS)).then_inc(S["rows_loaded"], 16)
            load_x(1, 1)
            sp.dma_start(rowb[:, :], rows_pack.partition_broadcast(ROWS)).then_inc(S["rows_loaded"], 16)
            for i in range(PER_GROUP):
                sp.dma_start(pos_sb[TOKENS * i:TOKENS * (i + 1), :], pos).then_inc(S["rows_loaded"], 16)
            sp.dma_start(wproj_sb[:, :, :], w_proj.rearrange("(k p) n -> p k n", p=128)).then_inc(S["wproj_loaded"], 16)
            sp.dma_start(wd_sb[:, :, :], wd.rearrange("(k p) n -> p k n", p=128)).then_inc(S["weights_loaded"], 16)
            sp.dma_start(wq_sb[:, :], wq).then_inc(S["weights_loaded"], 16)
            sp.dma_start(wk_sb[:, :, :], wk.rearrange("(k p) n -> p k n", p=128)).then_inc(S["weights_loaded"], 16)
            sp.dma_start(wvo_sb[:, :, :], wv_o.rearrange("(k p) n -> p k n", p=128)).then_inc(S["weights_loaded"], 16)
            sp.dma_start(wr_sb[:, :, :], w_router.rearrange("(k p) n -> p k n", p=128)).then_inc(S["weights_loaded"], 16)
            sp.dma_start(colb[:, :], cols_pack).then_inc(S["weights_loaded"], 16)
            sp.dma_start(rope_sb[:, :, :, :], rope.rearrange("t (k p) n -> p t k n", p=128)).then_inc(S["weights_loaded"], 16)

            with sp.Fori(1, GROUPS // 2 - 1) as half:
                load_x(half * 2, 0)
                load_x(half * 2 + 1, 1)
            load_x(GROUPS - 2, 0)
            load_x(GROUPS - 1, 1)

            sp.wait_ge(S["resid_done"], GROUPS)
            full = (GROUPS - 1) * ROWS
            sp.dma_start(scr_h[0:full, :].rearrange("(g p) d -> p g d", p=ROWS),
                         resid[:, 0:(GROUPS - 1) * DIM].rearrange("p (g d) -> p g d", d=DIM)).then_inc(S["hres_stored"], 16)
            sp.dma_start(scr_h[full:ALL_TOKENS, :], resid[0:ALL_TOKENS - full, (GROUPS - 1) * DIM:]).then_inc(S["hres_stored"], 16)
            sp.wait_ge(S["zero_ready"], 1)
            per = 128 * 4
            for i in range(SLOTS * SLOT // per):
                sp.dma_start(slots_in[i * per:(i + 1) * per, :].rearrange("(p r) d -> p (r d)", p=128),
                             zero_rows[:, :]).then_inc(S["zeroed"], 16)
            sp.dma_start(bias_raw[:, :], expert_bias).then_inc(S["bias_loaded"], 16)
            sp.wait_ge(S["bias_c"], 2)
            sp.dma_start(bias_parts.rearrange("t (p n) -> p t n", n=128), bias_hl[:, :, :].bitcast(f32)).then_inc(S["bias_stored"], 16)
            sp.wait_ge(S["bias_stored"], 16)
            sp.wait_ge(S["hres_stored"], 32)
            sp.wait_ge(S["zeroed"], 16 * (SLOTS * SLOT // per))

            sp.wait_ge(S["scattered"], 16 * 2 * GROUPS)
            sp.wait_ge(S["plan_ready"], 1)
            sp.dma_start(exp_rows[:, :], expert_rows.partition_broadcast(128)).then_inc(S["exp_rows_loaded"], 16)
            for e in range(EXPERTS):
                pieces = (wi[e].rearrange("(k p) n -> p k n", p=128), wg[e].rearrange("(k p) n -> p k n", p=128),
                          wo[e].rearrange("(k p) n -> p k n", p=128))
                for j, src in enumerate(pieces):
                    q = 3 * e + j
                    need(sp, "stage_used", q - 1)
                    k = src.shape[1]
                    sp.dma_start(stage[:, q % 2, :].rearrange("p (k n) -> p k n", k=k), src).then_inc(S[f"stage_loaded{q % 2}"], 16)
                if e >= 2:
                    done = sp.value_load(tiles_done[0:1, e - 2:e - 1], min_val=0, max_val=SLOTS)
                    sp.wait_ge(S["ug_ps"], done * 2 + 1)
                need(sp, "bias_ready", 16 * e)
                sp.dma_start(bias_sb[:, (e % 2) * WSZ:(e % 2 + 1) * WSZ].bitcast(f32).rearrange("t (w n) -> t w n", w=2),
                             bias_parts.rearrange("t (w e n) -> t w e n", w=2, e=EXPERTS)[:, :, e, :]).then_inc(S["bias_ready"], 16)

            sp.wait_ge(S["y_stored0"], 8 * SLOTS)
            sp.wait_ge(S["y_stored1"], 8 * SLOTS)
            def load_res(g, slot):
                n = rows_of(g)
                sp.dma_start(res_in[0:n, slot, :], scr_h[ds(g * ROWS, n), :]).then_inc(S[f"res_loaded{slot}"], 16)
            for g in range(4):
                load_res(g, g)
            for g in range(GROUPS):
                n = rows_of(g)
                sp.wait_ge(S["sum_c"], 2 * (g + 1))
                sp.dma_start(out[g * ROWS:g * ROWS + n, :], sum_b[0:n, g % 4, :]).then_inc(S[f"out_stored{g % 4}"], 16)
                if g + 4 < GROUPS:
                    load_res(g + 4, g % 4)
            for b in range(4):
                sp.wait_ge(S[f"out_stored{b}"], 16 * len(range(b, GROUPS, 4)))

        @block.gpsimd
        def _(pool):
            def phase1(s, par, pair):
                if live(s):
                    n = rows_of(s)
                    need(pool, "x_norm_ready", s + 1)
                    need(pool, "xT_ps", s - 1)
                    pool.tensor_tensor(x_aff[0:n, par, :], x_norm[0:n, par, :], ln1_rows[0:n, 0, :], ALU.mult).then_inc(S["x_aff_c"], 1)
                    need(pool, "x_aff_c", 2 * s + 1)
                    pool.tensor_tensor(x_aff[0:n, par, :], x_aff[0:n, par, :], ln1_rows[0:n, 1, :], ALU.add).then_inc(S["x_aff_c"], 1)
                g = s - 3
                if live(g):
                    n = rows_of(g)
                    here = resid[0:n, ds(g * DIM, DIM)]
                    need_first(pool, "z_norm_ready", g + 1)
                    pool.tensor_tensor(here, z_norm[0:n, 1 - par, :], mul_rows[0:n, :], ALU.mult).then_inc(S["resid_c"], 1)
                    need_first(pool, "resid_c", 2 * g + 1)
                    pool.tensor_tensor(here, here, add_rows[0:n, :], ALU.add).then_inc(S["resid_c"], 1)

            pool.wait_ge(S["rows_loaded"], 16 * (2 + PER_GROUP))
            pool.wait_ge(S["setup_c"], 4)
            sweep(pool, body=phase1, **P1)

            pool.wait_ge(S["rope_c"], 4 * 4 * CHUNKS)
            pool.wait_ge(S["lat_ready"], 2 * CHUNKS)

            def phase3(s, par, pair):
                if live(s):
                    m = images_of(s)
                    need_first(pool, "scores_ps", 2 * (s - 1))
                    for half in range(2):
                        k_src = kT[:, half, ds(s * ROWS, m * TOKENS)].rearrange("p (i t) -> p i t", t=TOKENS)
                        pool.tensor_tensor(
                            k_blocks[:, par, half, 0:m * HEAD_SPAN].rearrange("p (i h t) -> p i h t", i=m, h=8),
                            k_src.unsqueeze(2).broadcast_to([128, m, 8, TOKENS]),
                            cst(C_HEAD).unsqueeze(1).unsqueeze(3).broadcast_to([128, m, 8, TOKENS]), ALU.mult).then_inc(S["keys_ready"], 1)
                    need_first(pool, "v_ps", s - 1)
                    pool.tensor_copy(lat_g[:, par, 0:m * TOKENS], latT[:, ds(s * ROWS, m * TOKENS)]).then_inc(S["keys_ready"], 1)
                g = s - 1
                if live(g):
                    m, n, gp = images_of(g), rows_of(g), 1 - par
                    need(pool, "exp_ready", g + 1)
                    need(pool, "pT_ps", 4 * (g - 1))
                    pool.tensor_tensor(
                        p_wide[0:n, gp, 0:HEADS * n].rearrange("p (h i t) -> p h i t", h=HEADS, i=m),
                        probs[0:n, gp, :].rearrange("p (h t) -> p h t", t=TOKENS).unsqueeze(2).broadcast_to([n, HEADS, m, TOKENS]),
                        cst(C_IMAGE, n)[:, 0:m].unsqueeze(1).unsqueeze(3).broadcast_to([n, HEADS, m, TOKENS]),
                        ALU.mult).then_inc(S["p_wide_ready"], 1)

            sweep(pool, body=phase3, **P3)

            pool.wait_ge(S["resid_done"], GROUPS)
            pool.memset(zero_rows[:, :], 0.0).then_inc(S["zero_ready"], 1)
            pool.wait_ge(S["bias_loaded"], 16)
            pool.tensor_copy(bias_hl[:, 0, :], bias_raw[:, :]).then_inc(S["bias_c"], 1)
            pool.wait_ge(S["bias_c"], 1)
            pool.tensor_tensor(bias_hl[:, 1, :], bias_raw[:, :], bias_hl[:, 0, :].bitcast(f32), ALU.subtract).then_inc(S["bias_c"], 1)

            pool.wait_ge(S["zeroed"], 16 * (SLOTS * SLOT // 512))
            pool.wait_ge(S["plan_ready"], 1)
            for g in range(GROUPS):
                n = rows_of(g)
                for c in range(TOP):
                    pool.indirect_dma_start(out=slots_in, out_offset=bass.IndirectOffsetOnAxis(ap=choice_row[0:n, c, g:g + 1], axis=0),
                                            in_=x2[0:n, g, :], in_offset=None).then_inc(S["scattered"], 16)

            pool.wait_ge(S["scattered"], 16 * 2 * GROUPS)
            for e in range(EXPERTS):
                if e >= 2:
                    done = pool.value_load(tiles_done[0:1, e - 2:e - 1], min_val=0, max_val=SLOTS)
                for j, (hi, lo) in enumerate((wi_hl, wg_hl, wo_hl)):
                    q = 3 * e + j
                    if e >= 2:
                        if j < 2:
                            need_first(pool, "ug_ps", done * 2 + 1)
                        else:
                            need_first(pool, "y_ps", done + 1)
                    to = slice((e % 2) * WSZ, (e % 2 + 1) * WSZ)
                    pool.wait_ge(S[f"stage_loaded{q % 2}"], 16 * (q // 2 + 1))
                    pool.tensor_copy(hi[:, to], stage[:, q % 2, :]).then_inc(S["weights_ready"], 1)
                    pool.wait_ge(S["weights_ready"], 2 * q + 1)
                    pool.tensor_tensor(lo[:, to], stage[:, q % 2, :], hi[:, to].bitcast(f32), ALU.subtract).then_inc(S["weights_ready"], 1)
                    pool.wait_ge(S["weights_ready"], 2 * q + 2)
                    pool.sem_inc(S["stage_used"], 1)

            pool.wait_ge(S["y_stored0"], 8 * SLOTS)
            pool.wait_ge(S["y_stored1"], 8 * SLOTS)
            for g in range(GROUPS):
                n = rows_of(g)
                need(pool, "sum_c", 2 * (g - 3))
                for c in range(TOP):
                    pool.indirect_dma_start(out=got[0:n, g % 4, c, :], out_offset=None, in_=slots_out,
                                            in_offset=bass.IndirectOffsetOnAxis(ap=choice_row[0:n, c, g:g + 1], axis=0)).then_inc(S[f"got_y{g % 4}"], 16)

        @block.scalar
        def _(act):
            A = act.activation

            def phase1(s, par, pair):
                need(act, "ln_c", 6 * s + 1)
                A(ln_sd[:, par, :], ln_ve[:, par, :], ACT.Sqrt).then_inc(S["std_ready"], 1)
                g = s - 1
                if live(g):
                    n, gp = rows_of(g), 1 - par
                    need(act, "xT_ps", g + 1)
                    need(act, "z_ps", g - 1)
                    for b in range(2):
                        A(x_affT[:, gp, 3 * b:3 * b + 3, 0:n],
                          bank[b][:, 0:3 * ROWS].rearrange("p (k n) -> p k n", k=3)[:, :, 0:n], ACT.Copy).then_inc(S["x_affT_ready"], 1)
                g = s - 5
                if live(g):
                    n = rows_of(g)
                    need(act, "x1T_ps", g + 1)
                    A(x1T[:, :, ds(g * ROWS, n)], bank[4][:, 0:2 * ROWS].rearrange("p (k n) -> p k n", k=2)[:, :, 0:n],
                      ACT.Copy).then_inc(S["x1T_ready"], 1)

            sweep(act, body=phase1, **P1)

            act.wait_ge(S["weights_loaded"], 16 * 7)

            def phase2(c, par, pair):
                need(act, "rope_ps", 4 * (c - 1))
                need(act, "lat_ps", 2 * c + 1)
                A(ctq[:, par, :], bank[0][:, 0:CHUNK], ACT.Identity, bias=colb[:, 0:1]).then_inc(S["lat_ready"], 1)
                need(act, "lat_ps", 2 * c + 2)
                A(latT[:, ds(c * CHUNK, CHUNK)], bank[1][:, 0:CHUNK], ACT.Identity, bias=colb[:, 1:2]).then_inc(S["lat_ready"], 1)

            sweep(act, body=phase2, **P2)

            act.wait_ge(S["rope_c"], 4 * 4 * CHUNKS)
            act.wait_ge(S["attn_zero"], 2)

            def copy_round(g, gp, r):
                n = rows_of(g)
                b = bank[2 + r % 2]
                need(act, "pT_ps", 4 * g + r + 1)
                need(act, "pv_ps", 4 * (g - 1))
                A(pT[0:n, gp, r * ROUND * n:(r + 1) * ROUND * n], b[0:n, 0:ROUND * n], ACT.Copy).then_inc(S["pT_act"], 1)

            def phase3(s, par, pair):
                g = s - 3
                if live(g):
                    n, gp = rows_of(g), 1 - par
                    need(act, "attT_ps", g + 1)
                    need(act, "proj_ps", g - 1)
                    A(attT[:, gp, :, 0:n], bank[6][:, 0:2 * ROWS].rearrange("p (k n) -> p k n", k=2)[:, :, 0:n], ACT.Copy).then_inc(S["attT_ready"], 1)
                if live(s):
                    m = images_of(s)
                    need(act, "scores_ps", 2 * (s - 1))
                    A(q_pad[:, par, :, :].rearrange("p h (i w) -> p h i w", i=PER_GROUP)[:, :, 0:m, 0:TOKENS],
                      qT[:, :, ds(s * ROWS, m * TOKENS)].rearrange("p h (i t) -> p h i t", t=TOKENS), ACT.Copy).then_inc(S["queries_ready"], 1)
                if live(s - 2):
                    copy_round(s - 2, par, 0)
                g = s - 1
                if live(g):
                    n, gp = rows_of(g), 1 - par
                    need(act, "max_c", 2 * g + 2)
                    need(act, "p_wide_ready", g - 1)
                    A(probs[0:n, gp, :], shifted[0:n, gp, :], ACT.Exp, scale=SCORE_SCALE).then_inc(S["exp_ready"], 1)
                if live(s - 2):
                    copy_round(s - 2, par, 2)

            sweep(act, body=phase3, **P3)

            act.wait_ge(S["ln4_c"], GROUPS + 2)
            A(sc4[:, 1, :], sc4[:, 0, :], ACT.Sqrt).then_inc(S["sd4_ready"], 1)
            for g in range(GROUPS):
                n = rows_of(g)
                need(act, "x2T_ps", g + 1)
                need(act, "logits_ps", g - 1)
                A(x2T[:, g % 2, :, 0:n], bank[g % 2][:, 0:2 * ROWS].rearrange("p (k n) -> p k n", k=2)[:, :, 0:n], ACT.Copy).then_inc(S["x2T_ready"], 1)
            act.wait_ge(S["route_in"], 1)
            A(lg[:, 2, :], lg[:, 1, :], ACT.Exp).then_inc(S["exp4_ready"], 1)

            act.wait_ge(S["scattered"], 16 * 2 * GROUPS)
            act.wait_ge(S["plan_ready"], 1)

            def load_slot(j, buf):
                act.dma_start(xs[:, buf, :], slots_in[ds(j * SLOT, SLOT), :]).then_inc(S[f"xs_loaded{buf}"], 16)

            def split_x(j, par):
                need(act, "xsT_ps", j + 1)
                need(act, "ug_ps", 2 * (j - 1) + 1)
                A(xsT[0][:, par, :, :], bank[7][:, 0:256].rearrange("p (k n) -> p k n", k=2), ACT.Copy).then_inc(S["xs_hi"], 1)

            def gated(j, c):
                need(act, "ug_ps", 2 * j + c + 2)
                need(act, "hid_ready", 2 * (j - 1) + c + 1)
                A(act_u[:, c, :], bank[2 * c][:, :], ACT.Gelu).then_inc(S["gelu_c"], 1)
                A(act_g[:, c, :], bank[2 * c + 1][:, :], ACT.Tanh, scale=0.5).then_inc(S["gelu_c"], 1)

            def split_hidden(j, par, c):
                need(act, "hidT_ps", 2 * j + c + 1)
                need(act, "y_ps", j)
                A(hidT[0][:, par, 4 * c:4 * c + 4, :], bank[4 + c][:, :].rearrange("p (k n) -> p k n", k=4), ACT.Copy, scale=0.5).then_inc(S["hid_hi"], 1)

            def store_y(j, par):
                need(act, "y_out_ready", j + 1)
                act.dma_start(slots_out[ds(j * SLOT, SLOT), :], y_out[:, par, :]).then_inc(S[f"y_stored{par}"], 16)

            def slot(j, par, buf2):
                first = isinstance(j, int) and j == 0
                gated(j, 0)
                if not (isinstance(j, int) and j + 1 >= SLOTS):
                    split_x(j + 1, 1 - par)
                if not first:
                    split_hidden(j - 1, 1 - par, 1)
                gated(j, 1)
                split_hidden(j, par, 0)
                if not (isinstance(j, int) and j < 2):
                    store_y(j - 2, par)
                if not (isinstance(j, int) and j + 2 >= SLOTS):
                    need(act, "xs_done", j - 1)
                    load_slot(j + 2, buf2)

            for j in range(2):
                load_slot(j, j)
            split_x(0, 0)
            for j in range(4):
                slot(j, j % 2, (j + 2) % 4)
            with act.Fori(1, SLOTS // 4 - 1) as quad:
                for k in range(4):
                    slot(quad * 4 + k, k % 2, (k + 2) % 4)
            for j in range(SLOTS - 4, SLOTS):
                slot(j, j % 2, (j + 2) % 4)
            split_hidden(SLOTS - 1, (SLOTS - 1) % 2, 1)
            store_y(SLOTS - 2, 0)
            store_y(SLOTS - 1, 1)

        @block.vector
        def _(v):
            v.memset(x_in[:, :, :], 0.0).then_inc(S["setup_done"], 1)
            v.memset(ln_mv[:, :, :, :], 1.0).then_inc(S["setup_c"], 1)
            v.wait_ge(S["const_loaded"], 16)
            v.wait_ge(S["rows_loaded"], 16 * (2 + PER_GROUP))
            is_patch, is_cls = cst(C_PATCH, ROWS)[:, 0:1], cst(C_PATCH, ROWS)[:, 1:2]
            v.tensor_scalar(mul_rows[:, :], ln2_g, is_patch, None, ALU.mult).then_inc(S["setup_c"], 1)
            v.scalar_tensor_tensor(tmp_rows[:, :], ln2_b, is_patch, pos_sb[:, :], ALU.mult, ALU.add).then_inc(S["setup_c"], 1)
            v.wait_ge(S["setup_c"], 3)
            v.scalar_tensor_tensor(add_rows[:, :], cls_row, is_cls, tmp_rows[:, :], ALU.mult, ALU.add).then_inc(S["setup_c"], 1)

            def phase1(s, par, pair):
                g1, g2, g3 = s, s - 3, s - 4
                if live(g1):
                    n = rows_of(g1)
                    need(v, f"x_loaded{par}", x_loaded_after(g1, pair))
                    for b in range(2):
                        v.bn_stats(ln1_st[0:n, par, b, :], x_in[0:n, par, b * 384:(b + 1) * 384]).then_inc(S["ln1_c"], 1)
                    need_first(v, "ln1_c", 3 * g1 + 2)
                    v.bn_aggr(ln_mv[0:n, par, 0, :], ln1_st[0:n, par, :, :]).then_inc(S["ln1_c"], 1)
                if live(g2):
                    n = rows_of(g2)
                    need(v, "z_ps", g2 + 1)
                    v.tensor_tensor(z_sb[0:n, par, :], bank[2 + (1 - par)][0:n, 0:DIM], b_proj[0:n, :], ALU.add).then_inc(S["ln2_c"], 1)
                    need(v, "ln2_c", 3 * g2 + 1)
                    v.bn_stats(ln2_st[0:n, par, :], z_sb[0:n, par, :]).then_inc(S["ln2_c"], 1)
                    need_first(v, "ln2_c", 3 * g2 + 2)
                    v.bn_aggr(ln_mv[0:n, par, 1, :], ln2_st[0:n, par, :]).then_inc(S["ln2_c"], 1)
                if live(g3):
                    n = rows_of(g3)
                    need(v, "resid_c", 2 * g3 + 2)
                    v.bn_stats(ln3_st[0:n, par, :], resid[0:n, ds(g3 * DIM, DIM)]).then_inc(S["ln3_c"], 1)
                    need_first(v, "ln3_c", 2 * g3 + 1)
                    v.bn_aggr(ln_mv[0:n, par, 2, :], ln3_st[0:n, par, :]).then_inc(S["ln3_c"], 1)
                if live(g1): need(v, "ln1_c", 3 * g1 + 3)
                if live(g2): need(v, "ln2_c", 3 * g2 + 3)
                if live(g3): need(v, "ln3_c", 2 * g3 + 2)
                ve, r0 = ln_ve[:, par, :], ln_r0[:, par, :]
                t = [ln_t[:, par, i, :] for i in range(3)]
                v.tensor_scalar(ve, ln_mv[:, par, :, 1], 1e-5, None, ALU.add).then_inc(S["ln_c"], 1)
                need(v, "std_ready", s + 1)
                v.reciprocal(r0, ln_sd[:, par, :]).then_inc(S["ln_c"], 1)
                need(v, "ln_c", 6 * s + 2)
                v.tensor_tensor(t[0], r0, r0, ALU.mult).then_inc(S["ln_c"], 1)
                need(v, "ln_c", 6 * s + 3)
                v.tensor_tensor(t[1], t[0], ve, ALU.mult).then_inc(S["ln_c"], 1)
                need(v, "ln_c", 6 * s + 4)
                v.tensor_scalar(t[2], t[1], -0.5, 1.5, ALU.mult, ALU.add).then_inc(S["ln_c"], 1)
                need(v, "ln_c", 6 * s + 5)
                v.tensor_tensor(ln_rs[:, par, :], r0, t[2], ALU.mult).then_inc(S["ln_c"], 1)
                need(v, "ln_c", 6 * s + 6)

                def norm(o, i, n, w, name):
                    v.tensor_scalar(o, i, ln_mv[0:n, par, w, 0:1], ln_rs[0:n, par, w:w + 1], ALU.subtract, ALU.mult).then_inc(S[name], 1)
                if live(g1):
                    n = rows_of(g1)
                    need(v, "x_aff_c", 2 * (g1 - 1))
                    norm(x_norm[0:n, par, :], x_in[0:n, par, :], n, 0, "x_norm_ready")
                if live(g2):
                    n = rows_of(g2)
                    need(v, "resid_c", 2 * (g2 - 1))
                    norm(z_norm[0:n, 1 - par, :], z_sb[0:n, par, :], n, 1, "z_norm_ready")
                if live(g3):
                    n = rows_of(g3)
                    need(v, "x1T_ps", g3 - 1)
                    norm(x1[0:n, par, :], resid[0:n, ds(g3 * DIM, DIM)], n, 2, "x1_ready")

            sweep(v, body=phase1, **P1)
            v.wait_ge(S["x1T_ready"], GROUPS)
            v.wait_ge(S["resid_c"], 2 * GROUPS)
            v.wait_ge(S["weights_loaded"], 16 * 7)

            def phase2(c, par, pair):
                for j in range(4):
                    half, q, tri = j % 2, j // 2, c * 4 + j
                    base = 3 * (j % 2)
                    ps = [bank[2 + base + i][:, 0:CHUNK] for i in range(3)]
                    t = [rot[:, j % 2, i, :] for i in range(3)]
                    bcol = 2 + 6 * q + half
                    table = [rope_sb[:, w, half, :].unsqueeze(1).broadcast_to([128, CHUNK_IMAGES, TOKENS]) for w in range(2)]

                    def im(x):
                        return x.rearrange("p (i t) -> p i t", t=TOKENS)
                    need(v, "rope_ps", tri + 1)
                    need(v, "rope_c", tri * 4 - 4)
                    v.scalar_tensor_tensor(im(t[0]), im(ps[0]), colb[:, bcol:bcol + 1], table[0], ALU.add, ALU.mult).then_inc(S["rope_c"], 1)
                    v.scalar_tensor_tensor(im(t[1]), im(ps[1]), colb[:, bcol + 2:bcol + 3], table[1], ALU.add, ALU.mult).then_inc(S["rope_c"], 1)
                    need(v, "rope_c", tri * 4 + 1)
                    v.scalar_tensor_tensor(t[2], ps[2], colb[:, bcol + 4:bcol + 5], t[0], ALU.add, ALU.add).then_inc(S["rope_c"], 1)
                    need(v, "rope_c", tri * 4 + 3)
                    v.tensor_tensor((qT if q else kT)[:, half, ds(c * CHUNK, CHUNK)], t[2], t[1], ALU.add).then_inc(S["rope_c"], 1)

            sweep(v, body=phase2, **P2)
            v.wait_ge(S["rope_c"], 4 * 4 * CHUNKS)
            v.wait_ge(S["rope_ps"], 4 * CHUNKS)

            v.memset(q_pad[:, :, :, :], 0.0).then_inc(S["attn_zero"], 1)
            v.memset(v_one[:, :, :, :], 1.0).then_inc(S["attn_zero"], 1)
            v.wait_ge(S["attn_zero"], 2)

            def copy_round(g, gp, r):
                n = rows_of(g)
                need(v, "pT_ps", 4 * g + r + 1)
                need(v, "pv_ps", 4 * (g - 1))
                v.tensor_copy(pT[0:n, gp, r * ROUND * n:(r + 1) * ROUND * n], bank[2 + r % 2][0:n, 0:ROUND * n]).then_inc(S["pT_dve"], 1)

            def phase3(s, par, pair):
                if live(s - 2):
                    copy_round(s - 2, par, 1)
                g = s - 1
                if live(g):
                    n, gp = rows_of(g), 1 - par
                    need(v, "scores_ps", 2 * g + 2)
                    need(v, "exp_ready", g - 1)
                    for half in range(2):
                        sc = bank[half][0:n, 0:HEAD_SPAN].rearrange("p (h t) -> p h t", t=TOKENS)
                        ins = v.tensor_reduce(top[0:n, gp, 8 * half:8 * half + 8], sc, AX.X, ALU.max)
                    ins.then_inc(S["max_c"], 1)
                    need(v, "max_c", 2 * g + 1)
                    for half in range(2):
                        sc = bank[half][0:n, 0:HEAD_SPAN].rearrange("p (h t) -> p h t", t=TOKENS)
                        ins = v.tensor_tensor(shifted[0:n, gp, half * HEAD_SPAN:(half + 1) * HEAD_SPAN].rearrange("p (h t) -> p h t", t=TOKENS),
                                              sc, top[0:n, gp, 8 * half:8 * half + 8].unsqueeze(2).broadcast_to([n, 8, TOKENS]), ALU.subtract)
                    ins.then_inc(S["max_c"], 1)
                if live(s - 2):
                    copy_round(s - 2, par, 3)
                if live(g):
                    need(v, "v_ps", g + 1)
                    need(v, "pv_ps", 4 * (g - 1))
                    v.tensor_tensor(v_one[0:n, gp, :, 0:HEAD_DIM], bank[4][0:n, 0:DIM].rearrange("p (h d) -> p h d", h=HEADS),
                                    b_v[0:n, :].rearrange("p (h d) -> p h d", h=HEADS), ALU.add).then_inc(S["v_ready"], 1)
                g = s - 3
                if live(g):
                    n, gp = rows_of(g), 1 - par
                    here = resid[0:n, ds(g * DIM, DIM)]
                    need(v, "proj_ps", g + 1)
                    v.tensor_tensor(att_b[0:n, gp, :], bank[7][0:n, 0:DIM], b_o[0:n, :], ALU.add).then_inc(S["att_c"], 1)
                    need(v, "att_c", 1 * (g + 1))
                    v.tensor_tensor(here, here, att_b[0:n, gp, :], ALU.add).then_inc(S["resid_done"], 1)
                    need(v, "resid_done", g + 1)
                    v.bn_stats(ln4_stats[0:n, ds(g, 1), :], here).then_inc(S["ln4_c"], 1)
                g = s - 2
                if live(g):
                    n, gp = rows_of(g), par
                    pv = bank[5][0:n, 0:HEADS * 17].rearrange("p (h d) -> p h d", h=HEADS)
                    need(v, "pv_ps", 4 * g + 4)
                    need(v, "attT_ps", g - 1)
                    v.reciprocal(inv_sum[0:n, gp, :].unsqueeze(2), pv[:, :, 16:17]).then_inc(S["route_c"], 1)
                    need(v, "route_c", 2 * g + 1)
                    v.tensor_tensor(att[0:n, gp, :].rearrange("p (h d) -> p h d", h=HEADS), pv[:, :, 0:16],
                                    inv_sum[0:n, gp, :].unsqueeze(2).broadcast_to([n, HEADS, HEAD_DIM]), ALU.mult).then_inc(S["route_c"], 1)

            sweep(v, body=phase3, **P3)
            v.wait_ge(S["ln4_c"], GROUPS)
            v.wait_ge(S["pT_act"], 2 * GROUPS)
            v.wait_ge(S["attT_ready"], GROUPS)
            v.wait_ge(S["proj_ps"], GROUPS)

            count = [2 * GROUPS]

            def step(ins):
                count[0] += 1
                ins.then_inc(S["route_c"], 1)
                v.wait_ge(S["route_c"], count[0])

            step(v.memset(mv4[:, :, :], 1.0))
            for g in range(GROUPS):
                n = rows_of(g)
                ins = v.bn_aggr(mv4[0:n, g, :], ln4_stats[0:n, g, :])
            ins.then_inc(S["ln4_c"], 1)
            v.wait_ge(S["ln4_c"], GROUPS + 1)
            v.tensor_scalar(sc4[:, 0, :], mv4[:, :, 1], 1e-5, None, ALU.add).then_inc(S["ln4_c"], 1)
            v.wait_ge(S["sd4_ready"], 1)
            step(v.reciprocal(sc4[:, 2, :], sc4[:, 1, :]))
            step(v.tensor_tensor(sc4[:, 3, :], sc4[:, 2, :], sc4[:, 2, :], ALU.mult))
            step(v.tensor_tensor(sc4[:, 4, :], sc4[:, 3, :], sc4[:, 0, :], ALU.mult))
            step(v.tensor_scalar(sc4[:, 5, :], sc4[:, 4, :], -0.5, 1.5, ALU.mult, ALU.add))
            step(v.tensor_tensor(sc4[:, 6, :], sc4[:, 2, :], sc4[:, 5, :], ALU.mult))
            for g in range(GROUPS):
                n = rows_of(g)
                v.tensor_scalar(x2[0:n, g, :], resid[0:n, g * DIM:(g + 1) * DIM], mv4[0:n, g, 0:1], sc4[0:n, 6, g:g + 1],
                                ALU.subtract, ALU.mult).then_inc(S["x2_ready"], 1)
            def L(i, n=ROWS):
                return lg[0:n, i, :].rearrange("p (g e) -> p g e", e=EXPERTS)

            def per_token(x):
                return x.unsqueeze(2).broadcast_to([ROWS, GROUPS, EXPERTS])
            sm = [small[:, i, :] for i in range(12)]
            step(v.memset(lg[:, 0, :], 0.0))
            v.wait_ge(S["logits_ps"], GROUPS)
            full = (GROUPS - 1) * EXPERTS
            rest = rows_of(GROUPS - 1)
            step(v.tensor_tensor(lg[:, 0, 0:full].rearrange("p (g e) -> p g e", e=EXPERTS),
                                 bank[2][0:ROWS, 0:full].rearrange("p (g e) -> p g e", e=EXPERTS),
                                 b_router.unsqueeze(1).broadcast_to([ROWS, GROUPS - 1, EXPERTS]), ALU.add))
            step(v.tensor_tensor(lg[0:rest, 0, full:], bank[2][0:rest, full:full + EXPERTS], b_router[0:rest, :], ALU.add))
            step(v.tensor_reduce(sm[0], L(0), AX.X, ALU.max))
            v.tensor_tensor(L(1), L(0), per_token(sm[0]), ALU.subtract).then_inc(S["route_in"], 1)
            v.wait_ge(S["exp4_ready"], 1)
            step(v.tensor_reduce(sm[1], L(2), AX.X, ALU.add))
            step(v.reciprocal(sm[2], sm[1]))
            step(v.tensor_tensor(L(3), L(2), per_token(sm[2]), ALU.mult))
            rank = cst(C_RANK, ROWS).rearrange("p (g e) -> p g e", e=EXPERTS)

            def pick(src, best, sel, a, b):
                step(v.tensor_reduce(best, src, AX.X, ALU.max))
                step(v.tensor_tensor(L(a), src, per_token(best), ALU.is_equal))
                step(v.tensor_tensor(L(b), L(a), rank, ALU.mult))
                step(v.tensor_reduce(sm[3], L(b), AX.X, ALU.max))
                step(v.tensor_tensor(sel, L(b), per_token(sm[3]), ALU.is_equal))
            pick(L(3), sm[4], L(6), 4, 5)
            step(v.scalar_tensor_tensor(L(7), L(6), -2.0, L(3), ALU.mult, ALU.add))
            pick(L(7), sm[5], L(8), 4, 5)
            step(v.tensor_tensor(sm[6], sm[4], sm[5], ALU.add))
            step(v.reciprocal(sm[7], sm[6]))
            step(v.tensor_tensor(choice_weight[:, 0, :], sm[4], sm[7], ALU.mult))
            step(v.tensor_tensor(choice_weight[:, 1, :], sm[5], sm[7], ALU.mult))
            step(v.tensor_tensor(L(9), L(6), L(8), ALU.add))
            v.tensor_tensor(L(10), L(9), per_token(cst(C_VALID, ROWS)), ALU.mult).then_inc(S["route_in"], 1)
            v.wait_ge(S["route_ps"], 1)
            NEh = NE
            step(v.tensor_copy(lg[:, 11, :], bank[3][0:ROWS, 0:NEh]))
            step(v.tensor_copy(lg[:, 12, :], bank[4][0:ROWS, 0:NEh]))
            src, dst, shift = 12, 13, 1
            while shift < GROUPS:
                w = shift * EXPERTS
                step(v.tensor_copy(lg[:, dst, 0:w], lg[:, src, 0:w]))
                step(v.tensor_tensor(lg[:, dst, w:], lg[:, src, w:], lg[:, src, 0:NE - w], ALU.add))
                src, dst, shift = dst, src, shift * 2
            step(v.tensor_tensor(lg[:, 14, EXPERTS:], lg[:, 11, EXPERTS:], lg[:, src, 0:NE - EXPERTS], ALU.add))
            step(v.tensor_copy(lg[:, 14, 0:EXPERTS], lg[:, 11, 0:EXPERTS]))
            total = lg[:, src, NE - EXPERTS:NE]
            over_v = over[:, :].rearrange("p (e t) -> p e t", e=EXPERTS)
            step(v.tensor_tensor(over_v, total.unsqueeze(2).broadcast_to([ROWS, EXPERTS, 19]),
                                 cst(C_THRESH, ROWS).rearrange("p (e t) -> p e t", e=EXPERTS), ALU.is_gt))
            step(v.tensor_reduce(cnt[:, 0, :], over_v, AX.X, ALU.add))
            a, b = 0, 1
            for shift in (1, 2, 4):
                step(v.tensor_copy(cnt[:, b, 0:shift], cnt[:, a, 0:shift]))
                step(v.tensor_tensor(cnt[:, b, shift:], cnt[:, a, shift:], cnt[:, a, 0:EXPERTS - shift], ALU.add))
                a, b = b, b + 1
            step(v.memset(cnt[:, 6, :], 0.0))
            step(v.tensor_scalar(cnt[:, 6, 1:], cnt[:, a, 0:EXPERTS - 1], float(SLOT), None, ALU.mult))
            step(v.tensor_tensor(L(15), L(14), cnt[:, 6, :].unsqueeze(1).broadcast_to([ROWS, GROUPS, EXPERTS]), ALU.add))
            for c, sel in enumerate((6, 8)):
                step(v.tensor_tensor(L(4), L(15), L(sel), ALU.mult))
                step(v.tensor_reduce(sm[8 + c], L(4), AX.X, ALU.add))
                step(v.tensor_copy(choice_row[:, c, :], sm[8 + c]))
            step(v.tensor_tensor(smap[0:1, 0, :].rearrange("p (j e) -> p j e", e=8),
                                 cst(C_SLOTNO, 1).rearrange("p (j e) -> p j e", e=8),
                                 cnt[0:1, a, :].unsqueeze(1).broadcast_to([1, SLOTS, 8]), ALU.is_ge))
            step(v.tensor_tensor(smap[0:1, 1, :], smap[0:1, 0, :], cst(C_SIGN, 1), ALU.mult))
            step(v.tensor_reduce(smap_sum[0:1, 0, :], smap[0:1, 0, :].rearrange("p (j e) -> p j e", e=8)[:, :, 0:7], AX.X, ALU.add))
            step(v.tensor_reduce(smap_sum[0:1, 1, :], smap[0:1, 1, :].rearrange("p (j e) -> p j e", e=8)[:, :, 0:7], AX.X, ALU.add))
            step(v.tensor_copy(slot_expert[0:1, :], smap_sum[0:1, 0, :]))
            step(v.tensor_copy(slot_buffer[0:1, :], smap_sum[0:1, 1, :]))
            step(v.tensor_copy(tiles_done[0:1, :], cnt[0:1, a, :]))
            v.engine_nop().then_inc(S["plan_ready"], 1)

            v.wait_ge(S["scattered"], 16 * 2 * GROUPS)
            v.memset(hid[0:2, 0, 0:128], 1.0).then_inc(S["ones_ready"], 1)
            v.wait_ge(S["ones_ready"], 1)
            v.tensor_copy(ones2[:, :], hid[0:2, 0, 0:128]).then_inc(S["ones_ready"], 1)
            v.wait_ge(S["ones_ready"], 2)
            v.wait_ge(S["exp_rows_loaded"], 16)
            YC = 19

            def split_x(j, par):
                need(v, "xs_hi", j + 1)
                need(v, "ug_ps", 2 * (j - 1) + 1)
                v.tensor_tensor(xsT[1][:, par, :, :], bank[7][:, 0:256].rearrange("p (k n) -> p k n", k=2),
                                xsT[0][:, par, :, :].bitcast(f32), ALU.subtract).then_inc(S["xs_lo"], 1)

            def gate(j, c):
                need(v, "gelu_c", 4 * j + 2 * c + 2)
                need(v, "hidT_ps", 2 * (j - 1) + c + 1)
                v.scalar_tensor_tensor(hid[:, c, :], act_g[:, c, :], 1.0, act_u[:, c, :], ALU.add, ALU.mult).then_inc(S["hid_ready"], 1)

            def split_hidden(j, par, c):
                need(v, "hid_hi", 2 * j + c + 1)
                need(v, "y_ps", j)
                v.scalar_tensor_tensor(hidT[1][:, par, 4 * c:4 * c + 4, :], bank[4 + c][:, :].rearrange("p (k n) -> p k n", k=4), 0.5,
                                       hidT[0][:, par, 4 * c:4 * c + 4, :].bitcast(f32), ALU.mult, ALU.subtract).then_inc(S["hid_lo"], 1)

            def finish(j, par, buf, pair):
                k = [0]

                def link(ins, own=False):
                    k[0] += 1
                    ins.then_inc(S["y_c"], 1)
                    v.wait_ge(S["y_c"], j * YC + k[0])
                    if own:
                        v.nop(nofuse=True)
                e = v.value_load(slot_expert[0:1, ds(j, 1)], min_val=0, max_val=EXPERTS - 1)
                r = [y_res[:, par, i, :] for i in range(3)]
                c = [y_sc[:, i:i + 1] for i in range(12)]
                need(v, "y_ps", j + 2)
                link(v.tensor_tensor(r[0], bank[6][:, 0:DIM], xs[:, buf, :], ALU.add))
                v.sem_inc(S["xs_done"], 1)
                link(v.tensor_tensor(r[1], r[0], exp_rows[:, ds(e * DIM, DIM)], ALU.add))
                link(v.bn_stats(y_st[:, :], r[1]), own=True)
                link(v.bn_aggr(y_mv[:, :], y_st[:, :]))
                link(v.tensor_scalar(c[0], y_mv[:, 1:2], 1e-12, None, ALU.add))
                link(v.tensor_scalar(y_int[:, 0:1], c[0].bitcast(i32), 1, None, ALU.logical_shift_right))
                link(v.tensor_scalar(y_int[:, 1:2], y_int[:, 0:1], -1.0, float(0x5f3759df), ALU.mult, ALU.add))
                y = y_int[:, 1:2].bitcast(f32)
                for t in range(3):
                    a, b, nxt = c[1 + 3 * t], c[2 + 3 * t], c[3 + 3 * t]
                    link(v.tensor_scalar(a, y, y, c[0], ALU.mult, ALU.mult))
                    link(v.tensor_scalar(b, a, -0.5, 1.5, ALU.mult, ALU.add))
                    link(v.tensor_scalar(nxt, b, y, None, ALU.mult))
                    y = nxt
                link(v.tensor_scalar(r[0], r[1], y_mv[:, 0:1], y, ALU.subtract, ALU.mult))
                link(v.tensor_tensor(r[2], r[0], exp_rows[:, ds(e * DIM + EXPERTS * DIM, DIM)], ALU.mult))
                need(v, f"y_stored{par}", pair * 16)
                v.tensor_tensor(y_out[:, par, :], r[2], exp_rows[:, ds(e * DIM + 2 * EXPERTS * DIM, DIM)], ALU.add).then_inc(S["y_out_ready"], 1)
                v.wait_ge(S["y_out_ready"], j + 1)
                v.sem_inc(S["y_c"], 1)

            def slot(j, par, buf, quad):
                first = isinstance(j, int) and j == 0
                if not (isinstance(j, int) and j + 1 >= SLOTS):
                    split_x(j + 1, 1 - par)
                gate(j, 0)
                if not first:
                    split_hidden(j - 1, 1 - par, 1)
                gate(j, 1)
                split_hidden(j, par, 0)
                if not first:
                    finish(j - 1, 1 - par, (buf + 3) % 4, quad * 2 + (buf - 1) // 2)

            split_x(0, 0)
            for j in range(4):
                slot(j, j % 2, j, 0)
            with v.Fori(1, SLOTS // 4 - 1) as quad:
                for k in range(4):
                    slot(quad * 4 + k, k % 2, k, quad)
            for j in range(SLOTS - 4, SLOTS):
                slot(j, j % 2, j % 4, j // 4)
            split_hidden(SLOTS - 1, (SLOTS - 1) % 2, 1)
            finish(SLOTS - 1, (SLOTS - 1) % 2, (SLOTS - 1) % 4, (SLOTS - 1) // 2)

            for g in range(GROUPS):
                n, b = rows_of(g), g % 4
                v.wait_ge(S[f"res_loaded{b}"], 16 * (g // 4 + 1))
                v.wait_ge(S[f"got_y{b}"], 32 * (g // 4 + 1))
                need(v, f"out_stored{b}", 16 * (g // 4))
                v.scalar_tensor_tensor(sum_a[0:n, b, :], got[0:n, b, 0, :], choice_weight[0:n, 0, g:g + 1], res_in[0:n, b, :],
                                       ALU.mult, ALU.add).then_inc(S["sum_c"], 1)
                v.wait_ge(S["sum_c"], 2 * g + 1)
                v.scalar_tensor_tensor(sum_b[0:n, b, :], got[0:n, b, 1, :], choice_weight[0:n, 1, g:g + 1], sum_a[0:n, b, :],
                                       ALU.mult, ALU.add).then_inc(S["sum_c"], 1)

        @block.tensor
        def _(pe):
            mm, tr = pe.matmul, pe.transpose
            pe.wait_ge(S["const_loaded"], 16)
            pe.wait_ge(S["wproj_loaded"], 16)

            def phase1(s, par, pair):
                g = s - 1
                if live(g):
                    n, gp = rows_of(g), 1 - par
                    need(pe, "x_aff_c", 2 * g + 2)
                    need(pe, "x_affT_ready", 2 * g)
                    for k in range(6):
                        ins = tr(bank[k // 3][:, (k % 3) * ROWS:(k % 3) * ROWS + n], x_aff[0:n, gp, k * 128:(k + 1) * 128], ident[0:n, 0:n])
                    ins.then_inc(S["xT_ps"], 1)
                g5 = s - 5
                if live(g5):
                    n = rows_of(g5)
                    need(pe, "x1_ready", g5 + 1)
                    need(pe, "x1T_ready", g5)
                    for k in range(2):
                        ins = tr(bank[4][:, k * ROWS:k * ROWS + n], x1[0:n, 1 - par, k * 128:(k + 1) * 128], ident[0:n, 0:n])
                    ins.then_inc(S["x1T_ps"], 1)
                if live(g):
                    n = rows_of(g)
                    need(pe, "x_affT_ready", 2 * g + 2)
                    need(pe, "ln2_c", 3 * (g - 2) + 1)
                    for k in range(6):
                        ins = mm(bank[2 + gp][0:n, 0:DIM], x_affT[:, gp, k, 0:n], wproj_sb[:, k, :], start=(k == 0), stop=(k == 5))
                    ins.then_inc(S["z_ps"], 1)

            sweep(pe, body=phase1, **P1)

            pe.wait_ge(S["weights_loaded"], 16 * 7)
            pe.wait_ge(S["x1T_ready"], GROUPS)

            def phase2(c, par, pair):
                def xk(k):
                    return x1T[:, k, ds(c * CHUNK, CHUNK)]
                need(pe, "lat_ready", 2 * c)
                for w in range(2):
                    for k in range(2):
                        ins = mm(bank[w][:, 0:CHUNK], wd_sb[:, k, w * LATENT:(w + 1) * LATENT], xk(k), start=(k == 0), stop=(k == 1))
                    ins.then_inc(S["lat_ps"], 1)
                for j in range(4):
                    half, q, tri = j % 2, j // 2, c * 4 + j
                    b = bank[2 + 3 * (j % 2):5 + 3 * (j % 2)]
                    cut = slice(half * 128, half * 128 + 128)
                    need(pe, "rope_c", tri * 4 - 4)
                    if q == 0:
                        for r in range(2):
                            for k in range(2):
                                mm(b[r][:, 0:CHUNK], wk_sb[:, 2 * r + k, cut], xk(k), start=(k == 0), stop=(k == 1))
                        need(pe, "lat_ready", 2 * c + 2)
                        ins = mm(b[2][:, 0:CHUNK], wk_sb[:, 4, cut], latT[:, ds(c * CHUNK, CHUNK)], start=True, stop=True)
                    else:
                        for r in range(3):
                            ins = mm(b[r][:, 0:CHUNK], wq_sb[:, r * DIM + half * 128:r * DIM + half * 128 + 128], ctq[:, par, :], start=True, stop=True)
                    ins.then_inc(S["rope_ps"], 1)

            sweep(pe, body=phase2, **P2)

            pe.wait_ge(S["rope_c"], 4 * 4 * CHUNKS)

            def phase3(s, par, pair):
                gd, gc, gb = s - 3, s - 2, s - 1

                def scores(half):
                    n, m, gp = rows_of(gb), images_of(gb), 1 - par
                    need(pe, "keys_ready", 3 * gb + 3)
                    need(pe, "queries_ready", gb + 1)
                    need(pe, "max_c", 2 * gb)
                    for i in range(m):
                        ins = mm(bank[half][0:n, 0:HEAD_SPAN], q_pad[:, gp, half, i * ROWS:i * ROWS + n],
                                 k_blocks[:, gp, half, i * HEAD_SPAN:(i + 1) * HEAD_SPAN], start=(i == 0), stop=(i == m - 1))
                    ins.then_inc(S["scores_ps"], 1)

                def turn_round(r):
                    n = rows_of(gc)
                    need(pe, "p_wide_ready", gc + 1)
                    need(pe, "pT_act" if r % 2 == 0 else "pT_dve", 2 * gc + r // 2)
                    for h in range(ROUND):
                        head = r * ROUND + h
                        ins = tr(bank[2 + r % 2][0:n, h * n:(h + 1) * n], p_wide[0:n, par, head * n:(head + 1) * n], ident[0:n, 0:n])
                    ins.then_inc(S["pT_ps"], 1)

                def values_round(r):
                    n = rows_of(gc)
                    need(pe, "pT_act" if r % 2 == 0 else "pT_dve", 2 * gc + r // 2 + 1)
                    if r == 0:
                        need(pe, "v_ready", gc + 1)
                        need(pe, "route_c", 2 * gc)
                    for h in range(ROUND):
                        head = r * ROUND + h
                        ins = mm(bank[5][0:n, head * 17:(head + 1) * 17], pT[0:n, par, head * n:(head + 1) * n], v_one[0:n, par, head, :],
                                 start=True, stop=True)
                    ins.then_inc(S["pv_ps"], 1)

                if live(gd):
                    n, gp = rows_of(gd), 1 - par
                    need(pe, "route_c", 2 * gd + 2)
                    need(pe, "attT_ready", gd)
                    for k in range(2):
                        ins = tr(bank[6][:, k * ROWS:k * ROWS + n], att[0:n, gp, k * 128:(k + 1) * 128], ident[0:n, 0:n])
                    ins.then_inc(S["attT_ps"], 1)
                if live(gb):
                    scores(0)
                if live(gc):
                    turn_round(0)
                    turn_round(1)
                if live(gb):
                    scores(1)
                if live(gc):
                    values_round(0)
                    values_round(1)
                    turn_round(2)
                    turn_round(3)
                if live(gd):
                    n, gp = rows_of(gd), 1 - par
                    need(pe, "attT_ready", gd + 1)
                    need(pe, "att_c", gd)
                    for k in range(2):
                        ins = mm(bank[7][0:n, 0:DIM], attT[:, gp, k, 0:n], wvo_sb[:, 1 + k, :], start=(k == 0), stop=(k == 1))
                    ins.then_inc(S["proj_ps"], 1)
                if live(gb):
                    n, gp = rows_of(gb), 1 - par
                    need(pe, "v_ready", gb)
                    mm(bank[4][0:n, 0:DIM], lat_g[:, gp, 0:n], wvo_sb[:, 0, :], start=True, stop=True).then_inc(S["v_ps"], 1)
                if live(gc):
                    values_round(2)
                    values_round(3)

            sweep(pe, body=phase3, **P3)

            pe.wait_ge(S["att_c"], GROUPS)
            pe.wait_ge(S["resid_done"], GROUPS)
            for g in range(GROUPS + 1):
                if g < GROUPS:
                    n = rows_of(g)
                    need(pe, "x2_ready", g + 1)
                    need(pe, "x2T_ready", g - 1)
                    for k in range(2):
                        ins = tr(bank[g % 2][:, k * ROWS:k * ROWS + n], x2[0:n, g, k * 128:(k + 1) * 128], ident[0:n, 0:n])
                    ins.then_inc(S["x2T_ps"], 1)
                if g >= 1:
                    h = g - 1
                    n = rows_of(h)
                    need(pe, "x2T_ready", h + 1)
                    for k in range(2):
                        ins = mm(bank[2][0:n, h * EXPERTS:(h + 1) * EXPERTS], x2T[:, h % 2, k, 0:n], wr_sb[:, k, :], start=(k == 0), stop=(k == 1))
                    ins.then_inc(S["logits_ps"], 1)
            pe.wait_ge(S["route_in"], 2)
            mm(bank[3][0:ROWS, 0:NE], cst(C_BEFORE, ROWS), lg[:, 10, :], start=True, stop=True)
            mm(bank[4][0:ROWS, 0:NE], cst(C_ONES, ROWS), lg[:, 10, :], start=True, stop=True).then_inc(S["route_ps"], 1)

            pe.sem_inc(S["ug_ps"], 1)
            pe.sem_inc(S["y_ps"], 1)
            pe.wait_ge(S["plan_ready"], 1)
            pe.wait_ge(S["ones_ready"], 2)

            def turn_x(j, buf, quad):
                need(pe, f"xs_loaded{buf}", quad * 16 + 16)
                need(pe, "xs_lo", j)
                for k in range(2):
                    ins = tr(bank[7][:, k * 128:(k + 1) * 128], xs[:, buf, k * 128:(k + 1) * 128], ident)
                ins.then_inc(S["xsT_ps"], 1)

            def up(j, par, c, e, w0):
                if c == 0:
                    pe.wait_ge(S["weights_ready"], e * 6 + 6)
                    pe.wait_ge(S["bias_ready"], e * 16 + 16)
                    need(pe, "xs_lo", j + 1)
                need(pe, "gelu_c", 4 * (j - 1) + 2 * c + 2)
                for t, w in enumerate((wi_hl, wg_hl)):
                    dst = bank[2 * c + t][:, :]
                    mm(dst, ones2[:, :], bias_sb[:, ds(w0 + t * FFN + c * 512, 512)], start=True, stop=False)
                    for k in range(2):
                        at = ds(w0 + k * FFN + c * 512, 512)
                        mm(dst, xsT[0][:, par, k, :], w[0][:, at], start=False, stop=False)
                        mm(dst, xsT[0][:, par, k, :], w[1][:, at], start=False, stop=False)
                        ins = mm(dst, xsT[1][:, par, k, :], w[0][:, at], start=False, stop=(k == 1))
                ins.then_inc(S["ug_ps"], 1)

            def turn_hidden(j, c):
                need(pe, "hid_ready", 2 * j + c + 1)
                need(pe, "hid_lo", 2 * (j - 1) + c + 1)
                for k in range(4):
                    ins = tr(bank[4 + c][:, k * 128:(k + 1) * 128], hid[:, c, k * 128:(k + 1) * 128], ident)
                ins.then_inc(S["hidT_ps"], 1)

            def down(j, par, w0):
                need(pe, "hid_lo", 2 * j + 2)
                need(pe, "y_c", (j - 1) * YC + 1)
                for k in range(8):
                    at = ds(w0 + k * DIM, DIM)
                    mm(bank[6][:, 0:DIM], hidT[0][:, par, k, :], wo_hl[0][:, at], start=(k == 0), stop=False)
                    mm(bank[6][:, 0:DIM], hidT[0][:, par, k, :], wo_hl[1][:, at], start=False, stop=False)
                    ins = mm(bank[6][:, 0:DIM], hidT[1][:, par, k, :], wo_hl[0][:, at], start=False, stop=(k == 7))
                ins.then_inc(S["y_ps"], 1)

            YC = 19

            def of_slot(j):
                e = pe.value_load(slot_expert[0:1, ds(j, 1)], min_val=0, max_val=EXPERTS - 1)
                w = pe.value_load(slot_buffer[0:1, ds(j, 1)], min_val=0, max_val=1)
                return e, w * WSZ

            def slot(j, par, buf, quad):
                first = isinstance(j, int) and j == 0
                e, w0 = of_slot(j)
                up(j, par, 0, e, w0)
                if not (isinstance(j, int) and j + 1 >= SLOTS):
                    turn_x(j + 1, (buf + 1) % 4, quad + (buf + 1) // 4)
                if not first:
                    turn_hidden(j - 1, 1)
                up(j, par, 1, e, w0)
                turn_hidden(j, 0)
                if not first:
                    down(j - 1, 1 - par, of_slot(j - 1)[1])

            turn_x(0, 0, 0)
            for j in range(4):
                slot(j, j % 2, j, 0)
            with pe.Fori(1, SLOTS // 4 - 1) as quad:
                for k in range(4):
                    slot(quad * 4 + k, k % 2, k, quad)
            for j in range(SLOTS - 4, SLOTS):
                slot(j, j % 2, j % 4, j // 4)
            turn_hidden(SLOTS - 1, 1)
            down(SLOTS - 1, (SLOTS - 1) % 2, of_slot(SLOTS - 1)[1])


def kernel(**inputs):
    import numpy as np
    import concourse.bacc as bacc
    from concourse.bass_utils import run_bass_kernel_spmd as run

    x = {k: np.asarray(a) for k, a in inputs.items()}
    P = 16
    side = 96 // P
    patches = x["x"].reshape(IMAGES, 3, side, P, side, P).transpose(0, 2, 4, 3, 5, 1).reshape(IMAGES * PATCHES, PATCH_DIM)

    cols, width = constant_columns()
    consts = np.zeros((128, width), np.float32)
    p = np.arange(128)[:, None]

    def put(which, a):
        lo, hi = cols[which]
        consts[:, lo:hi] = np.broadcast_to(a, (128, hi - lo))
    put(C_IDENT, np.eye(128))
    put(C_BEFORE, p < np.arange(ROWS)[None])
    put(C_ONES, 1.0)
    put(C_HEAD, p // HEAD_DIM == np.arange(8)[None])
    put(C_IMAGE, p // TOKENS == np.arange(3)[None])
    put(C_PATCH, np.concatenate([p % TOKENS != 0, p % TOKENS == 0], 1))
    put(C_RANK, np.tile(EXPERTS - np.arange(EXPERTS), GROUPS)[None])
    put(C_VALID, p + ROWS * np.arange(GROUPS)[None] < ALL_TOKENS)
    put(C_THRESH, np.tile(SLOT * np.arange(19), EXPERTS)[None])
    put(C_SLOTNO, np.repeat(np.arange(SLOTS), 8)[None])
    put(C_SIGN, np.tile([1, -1] * 4, SLOTS)[None])
    half = DIM // 2
    theta = (np.float32(10000.0) ** (np.float32(-2.0) * np.arange(half, dtype=np.float32))).astype(np.float32) / np.float32(half)
    angle = (np.arange(TOKENS, dtype=np.float32)[:, None] * theta[None, :].astype(np.float32)).astype(np.float32)
    sign = np.tile(np.array([-1.0, 1.0], np.float32), half)[:, None]
    rope = np.stack([np.repeat(np.cos(angle).T, 2, axis=0), np.repeat(np.sin(angle).T, 2, axis=0) * sign]).astype(np.float32)

    def partner(a):
        return a.reshape(*a.shape[:-1], half, 2)[..., ::-1].reshape(a.shape)

    def columns(a):
        return a.reshape(-1, 128).T
    a = {k[len("L0_attn_"):]: t for k, t in x.items() if k.startswith("L0_attn_")}
    arrays = {
        "patches": patches,
        "consts": consts,
        "w_proj": x["L0_tok_W_proj"],
        "rows_pack": np.concatenate([x["L0_tok_ln2_g"], x["L0_tok_ln2_b"], x["L0_tok_cls_token"].reshape(-1), x["L0_tok_b_proj"],
                                     a["Wu_v_b"], a["Wo_b"], x["L0_ffn_br"]]),
        "row_tables": np.stack([x["L0_tok_ln1_g"], x["L0_tok_ln1_b"]]),
        "pos": x["L0_tok_pos_emb"][0],
        "wd": np.concatenate([a["Wd_q_w"], a["Wd_kv_w"]], 1),
        "wq": np.concatenate([a["Wq_r_w"], partner(a["Wq_r_w"]), a["Wu_q_w"]], 1),
        "wk": np.concatenate([a["Wk_r_w"], partner(a["Wk_r_w"]), a["Wu_k_w"]], 0),
        "wv_o": np.concatenate([a["Wu_v_w"], a["Wo_w"]], 0),
        "cols_pack": np.concatenate([columns(a["Wd_q_b"]), columns(a["Wd_kv_b"]),
                                     columns(a["Wk_r_b"]), columns(partner(a["Wk_r_b"])), columns(a["Wu_k_b"]),
                                     columns(a["Wq_r_b"]), columns(partner(a["Wq_r_b"])), columns(a["Wu_q_b"])], 1),
        "rope": rope,
        "w_router": x["L0_ffn_Wr"],
        "wi": x["L0_ffn_Wi"],
        "wg": x["L0_ffn_Wg"],
        "wo": x["L0_ffn_Wo"],
        "expert_bias": np.concatenate([x["L0_ffn_bi"], x["L0_ffn_bg"]], 0).reshape(128, 128),
        "expert_rows": np.concatenate([x["L0_ffn_bo"].reshape(-1), x["L0_ffn_gamma"].reshape(-1), x["L0_ffn_beta"].reshape(-1)]),
    }
    arrays = {k: np.ascontiguousarray(t) for k, t in arrays.items()}
    f32 = mybir.dt.float32
    nc = bacc.Bacc("TRN2", target_bir_lowering=False, num_devices=1)
    args = {k: nc.dram_tensor(k, t.shape, f32, kind="ExternalInput").ap() for k, t in arrays.items()}
    args["out"] = nc.dram_tensor("out", (ALL_TOKENS, DIM), f32, kind="ExternalOutput").ap()
    args["scr_h"] = nc.dram_tensor("scr_h", (ALL_TOKENS, DIM), f32, kind="Internal").ap()
    args["slots_in"] = nc.dram_tensor("slots_in", (SLOTS * SLOT, DIM), f32, kind="Internal").ap()
    args["slots_out"] = nc.dram_tensor("slots_out", (SLOTS * SLOT, DIM), f32, kind="Internal").ap()
    args["bias_parts"] = nc.dram_tensor("bias_parts", (2, 2 * EXPERTS * FFN), f32, kind="Internal").ap()
    build(nc, **args)
    r = run(nc, [arrays], core_ids=[0])
    return r.results[0]["out"].reshape(IMAGES, TOKENS, DIM)
```

```python
import concourse.bass as bass
from concourse import mybir
from contextlib import ExitStack

IMAGES, PATCHES, TOKENS, DIM = 64, 36, 37, 256
PATCH_DIM = 768
ALL_TOKENS = IMAGES * TOKENS
PER_GROUP = 3
GROUPS = -(-IMAGES // PER_GROUP)
ROWS = PER_GROUP * TOKENS
HEADS, HEAD_DIM = 16, 16
LATENT = 128
EXPERTS, TOP, FFN = 8, 2, 1024
SLOT = 128
X_BUFFERS = 8
CODE = 5
SLOTS = (ALL_TOKENS * TOP + EXPERTS * (SLOT - 1)) // SLOT
CHUNKS = 8
CHUNK = ALL_TOKENS // CHUNKS
CHUNK_IMAGES = CHUNK // TOKENS
SCORE_SCALE = float(1.0 / (HEADS + 2 * LATENT) ** 0.5)
HEAD_SPAN = TOKENS * (HEADS // 2)
ROUND = 4
ROW_TOKEN, ROW_WEIGHT = DIM, DIM + 1
ROW = DIM + 1 + EXPERTS
PIECE = 2 * FFN
PIECES = 3 * EXPERTS
PIECES_EARLY = 12
BIAS_COLS = EXPERTS * (2 * FFN + DIM) // 128
C_IDENT, C_BEFORE, C_ONES, C_HEAD, C_IMAGE, C_PATCH, C_RANK, C_VALID, C_THRESH, C_SLOTNO, C_NOT_IMAGE, C_TOKEN, C_PAD = range(13)


def constant_columns():
    widths = [128, ROWS, ROWS, 8, 3, 2, GROUPS * 8, GROUPS, 8 * 19, SLOTS * 8, 3, GROUPS, 1]
    start, out = 0, []
    for w in widths:
        out.append((start, start + w))
        start += w
    return out, start


def images_of(g):
    return IMAGES - PER_GROUP * (GROUPS - 1) if isinstance(g, int) and g == GROUPS - 1 else PER_GROUP


def build(nc, patches, consts, w_proj, rows_pack, pos, wd, wq, wk, wv_o, cols_pack, rope, w_router,
          expert_weights, expert_bias, expert_rows, out, slots_in, bias_parts, weight_hi, weight_lo):
    f32, f32r, i32 = mybir.dt.float32, mybir.dt.float32r, mybir.dt.int32
    ALU, ACT, AX = mybir.AluOpType, mybir.ActivationFunctionType, mybir.AxisListType
    ds = bass.ds
    cols, const_width = constant_columns()

    whole = ExitStack()
    with whole:
        def sb(name, shape, dt=f32, ctx=whole):
            return ctx.enter_context(nc.sbuf_tensor(name, shape, dt))

        def pb(name, shape, ctx, dt=f32):
            return ctx.enter_context(nc.psum_tensor(name, shape, dt))

        def sem(name):
            return whole.enter_context(nc.semaphore(name))

        const = sb("const", [128, const_width])

        def cst(which, p=128):
            a, b = cols[which]
            return const[0:p, a:b]

        ident = cst(C_IDENT)
        choice_row = sb("choice_row", [ROWS, TOP, GROUPS], i32)
        slot_expert = sb("slot_expert", [1, SLOTS], i32)
        tiles_done = sb("tiles_done", [1, EXPERTS], i32)
        slot_code = sb("slot_code", [1, SLOTS], i32)

        early = ExitStack()
        def eb(name, shape, dt=f32):
            return sb(name, shape, dt, early)
        resid = eb("resid", [ROWS, GROUPS * DIM])
        x1T = eb("x1T", [128, 2, ALL_TOKENS])
        qT = eb("qT", [128, 2, ALL_TOKENS])
        kT = eb("kT", [128, 2, ALL_TOKENS])
        latT = eb("latT", [128, ALL_TOKENS])
        wd_sb = eb("wd_sb", [128, 2, 2 * LATENT])
        wq_sb = eb("wq_sb", [128, 3 * DIM])
        wk_sb = eb("wk_sb", [128, 5, DIM])
        wvo_sb = eb("wvo_sb", [128, 3, DIM])
        wr_sb = eb("wr_sb", [128, 2, EXPERTS])
        colb = eb("colb", [128, 26])
        rope_sb = eb("rope_sb", [128, 2, 2, TOKENS])
        rowb = eb("rowb", [ROWS, 6 * DIM + EXPERTS])
        ln2_g, ln2_b, cls_row, b_proj, b_v, b_o = (rowb[:, i * DIM:(i + 1) * DIM] for i in range(6))
        b_router = rowb[:, 6 * DIM:6 * DIM + EXPERTS]
        pos_sb = eb("pos_sb", [ROWS, DIM])
        ln4_stats = eb("ln4_stats", [ROWS, GROUPS, 6])
        raw_piece = eb("raw_piece", [128, PIECE])
        hi_piece = eb("hi_piece", [128, PIECE], f32r)
        lo_piece = eb("lo_piece", [128, PIECE], f32r)

        one = ExitStack()
        def ob(name, shape, dt=f32):
            return sb(name, shape, dt, one)
        wproj_sb = ob("wproj_sb", [128, 6, DIM])
        bias_raw = ob("bias_raw", [128, BIAS_COLS])
        bias_hl = ob("bias_hl", [128, 2, BIAS_COLS], f32r)
        x_in = ob("x_in", [ROWS, 2, PATCH_DIM])
        x_norm = ob("x_norm", [ROWS, 2, PATCH_DIM])
        x_affT = ob("x_affT", [128, 2, 6, ROWS])
        z_sb = ob("z_sb", [ROWS, 2, DIM])
        z_norm = ob("z_norm", [ROWS, 2, DIM])
        x1 = ob("x1", [ROWS, 2, DIM])
        add_rows = ob("add_rows", [ROWS, DIM])
        mul_rows = ob("mul_rows", [ROWS, DIM])
        tmp_rows = ob("tmp_rows", [ROWS, DIM])
        ln1_st = ob("ln1_st", [ROWS, 2, 2, 6])
        ln2_st = ob("ln2_st", [ROWS, 2, 6])
        ln3_st = ob("ln3_st", [ROWS, 2, 6])
        ln_mv = ob("ln_mv", [ROWS, 2, 3, 2])
        ln_ve = ob("ln_ve", [ROWS, 2, 3])
        ln_sd = ob("ln_sd", [ROWS, 2, 3])
        ln_r0 = ob("ln_r0", [ROWS, 2, 3])
        ln_t = ob("ln_t", [ROWS, 2, 3, 3])
        ln_rs = ob("ln_rs", [ROWS, 2, 3])
        fill = ob("fill", [128, 4, ROW])
        one.close()
        two = ExitStack()
        ctq = sb("ctq", [128, 2, CHUNK], f32, two)
        rot = sb("rot", [128, 2, 3, CHUNK], f32, two)
        two.close()
        three = ExitStack()
        def tb(name, shape, dt=f32):
            return sb(name, shape, dt, three)
        k_blocks = tb("k_blocks", [128, 2, 2, PER_GROUP * HEAD_SPAN])
        q_pad = tb("q_pad", [128, 2, 2, PER_GROUP * (ROWS + TOKENS)])
        lat_g = tb("lat_g", [128, 2, ROWS])
        shifted = tb("shifted", [ROWS, 2, HEADS * TOKENS])
        p_wide = tb("p_wide", [ROWS, 2, HEADS * ROWS])
        pT = tb("pT", [ROWS, 2, HEADS * ROWS])
        v_one = tb("v_one", [ROWS, 2, HEADS, HEAD_DIM + 1])
        top = tb("top", [ROWS, 2, HEADS])
        inv_sum = tb("inv_sum", [ROWS, 2, HEADS])
        att = tb("att", [ROWS, 2, DIM])
        attT = tb("attT", [128, 2, 2, ROWS])
        att_b = tb("att_b", [ROWS, 2, DIM])
        three.close()
        four = ExitStack()
        def fb(name, shape, dt=f32):
            return sb(name, shape, dt, four)
        x2 = fb("x2", [ROWS, GROUPS, ROW])
        x2T = fb("x2T", [128, 2, 2, ROWS])
        mv4 = fb("mv4", [ROWS, GROUPS, 2])
        sc4 = fb("sc4", [ROWS, 8, GROUPS])
        NE = GROUPS * EXPERTS
        lg = fb("lg", [ROWS, 16, NE])
        small = fb("small", [ROWS, 12, GROUPS])
        cnt = fb("cnt", [ROWS, 8, EXPERTS])
        over = fb("over", [ROWS, EXPERTS * 19])
        smap = fb("smap", [1, SLOTS * 8])
        smap_sum = fb("smap_sum", [1, SLOTS])
        code = fb("code", [1, CODE, SLOTS])
        four.close()
        early.close()
        late = ExitStack()
        def lb(name, shape, dt=f32):
            return sb(name, shape, dt, late)
        WSZ = PIECE
        wi_hl = [lb(f"wi_{p}", [128, 2 * WSZ], f32r) for p in ("hi", "lo")]
        wg_hl = [lb(f"wg_{p}", [128, 2 * WSZ], f32r) for p in ("hi", "lo")]
        wo_hl = [lb(f"wo_{p}", [128, 2 * WSZ], f32r) for p in ("hi", "lo")]
        bias_sb = lb("bias_sb", [2, 2 * WSZ], f32r)
        ones2 = lb("ones2", [2, 128], f32r)
        bias_out = lb("bias_out", [2, 2 * DIM], f32r)
        exp_rows = lb("exp_rows", [128, 2 * 2 * DIM])
        xs = lb("xs", [128, X_BUFFERS, ROW])
        xsT = [lb(f"xsT_{p}", [128, 2, 2, 128], f32r) for p in ("hi", "lo")]
        act_u = lb("act_u", [128, 2, 512])
        act_g = lb("act_g", [128, 2, 512])
        hid = lb("hid", [128, 2, 512])
        hidT = [lb(f"hidT_{p}", [128, 2, 8, 128], f32r) for p in ("hi", "lo")]
        y_res = lb("y_res", [128, DIM])
        y_norm = lb("y_norm", [128, 2, DIM])
        y_scaled = lb("y_scaled", [128, DIM])
        y_shifted = lb("y_shifted", [128, DIM])
        y_out = lb("y_out", [128, 2, DIM])
        y_token = lb("y_token", [128, 2, 1], i32)
        y_st = lb("y_st", [128, 6])
        y_mv = lb("y_mv", [128, 2])
        y_sc = lb("y_sc", [128, 12])
        y_int = lb("y_int", [128, 2], i32)
        late.close()
        bank = [pb(f"bank{i}", [128, 512], whole) for i in range(8)]

        S = {n: sem(n) for n in (
            "const_loaded wproj_loaded rows_loaded weights_loaded piece_loaded piece_hi piece_lo hi_stored lo_stored fill_ready x_loaded0 x_loaded1 setup_done setup_c "
            "ln1_c ln2_c ln3_c ln_c std_ready x_norm_ready xT_ps x_affT_ready z_ps z_norm_ready resid_c "
            "x1_ready x1T_ps x1T_ready "
            "lat_ps lat_ready rope_ps rope_c "
            "attn_zero keys_ready keys_act_ready queries_ready scores_ps v_ps v_ready max_c p_wide_ready "
            "pT_ps pT_act pT_dve pv_ps att_c attT_ps attT_ready proj_ps resid_done "
            "ln4_c x2_ready x2T_ps x2T_ready logits_ps sd4_ready route_c route_ps route_in exp4_ready "
            "bias_loaded bias_c bias_stored filled resid_stored "
            "scattered plan_ready code_c "
            "up_loaded down_loaded rows5_loaded ones_ready added "
            "" + " ".join(f"xs_loaded{i}" for i in range(X_BUFFERS)) + " xsT_ps xs_hi xs_lo ug_ps gelu_c hid_ready hidT_ps hid_hi hid_lo y_ps y_c y_norm_ready y_scaled_c y_out_ready ").split()}

        block = whole.enter_context(nc.Block())

        def need(eng, name, n):
            if isinstance(n, int) and n <= 0:
                return
            eng.wait_ge(S[name], n)

        def need_first(eng, name, n):
            if isinstance(n, int) and n <= 0:
                return
            eng.wait_ge(S[name], n)
            eng.nop(nofuse=True)

        def sweep(eng, head, tail, total, body):
            for s in range(min(head, total)):
                body(s, s % 2, s // 2)
            if tail > head:
                with eng.Fori(head // 2, tail // 2) as half:
                    body(half * 2, 0, half)
                    body(half * 2 + 1, 1, half)
            for s in range(tail, total):
                body(s, s % 2, s // 2)

        def slot_groups(eng, group, tail):
            group(0, 0, 4)
            with eng.Fori(0, (SLOTS - 4 - tail) // X_BUFFERS) as turn:
                group(turn * X_BUFFERS + 4, 4, X_BUFFERS)
            if tail:
                group(SLOTS - tail, 4, tail)

        def live(g):
            return not isinstance(g, int) or 0 <= g < GROUPS

        def rows_of(g):
            return images_of(g) * TOKENS

        P1 = dict(head=6, tail=20, total=GROUPS + 5)
        P3 = dict(head=4, tail=20, total=GROUPS + 3)
        P2 = dict(head=2, tail=8, total=CHUNKS)
        UP_LOADS, DOWN_LOADS = 16 * 5, 16 * 3
        YC = 13

        def x_loaded_after(g, pair):
            return pair * (16 * PER_GROUP) + 16 * images_of(g)

        @block.sync
        def _(sp):
            def load_x(g, par):
                need(sp, "x_norm_ready", g - 1)
                for i in range(images_of(g)):
                    sp.dma_start(x_in[TOKENS * i + 1:TOKENS * (i + 1), par, :],
                                 patches[ds((g * PER_GROUP + i) * PATCHES, PATCHES), :]).then_inc(S[f"x_loaded{par}"], 16)

            sp.wait_ge(S["setup_done"], 1)
            load_x(0, 0)
            sp.dma_start(const[:, :], consts).then_inc(S["const_loaded"], 16)
            load_x(1, 1)
            sp.dma_start(rowb[:, :], rows_pack.partition_broadcast(ROWS)).then_inc(S["rows_loaded"], 16)
            for i in range(PER_GROUP):
                sp.dma_start(pos_sb[TOKENS * i:TOKENS * (i + 1), :], pos).then_inc(S["rows_loaded"], 16)
            sp.dma_start(colb[:, :], cols_pack).then_inc(S["rows_loaded"], 16)
            sp.dma_start(wproj_sb[:, :, :], w_proj.rearrange("(k p) n -> p k n", p=128)).then_inc(S["wproj_loaded"], 16)
            sp.dma_start(wd_sb[:, :, :], wd.rearrange("(k p) n -> p k n", p=128)).then_inc(S["weights_loaded"], 16)
            sp.dma_start(wq_sb[:, :], wq).then_inc(S["weights_loaded"], 16)
            sp.dma_start(wk_sb[:, :, :], wk.rearrange("(k p) n -> p k n", p=128)).then_inc(S["weights_loaded"], 16)
            sp.dma_start(wvo_sb[:, :, :], wv_o.rearrange("(k p) n -> p k n", p=128)).then_inc(S["weights_loaded"], 16)
            sp.dma_start(wr_sb[:, :, :], w_router.rearrange("(k p) n -> p k n", p=128)).then_inc(S["weights_loaded"], 16)
            sp.dma_start(rope_sb[:, :, :, :], rope.rearrange("t (k p) n -> p t k n", p=128)).then_inc(S["weights_loaded"], 16)

            sp.dma_start(bias_raw[:, :], expert_bias).then_inc(S["bias_loaded"], 16)

            def out_high(q):
                need(sp, "piece_hi", q + 1)
                sp.dma_start(weight_hi[ds(q * 128, 128), :], hi_piece[:, :].bitcast(f32)).then_inc(S["hi_stored"], 16)

            def out_low(q):
                need(sp, "piece_lo", 2 * q + 2)
                sp.dma_start(weight_lo[ds(q * 128, 128), :], lo_piece[:, :].bitcast(f32)).then_inc(S["lo_stored"], 16)

            def piece_in(q):
                need(sp, "piece_lo", 2 * q)
                sp.dma_start(raw_piece[:, :], expert_weights[ds(q * 128, 128), :]).then_inc(S["piece_loaded"], 16)

            def within(pair, lo, hi):
                return not isinstance(pair, int) or lo <= pair < hi

            sp.wait_ge(S["bias_c"], 2)
            sp.dma_start(bias_parts.rearrange("t (p n) -> p t n", n=BIAS_COLS), bias_hl[:, :, :].bitcast(f32)).then_inc(S["bias_stored"], 16)

            def phase1(s, par, pair):
                if not (isinstance(s, int) and (s < 2 or s >= GROUPS)):
                    load_x(s, par)
                if par == 1:
                    if within(pair, 1, PIECES_EARLY + 1):
                        out_high(pair - 1)
                    if within(pair, 0, PIECES_EARLY):
                        piece_in(pair)
                elif within(pair, 2, PIECES_EARLY + 2):
                    out_low(pair - 2)
            sweep(sp, body=phase1, **P1)
            sp.wait_ge(S["fill_ready"], 2)
            per = 128 * 4
            for i in range(SLOTS // 4):
                sp.dma_start(slots_in[i * per:(i + 1) * per, :].rearrange("(s p) d -> p s d", p=128),
                             fill[:, :, :]).then_inc(S["filled"], 16)
            sp.dma_start(out[ALL_TOKENS:ALL_TOKENS + 128, :], fill[:, 0, 0:DIM]).then_inc(S["filled"], 16)
            sp.wait_ge(S["filled"], 16 * (SLOTS // 4 + 1))
            sp.wait_ge(S["bias_stored"], 16)

            def phase3(s, par, pair):
                if par == 0:
                    q, late = PIECES_EARLY + pair, PIECES - PIECES_EARLY
                    if within(pair, 1, late + 1):
                        out_high(q - 1)
                    if within(pair, 0, late):
                        piece_in(q)
                    if within(pair, 1, late + 1):
                        out_low(q - 1)
                g = s - 3
                if live(g):
                    n = rows_of(g)
                    need(sp, "resid_done", g + 1)
                    sp.dma_start(out[ds(g * ROWS, n), :], resid[0:n, ds(g * DIM, DIM)]).then_inc(S["resid_stored"], 16)
            sweep(sp, body=phase3, **P3)
            sp.wait_ge(S["hi_stored"], 16 * PIECES)
            sp.wait_ge(S["lo_stored"], 16 * PIECES)
            sp.wait_ge(S["resid_stored"], 16 * GROUPS)
            sp.wait_ge(S["x2_ready"], GROUPS)

            bias_up = bias_parts[:, 0:2 * EXPERTS * FFN].rearrange("t (w e n) -> t w e n", w=2, e=EXPERTS)
            bias_down = bias_parts[:, 2 * EXPERTS * FFN:].rearrange("t (e n) -> t e n", e=EXPERTS)
            for e in range(EXPERTS):
                need(sp, "up_loaded", UP_LOADS * e)
                need(sp, "down_loaded", DOWN_LOADS * e)
                need(sp, "rows5_loaded", 16 * e)
                if e >= 2:
                    if e == 2:
                        sp.wait_ge(S["plan_ready"], 1)
                    done = sp.value_load(tiles_done[0:1, e - 2:e - 1], min_val=0, max_val=SLOTS)
                    sp.wait_ge(S["ug_ps"], done * 2 + 1)
                to = slice((e % 2) * WSZ, (e % 2 + 1) * WSZ)

                def load_part(j, name):
                    q = 3 * e + j
                    for dst, src in zip((wi_hl, wg_hl, wo_hl)[j], (weight_hi, weight_lo)):
                        sp.dma_start(dst[:, to].bitcast(f32), src[q * 128:(q + 1) * 128, :]).then_inc(S[name], 16)
                load_part(0, "up_loaded")
                load_part(1, "up_loaded")
                if e == 0:
                    sp.wait_ge(S["route_in"], 1)
                sp.dma_start(bias_sb[:, to].bitcast(f32).rearrange("t (w n) -> t w n", w=2), bias_up[:, :, e, :]).then_inc(S["up_loaded"], 16)
                if e >= 2:
                    sp.wait_ge(S["y_ps"], done + 1)
                load_part(2, "down_loaded")
                sp.dma_start(bias_out[:, (e % 2) * DIM:(e % 2 + 1) * DIM].bitcast(f32), bias_down[:, e, :]).then_inc(S["down_loaded"], 16)
                if e >= 2:
                    sp.wait_ge(S["y_out_ready"], done + 1)
                sp.dma_start(exp_rows[:, (e % 2) * 2 * DIM:(e % 2 + 1) * 2 * DIM],
                             expert_rows[e, :].partition_broadcast(128)).then_inc(S["rows5_loaded"], 16)

        @block.gpsimd
        def _(pool):
            pool.memset(fill[:, :, :], 0.0).then_inc(S["fill_ready"], 1)
            pool.wait_ge(S["fill_ready"], 1)
            pool.wait_ge(S["const_loaded"], 16)
            pool.tensor_copy(fill[:, :, ROW_TOKEN:ROW_TOKEN + 1].bitcast(i32),
                             cst(C_PAD).unsqueeze(1).broadcast_to([128, 4, 1])).then_inc(S["fill_ready"], 1)
            pool.wait_ge(S["bias_loaded"], 16)
            pool.tensor_copy(bias_hl[:, 0, :], bias_raw[:, :]).then_inc(S["bias_c"], 1)
            pool.wait_ge(S["bias_c"], 1)
            pool.tensor_tensor(bias_hl[:, 1, :], bias_raw[:, :], bias_hl[:, 0, :].bitcast(f32), ALU.subtract).then_inc(S["bias_c"], 1)

            def split_piece(pair, base, limit, half):
                if isinstance(pair, int) and base + pair >= limit:
                    return
                q = base + pair
                part = slice(half * (PIECE // 2), (half + 1) * (PIECE // 2))
                if half == 0:
                    need_first(pool, "lo_stored", q * 16)
                    need_first(pool, "piece_hi", q + 1)
                pool.tensor_tensor(lo_piece[:, part], raw_piece[:, part], hi_piece[:, part].bitcast(f32), ALU.subtract).then_inc(S["piece_lo"], 1)

            def phase1(s, par, pair):
                g = s - 3
                if live(g):
                    n = rows_of(g)
                    here = resid[0:n, ds(g * DIM, DIM)]
                    need_first(pool, "z_norm_ready", g + 1)
                    pool.tensor_tensor(here, z_norm[0:n, 1 - par, :], mul_rows[0:n, :], ALU.mult).then_inc(S["resid_c"], 1)
                    need_first(pool, "resid_c", 2 * g + 1)
                    pool.tensor_tensor(here, here, add_rows[0:n, :], ALU.add).then_inc(S["resid_c"], 1)
                if par == 1:
                    for half in range(2):
                        split_piece(pair, 0, PIECES_EARLY, half)

            pool.wait_ge(S["rows_loaded"], 16 * (2 + PER_GROUP))
            pool.wait_ge(S["setup_c"], 4)
            sweep(pool, body=phase1, **P1)

            pool.wait_ge(S["rope_c"], 4 * 4 * CHUNKS)
            pool.wait_ge(S["lat_ready"], 2 * CHUNKS)
            pool.wait_ge(S["filled"], 16 * (SLOTS // 4 + 1))

            def phase3(s, par, pair):
                if live(s):
                    m = images_of(s)
                    need_first(pool, "scores_ps", 2 * (s - 1))
                    k_src = kT[:, 0, ds(s * ROWS, m * TOKENS)].rearrange("p (i t) -> p i t", t=TOKENS)
                    pool.tensor_tensor(
                        k_blocks[:, par, 0, 0:m * HEAD_SPAN].rearrange("p (i h t) -> p i h t", i=m, h=8),
                        k_src.unsqueeze(2).broadcast_to([128, m, 8, TOKENS]),
                        cst(C_HEAD).unsqueeze(1).unsqueeze(3).broadcast_to([128, m, 8, TOKENS]), ALU.mult).then_inc(S["keys_ready"], 1)
                    need_first(pool, "v_ps", s - 1)
                    pool.tensor_copy(lat_g[:, par, 0:m * TOKENS], latT[:, ds(s * ROWS, m * TOKENS)]).then_inc(S["keys_ready"], 1)
                if par == 1:
                    for half in range(2):
                        split_piece(pair, PIECES_EARLY, PIECES, half)

            sweep(pool, body=phase3, **P3)

            pool.wait_ge(S["plan_ready"], 1)
            for g in range(GROUPS):
                n = rows_of(g)
                for c in range(TOP):
                    pool.indirect_dma_start(out=slots_in, out_offset=bass.IndirectOffsetOnAxis(ap=choice_row[0:n, c, g:g + 1], axis=0),
                                            in_=x2[0:n, g, :], in_offset=None).then_inc(S["scattered"], 16)

            pool.wait_ge(S["resid_stored"], 16 * GROUPS)
            pool.sem_inc(S["y_out_ready"], 1)

            def add_slot(j, buf):
                par = buf % 2
                e = pool.value_load(slot_expert[0:1, ds(j, 1)], min_val=0, max_val=EXPERTS - 1)
                row = (e % 2) * (2 * DIM)
                need_first(pool, "rows5_loaded", e * 16 + 16)
                need_first(pool, "y_norm_ready", j + 1)
                pool.tensor_tensor(y_scaled[:, :], y_norm[:, par, :], exp_rows[:, ds(row, DIM)], ALU.mult).then_inc(S["y_scaled_c"], 1)
                need_first(pool, "y_scaled_c", 2 * j + 1)
                pool.tensor_tensor(y_shifted[:, :], y_scaled[:, :], exp_rows[:, ds(row + DIM, DIM)], ALU.add).then_inc(S["y_scaled_c"], 1)
                need_first(pool, "y_scaled_c", 2 * j + 2)
                need_first(pool, "added", 16 * j)
                pool.tensor_copy(y_token[:, par, :], xs[:, buf, ROW_TOKEN:ROW_TOKEN + 1].bitcast(i32))
                pool.tensor_tensor(y_out[:, par, :], y_shifted[:, :], xs[:, buf, ds(e + ROW_WEIGHT, 1)].broadcast_to([128, DIM]),
                                   ALU.mult).then_inc(S["y_out_ready"], 1)
                need_first(pool, "y_out_ready", j + 2)
                pool.indirect_dma_start(out=out, out_offset=bass.IndirectOffsetOnAxis(ap=y_token[:, par, :], axis=0),
                                        in_=y_out[:, par, :], in_offset=None, compute_op=ALU.add).then_inc(S["added"], 16)

            def group(j, buf, count):
                for k in range(count):
                    add_slot(j + k, (buf + k) % X_BUFFERS)
            slot_groups(pool, group, tail=0)
            pool.wait_ge(S["added"], 16 * SLOTS)

        @block.scalar
        def _(act):
            A = act.activation

            def phase1(s, par, pair):
                g = s - 1
                if live(g):
                    n, gp = rows_of(g), 1 - par
                    need(act, "xT_ps", g + 1)
                    need(act, "z_ps", g - 1)
                    for k in range(6):
                        ins = A(x_affT[:, gp, k, 0:n], bank[k // 3][:, (k % 3) * ROWS:(k % 3) * ROWS + n], ACT.Identity,
                                scale=colb[:, 14 + k:15 + k], bias=colb[:, 20 + k:21 + k])
                        if k % 3 == 2:
                            ins.then_inc(S["x_affT_ready"], 1)
                need(act, "ln_c", 6 * s + 1)
                A(ln_sd[:, par, :], ln_ve[:, par, :], ACT.Sqrt).then_inc(S["std_ready"], 1)
                g = s - 5
                if live(g):
                    n = rows_of(g)
                    need(act, "x1T_ps", g + 1)
                    A(x1T[:, :, ds(g * ROWS, n)], bank[4][:, 0:2 * ROWS].rearrange("p (k n) -> p k n", k=2)[:, :, 0:n],
                      ACT.Copy).then_inc(S["x1T_ready"], 1)

            act.wait_ge(S["rows_loaded"], 16 * (2 + PER_GROUP))
            sweep(act, body=phase1, **P1)

            def phase2(c, par, pair):
                need(act, "rope_ps", 4 * (c - 1))
                need(act, "lat_ps", 2 * c + 1)
                A(ctq[:, par, :], bank[0][:, 0:CHUNK], ACT.Identity, bias=colb[:, 0:1]).then_inc(S["lat_ready"], 1)
                need(act, "lat_ps", 2 * c + 2)
                A(latT[:, ds(c * CHUNK, CHUNK)], bank[1][:, 0:CHUNK], ACT.Identity, bias=colb[:, 1:2]).then_inc(S["lat_ready"], 1)

            sweep(act, body=phase2, **P2)

            act.wait_ge(S["rope_c"], 4 * 4 * CHUNKS)
            act.wait_ge(S["attn_zero"], 2)

            def copy_round(g, gp, r):
                n = rows_of(g)
                b = bank[2 + r % 2]
                need(act, "pT_ps", 4 * g + r + 1)
                need(act, "pv_ps", 4 * (g - 1))
                A(pT[0:n, gp, r * ROUND * n:(r + 1) * ROUND * n], b[0:n, 0:ROUND * n], ACT.Copy).then_inc(S["pT_act"], 1)

            def phase3(s, par, pair):
                if live(s - 2):
                    copy_round(s - 2, par, 0)
                g = s - 3
                if live(g):
                    n, gp = rows_of(g), 1 - par
                    need(act, "attT_ps", g + 1)
                    need(act, "proj_ps", g - 1)
                    A(attT[:, gp, :, 0:n], bank[6][:, 0:2 * ROWS].rearrange("p (k n) -> p k n", k=2)[:, :, 0:n], ACT.Copy).then_inc(S["attT_ready"], 1)
                if live(s - 2):
                    copy_round(s - 2, par, 2)
                g = s - 1
                if live(g):
                    n, gp = rows_of(g), 1 - par
                    need(act, "max_c", 2 * g + 2)
                    need(act, "pT_ps", 4 * (g - 1))
                    m = images_of(g)
                    wide = p_wide[0:n, gp, 0:HEADS * n].rearrange("p (h i t) -> p h i t", h=HEADS, i=m)
                    for i in range(m):
                        ins = A(wide[:, :, i, :], shifted[0:n, gp, :].rearrange("p (h t) -> p h t", t=TOKENS), ACT.Exp,
                                scale=SCORE_SCALE, bias=cst(C_NOT_IMAGE, n)[:, i:i + 1])
                    ins.then_inc(S["p_wide_ready"], 1)
                if live(s):
                    m = images_of(s)
                    need(act, "scores_ps", 2 * (s - 1))
                    A(q_pad[:, par, :, :].rearrange("p h (i w) -> p h i w", i=PER_GROUP)[:, :, 0:m, 0:TOKENS],
                      qT[:, :, ds(s * ROWS, m * TOKENS)].rearrange("p h (i t) -> p h i t", t=TOKENS), ACT.Copy).then_inc(S["queries_ready"], 1)
                    k_src = kT[:, 1, ds(s * ROWS, m * TOKENS)].rearrange("p (i t) -> p i t", t=TOKENS)
                    blocks = k_blocks[:, par, 1, 0:m * HEAD_SPAN].rearrange("p (i h t) -> p i h t", i=m, h=8)
                    for h in range(8):
                        ins = A(blocks[:, :, h, :], k_src, ACT.Copy, scale=cst(C_HEAD)[:, h:h + 1])
                    ins.then_inc(S["keys_act_ready"], 1)

            sweep(act, body=phase3, **P3)

            act.wait_ge(S["ln4_c"], GROUPS + 2)
            A(sc4[:, 1, :], sc4[:, 0, :], ACT.Sqrt).then_inc(S["sd4_ready"], 1)
            for g in range(GROUPS):
                n = rows_of(g)
                need(act, "x2T_ps", g + 1)
                need(act, "logits_ps", g - 1)
                A(x2T[:, g % 2, :, 0:n], bank[g % 2][:, 0:2 * ROWS].rearrange("p (k n) -> p k n", k=2)[:, :, 0:n], ACT.Copy).then_inc(S["x2T_ready"], 1)
            act.wait_ge(S["route_in"], 1)
            A(lg[:, 2, :], lg[:, 1, :], ACT.Exp).then_inc(S["exp4_ready"], 1)

            act.wait_ge(S["scattered"], 16 * 2 * GROUPS)
            act.wait_ge(S["hi_stored"], 16 * PIECES)
            act.wait_ge(S["lo_stored"], 16 * PIECES)
            act.wait_ge(S["resid_stored"], 16 * GROUPS)
            act.wait_ge(S["plan_ready"], 1)

            def load_slot(j, buf):
                act.dma_start(xs[:, buf, :], slots_in[ds(j * SLOT, SLOT), :]).then_inc(S[f"xs_loaded{buf}"], 16)

            def split_x(j, par):
                need(act, "xsT_ps", j + 1)
                need(act, "ug_ps", 2 * (j - 1) + 1)
                A(xsT[0][:, par, :, :], bank[7][:, 0:256].rearrange("p (k n) -> p k n", k=2), ACT.Copy).then_inc(S["xs_hi"], 1)

            def gated(j, c):
                need(act, "ug_ps", 2 * j + c + 2)
                need(act, "hid_ready", 2 * (j - 1) + c + 1)
                A(act_u[:, c, :], bank[2 * c][:, :], ACT.Gelu).then_inc(S["gelu_c"], 1)
                A(act_g[:, c, :], bank[2 * c + 1][:, :], ACT.Tanh, scale=0.5).then_inc(S["gelu_c"], 1)

            def split_hidden(j, par, c):
                need(act, "hidT_ps", 2 * j + c + 1)
                need(act, "y_ps", j)
                A(hidT[0][:, par, 4 * c:4 * c + 4, :], bank[4 + c][:, :].rearrange("p (k n) -> p k n", k=4), ACT.Copy, scale=0.5).then_inc(S["hid_hi"], 1)

            def slot(j, buf, first, last):
                par = buf % 2
                gated(j, 0)
                if not first:
                    split_hidden(j - 1, 1 - par, 1)
                if not last:
                    split_x(j + 1, 1 - par)
                gated(j, 1)
                split_hidden(j, par, 0)
                if not (isinstance(j, int) and j + 4 >= SLOTS):
                    need(act, "y_out_ready", j - 2)
                    load_slot(j + 4, (buf + 4) % X_BUFFERS)

            def group(j, buf, count):
                for k in range(count):
                    slot(j + k, (buf + k) % X_BUFFERS, isinstance(j, int) and j + k == 0, isinstance(j, int) and j + k + 1 == SLOTS)

            for j in range(4):
                load_slot(j, j)
            split_x(0, 0)
            slot_groups(act, group, tail=8)
            split_hidden(SLOTS - 1, (SLOTS - 1) % 2, 1)

        @block.vector
        def _(v):
            v.memset(x_in[:, :, :], 0.0).then_inc(S["setup_done"], 1)
            v.memset(ln_mv[:, :, :, :], 1.0).then_inc(S["setup_c"], 1)
            v.wait_ge(S["const_loaded"], 16)
            v.wait_ge(S["rows_loaded"], 16 * (2 + PER_GROUP))
            is_patch, is_cls = cst(C_PATCH, ROWS)[:, 0:1], cst(C_PATCH, ROWS)[:, 1:2]
            v.tensor_scalar(mul_rows[:, :], ln2_g, is_patch, None, ALU.mult).then_inc(S["setup_c"], 1)
            v.scalar_tensor_tensor(tmp_rows[:, :], ln2_b, is_patch, pos_sb[:, :], ALU.mult, ALU.add).then_inc(S["setup_c"], 1)
            v.wait_ge(S["setup_c"], 3)
            v.scalar_tensor_tensor(add_rows[:, :], cls_row, is_cls, tmp_rows[:, :], ALU.mult, ALU.add).then_inc(S["setup_c"], 1)

            def round_piece(pair, base, limit):
                if isinstance(pair, int) and base + pair >= limit:
                    return
                q = base + pair
                need_first(v, "hi_stored", q * 16)
                need_first(v, "piece_loaded", q * 16 + 16)
                v.tensor_copy(hi_piece[:, :], raw_piece[:, :]).then_inc(S["piece_hi"], 1)

            def phase1(s, par, pair):
                g1, g2, g3 = s, s - 3, s - 4
                if live(g1):
                    n = rows_of(g1)
                    need(v, f"x_loaded{par}", x_loaded_after(g1, pair))
                    for b in range(2):
                        v.bn_stats(ln1_st[0:n, par, b, :], x_in[0:n, par, b * 384:(b + 1) * 384]).then_inc(S["ln1_c"], 1)
                if live(g2):
                    n = rows_of(g2)
                    need(v, "z_ps", g2 + 1)
                    v.tensor_tensor(z_sb[0:n, par, :], bank[2 + (1 - par)][0:n, 0:DIM], b_proj[0:n, :], ALU.add).then_inc(S["ln2_c"], 1)
                if live(g1):
                    n = rows_of(g1)
                    need_first(v, "ln1_c", 3 * g1 + 2)
                    v.bn_aggr(ln_mv[0:n, par, 0, :], ln1_st[0:n, par, :, :]).then_inc(S["ln1_c"], 1)
                if live(g3):
                    n = rows_of(g3)
                    need(v, "resid_c", 2 * g3 + 2)
                    v.bn_stats(ln3_st[0:n, par, :], resid[0:n, ds(g3 * DIM, DIM)]).then_inc(S["ln3_c"], 1)
                if live(g2):
                    n = rows_of(g2)
                    need(v, "ln2_c", 3 * g2 + 1)
                    v.bn_stats(ln2_st[0:n, par, :], z_sb[0:n, par, :]).then_inc(S["ln2_c"], 1)
                if live(g3):
                    n = rows_of(g3)
                    need_first(v, "ln3_c", 2 * g3 + 1)
                    v.bn_aggr(ln_mv[0:n, par, 2, :], ln3_st[0:n, par, :]).then_inc(S["ln3_c"], 1)
                if live(g2):
                    n = rows_of(g2)
                    need_first(v, "ln2_c", 3 * g2 + 2)
                    v.bn_aggr(ln_mv[0:n, par, 1, :], ln2_st[0:n, par, :]).then_inc(S["ln2_c"], 1)
                if live(g1): need(v, "ln1_c", 3 * g1 + 3)
                if live(g2): need(v, "ln2_c", 3 * g2 + 3)
                if live(g3): need(v, "ln3_c", 2 * g3 + 2)
                ve, r0 = ln_ve[:, par, :], ln_r0[:, par, :]
                t = [ln_t[:, par, i, :] for i in range(3)]
                v.tensor_scalar(ve, ln_mv[:, par, :, 1], 1e-5, None, ALU.add).then_inc(S["ln_c"], 1)
                need(v, "std_ready", s + 1)
                v.reciprocal(r0, ln_sd[:, par, :]).then_inc(S["ln_c"], 1)
                need(v, "ln_c", 6 * s + 2)
                v.tensor_tensor(t[0], r0, r0, ALU.mult).then_inc(S["ln_c"], 1)
                need(v, "ln_c", 6 * s + 3)
                v.tensor_tensor(t[1], t[0], ve, ALU.mult).then_inc(S["ln_c"], 1)
                need(v, "ln_c", 6 * s + 4)
                v.tensor_scalar(t[2], t[1], -0.5, 1.5, ALU.mult, ALU.add).then_inc(S["ln_c"], 1)
                need(v, "ln_c", 6 * s + 5)
                v.tensor_tensor(ln_rs[:, par, :], r0, t[2], ALU.mult).then_inc(S["ln_c"], 1)
                need(v, "ln_c", 6 * s + 6)

                def norm(o, i, n, w, name):
                    v.tensor_scalar(o, i, ln_mv[0:n, par, w, 0:1], ln_rs[0:n, par, w:w + 1], ALU.subtract, ALU.mult).then_inc(S[name], 1)
                if live(g1):
                    n = rows_of(g1)
                    need(v, "xT_ps", g1 - 1)
                    norm(x_norm[0:n, par, :], x_in[0:n, par, :], n, 0, "x_norm_ready")
                if live(g2):
                    n = rows_of(g2)
                    need(v, "resid_c", 2 * (g2 - 1))
                    norm(z_norm[0:n, 1 - par, :], z_sb[0:n, par, :], n, 1, "z_norm_ready")
                if live(g3):
                    n = rows_of(g3)
                    need(v, "x1T_ps", g3 - 1)
                    norm(x1[0:n, par, :], resid[0:n, ds(g3 * DIM, DIM)], n, 2, "x1_ready")
                if par == 1:
                    round_piece(pair, 0, PIECES_EARLY)

            sweep(v, body=phase1, **P1)
            v.wait_ge(S["x1T_ready"], GROUPS)
            v.wait_ge(S["resid_c"], 2 * GROUPS)
            v.wait_ge(S["weights_loaded"], 16 * 6)

            def phase2(c, par, pair):
                for j in range(4):
                    half, q, tri = j % 2, j // 2, c * 4 + j
                    base = 3 * (j % 2)
                    ps = [bank[2 + base + i][:, 0:CHUNK] for i in range(3)]
                    t = [rot[:, j % 2, i, :] for i in range(3)]
                    bcol = 2 + 6 * q + half
                    table = [rope_sb[:, w, half, :].unsqueeze(1).broadcast_to([128, CHUNK_IMAGES, TOKENS]) for w in range(2)]

                    def im(x):
                        return x.rearrange("p (i t) -> p i t", t=TOKENS)
                    need(v, "rope_ps", tri + 1)
                    need(v, "rope_c", tri * 4 - 4)
                    v.scalar_tensor_tensor(im(t[0]), im(ps[0]), colb[:, bcol:bcol + 1], table[0], ALU.add, ALU.mult).then_inc(S["rope_c"], 1)
                    v.scalar_tensor_tensor(im(t[1]), im(ps[1]), colb[:, bcol + 2:bcol + 3], table[1], ALU.add, ALU.mult).then_inc(S["rope_c"], 1)
                    need(v, "rope_c", tri * 4 + 1)
                    v.scalar_tensor_tensor(t[2], ps[2], colb[:, bcol + 4:bcol + 5], t[0], ALU.add, ALU.add).then_inc(S["rope_c"], 1)
                    need(v, "rope_c", tri * 4 + 3)
                    v.tensor_tensor((qT if q else kT)[:, half, ds(c * CHUNK, CHUNK)], t[2], t[1], ALU.add).then_inc(S["rope_c"], 1)

            sweep(v, body=phase2, **P2)
            v.wait_ge(S["rope_c"], 4 * 4 * CHUNKS)
            v.wait_ge(S["rope_ps"], 4 * CHUNKS)

            v.wait_ge(S["filled"], 16 * (SLOTS // 4 + 1))
            v.memset(q_pad[:, :, :, :], 0.0).then_inc(S["attn_zero"], 1)
            v.memset(v_one[:, :, :, :], 1.0).then_inc(S["attn_zero"], 1)
            v.wait_ge(S["attn_zero"], 2)

            def copy_round(g, gp, r):
                n = rows_of(g)
                need(v, "pT_ps", 4 * g + r + 1)
                need(v, "pv_ps", 4 * (g - 1))
                v.tensor_copy(pT[0:n, gp, r * ROUND * n:(r + 1) * ROUND * n], bank[2 + r % 2][0:n, 0:ROUND * n]).then_inc(S["pT_dve"], 1)

            def phase3(s, par, pair):
                g = s - 1
                if live(g):
                    n, gp = rows_of(g), 1 - par
                    need(v, "scores_ps", 2 * g + 2)
                    need(v, "p_wide_ready", g - 1)
                    for half in range(2):
                        sc = bank[half][0:n, 0:HEAD_SPAN].rearrange("p (h t) -> p h t", t=TOKENS)
                        ins = v.tensor_reduce(top[0:n, gp, 8 * half:8 * half + 8], sc, AX.X, ALU.max)
                    ins.then_inc(S["max_c"], 1)
                if live(s - 2):
                    copy_round(s - 2, par, 1)
                if live(g):
                    n, gp = rows_of(g), 1 - par
                    need(v, "max_c", 2 * g + 1)
                    for half in range(2):
                        sc = bank[half][0:n, 0:HEAD_SPAN].rearrange("p (h t) -> p h t", t=TOKENS)
                        ins = v.tensor_tensor(shifted[0:n, gp, half * HEAD_SPAN:(half + 1) * HEAD_SPAN].rearrange("p (h t) -> p h t", t=TOKENS),
                                              sc, top[0:n, gp, 8 * half:8 * half + 8].unsqueeze(2).broadcast_to([n, 8, TOKENS]), ALU.subtract)
                    ins.then_inc(S["max_c"], 1)
                    need(v, "v_ps", g + 1)
                    need(v, "pv_ps", 4 * (g - 1))
                    v.tensor_tensor(v_one[0:n, gp, :, 0:HEAD_DIM], bank[4][0:n, 0:DIM].rearrange("p (h d) -> p h d", h=HEADS),
                                    b_v[0:n, :].rearrange("p (h d) -> p h d", h=HEADS), ALU.add).then_inc(S["v_ready"], 1)
                if live(s - 2):
                    copy_round(s - 2, par, 3)
                g = s - 3
                if live(g):
                    n, gp = rows_of(g), 1 - par
                    here = resid[0:n, ds(g * DIM, DIM)]
                    need(v, "proj_ps", g + 1)
                    v.tensor_tensor(att_b[0:n, gp, :], bank[7][0:n, 0:DIM], b_o[0:n, :], ALU.add).then_inc(S["att_c"], 1)
                    need(v, "att_c", 1 * (g + 1))
                    v.tensor_tensor(here, here, att_b[0:n, gp, :], ALU.add).then_inc(S["resid_done"], 1)
                    need(v, "resid_done", g + 1)
                    v.bn_stats(ln4_stats[0:n, ds(g, 1), :], here).then_inc(S["ln4_c"], 1)
                g = s - 2
                if live(g):
                    n, gp = rows_of(g), par
                    pv = bank[5][0:n, 0:HEADS * 17].rearrange("p (h d) -> p h d", h=HEADS)
                    need(v, "pv_ps", 4 * g + 4)
                    need(v, "attT_ps", g - 1)
                    v.reciprocal(inv_sum[0:n, gp, :].unsqueeze(2), pv[:, :, 16:17]).then_inc(S["route_c"], 1)
                    need(v, "route_c", 2 * g + 1)
                    v.tensor_tensor(att[0:n, gp, :].rearrange("p (h d) -> p h d", h=HEADS), pv[:, :, 0:16],
                                    inv_sum[0:n, gp, :].unsqueeze(2).broadcast_to([n, HEADS, HEAD_DIM]), ALU.mult).then_inc(S["route_c"], 1)
                if par == 1:
                    round_piece(pair, PIECES_EARLY, PIECES)

            sweep(v, body=phase3, **P3)
            v.wait_ge(S["ln4_c"], GROUPS)
            v.wait_ge(S["pT_act"], 2 * GROUPS)
            v.wait_ge(S["attT_ready"], GROUPS)
            v.wait_ge(S["proj_ps"], GROUPS)

            count = [2 * GROUPS]

            def step(ins):
                count[0] += 1
                ins.then_inc(S["route_c"], 1)
                v.wait_ge(S["route_c"], count[0])

            step(v.memset(mv4[:, :, :], 1.0))
            for g in range(GROUPS):
                n = rows_of(g)
                ins = v.bn_aggr(mv4[0:n, g, :], ln4_stats[0:n, g, :])
            ins.then_inc(S["ln4_c"], 1)
            v.wait_ge(S["ln4_c"], GROUPS + 1)
            v.tensor_scalar(sc4[:, 0, :], mv4[:, :, 1], 1e-5, None, ALU.add).then_inc(S["ln4_c"], 1)
            v.wait_ge(S["sd4_ready"], 1)
            step(v.reciprocal(sc4[:, 2, :], sc4[:, 1, :]))
            step(v.tensor_tensor(sc4[:, 3, :], sc4[:, 2, :], sc4[:, 2, :], ALU.mult))
            step(v.tensor_tensor(sc4[:, 4, :], sc4[:, 3, :], sc4[:, 0, :], ALU.mult))
            step(v.tensor_scalar(sc4[:, 5, :], sc4[:, 4, :], -0.5, 1.5, ALU.mult, ALU.add))
            step(v.tensor_tensor(sc4[:, 6, :], sc4[:, 2, :], sc4[:, 5, :], ALU.mult))
            for g in range(GROUPS):
                n = rows_of(g)
                v.tensor_scalar(x2[0:n, g, 0:DIM], resid[0:n, g * DIM:(g + 1) * DIM], mv4[0:n, g, 0:1], sc4[0:n, 6, g:g + 1],
                                ALU.subtract, ALU.mult).then_inc(S["x2_ready"], 1)
            def L(i, n=ROWS):
                return lg[0:n, i, :].rearrange("p (g e) -> p g e", e=EXPERTS)

            def per_token(x):
                return x.unsqueeze(2).broadcast_to([ROWS, GROUPS, EXPERTS])
            sm = [small[:, i, :] for i in range(12)]
            step(v.memset(lg[:, 0, :], 0.0))
            v.wait_ge(S["logits_ps"], GROUPS)
            full = (GROUPS - 1) * EXPERTS
            rest = rows_of(GROUPS - 1)
            step(v.tensor_tensor(lg[:, 0, 0:full].rearrange("p (g e) -> p g e", e=EXPERTS),
                                 bank[2][0:ROWS, 0:full].rearrange("p (g e) -> p g e", e=EXPERTS),
                                 b_router.unsqueeze(1).broadcast_to([ROWS, GROUPS - 1, EXPERTS]), ALU.add))
            step(v.tensor_tensor(lg[0:rest, 0, full:], bank[2][0:rest, full:full + EXPERTS], b_router[0:rest, :], ALU.add))
            step(v.tensor_reduce(sm[0], L(0), AX.X, ALU.max))
            v.tensor_tensor(L(1), L(0), per_token(sm[0]), ALU.subtract).then_inc(S["route_in"], 1)
            v.wait_ge(S["exp4_ready"], 1)
            step(v.tensor_reduce(sm[1], L(2), AX.X, ALU.add))
            step(v.reciprocal(sm[2], sm[1]))
            step(v.tensor_tensor(L(3), L(2), per_token(sm[2]), ALU.mult))
            rank = cst(C_RANK, ROWS).rearrange("p (g e) -> p g e", e=EXPERTS)

            def pick(src, best, sel, a, b):
                step(v.tensor_reduce(best, src, AX.X, ALU.max))
                step(v.tensor_tensor(L(a), src, per_token(best), ALU.is_equal))
                step(v.tensor_tensor(L(b), L(a), rank, ALU.mult))
                step(v.tensor_reduce(sm[3], L(b), AX.X, ALU.max))
                step(v.tensor_tensor(sel, L(b), per_token(sm[3]), ALU.is_equal))
            pick(L(3), sm[4], L(6), 4, 5)
            step(v.scalar_tensor_tensor(L(7), L(6), -2.0, L(3), ALU.mult, ALU.add))
            pick(L(7), sm[5], L(8), 4, 5)
            step(v.tensor_tensor(sm[6], sm[4], sm[5], ALU.add))
            step(v.reciprocal(sm[7], sm[6]))
            step(v.tensor_tensor(sm[10], sm[4], sm[7], ALU.mult))
            step(v.tensor_tensor(sm[11], sm[5], sm[7], ALU.mult))
            step(v.tensor_tensor(L(9), L(6), L(8), ALU.add))
            v.tensor_tensor(L(10), L(9), per_token(cst(C_VALID, ROWS)), ALU.mult).then_inc(S["route_in"], 1)
            step(v.tensor_tensor(L(4), L(6), per_token(sm[10]), ALU.mult))
            step(v.tensor_tensor(L(5), L(8), per_token(sm[11]), ALU.mult))
            step(v.tensor_tensor(x2[:, :, ROW_WEIGHT:ROW], L(4), L(5), ALU.add))
            step(v.tensor_copy(x2[:, :, ROW_TOKEN:ROW_TOKEN + 1].bitcast(i32), cst(C_TOKEN, ROWS).unsqueeze(2)))
            v.wait_ge(S["route_ps"], 1)
            NEh = NE
            step(v.tensor_copy(lg[:, 11, :], bank[3][0:ROWS, 0:NEh]))
            step(v.tensor_copy(lg[:, 12, :], bank[4][0:ROWS, 0:NEh]))
            src, dst, shift = 12, 13, 1
            while shift < GROUPS:
                w = shift * EXPERTS
                step(v.tensor_copy(lg[:, dst, 0:w], lg[:, src, 0:w]))
                step(v.tensor_tensor(lg[:, dst, w:], lg[:, src, w:], lg[:, src, 0:NE - w], ALU.add))
                src, dst, shift = dst, src, shift * 2
            step(v.tensor_tensor(lg[:, 14, EXPERTS:], lg[:, 11, EXPERTS:], lg[:, src, 0:NE - EXPERTS], ALU.add))
            step(v.tensor_copy(lg[:, 14, 0:EXPERTS], lg[:, 11, 0:EXPERTS]))
            total = lg[:, src, NE - EXPERTS:NE]
            over_v = over[:, :].rearrange("p (e t) -> p e t", e=EXPERTS)
            step(v.tensor_tensor(over_v, total.unsqueeze(2).broadcast_to([ROWS, EXPERTS, 19]),
                                 cst(C_THRESH, ROWS).rearrange("p (e t) -> p e t", e=EXPERTS), ALU.is_gt))
            step(v.tensor_reduce(cnt[:, 0, :], over_v, AX.X, ALU.add))
            a, b = 0, 1
            for shift in (1, 2, 4):
                step(v.tensor_copy(cnt[:, b, 0:shift], cnt[:, a, 0:shift]))
                step(v.tensor_tensor(cnt[:, b, shift:], cnt[:, a, shift:], cnt[:, a, 0:EXPERTS - shift], ALU.add))
                a, b = b, b + 1
            step(v.memset(cnt[:, 6, :], 0.0))
            step(v.tensor_scalar(cnt[:, 6, 1:], cnt[:, a, 0:EXPERTS - 1], float(SLOT), None, ALU.mult))
            step(v.tensor_tensor(L(15), L(14), cnt[:, 6, :].unsqueeze(1).broadcast_to([ROWS, GROUPS, EXPERTS]), ALU.add))
            for c, sel in enumerate((6, 8)):
                step(v.tensor_tensor(L(4), L(15), L(sel), ALU.mult))
                step(v.tensor_reduce(sm[8 + c], L(4), AX.X, ALU.add))
                step(v.tensor_copy(choice_row[:, c, :], sm[8 + c]))
            step(v.tensor_tensor(smap[0:1, :].rearrange("p (j e) -> p j e", e=8),
                                 cst(C_SLOTNO, 1).rearrange("p (j e) -> p j e", e=8),
                                 cnt[0:1, a, :].unsqueeze(1).broadcast_to([1, SLOTS, 8]), ALU.is_ge))
            step(v.tensor_reduce(smap_sum[0:1, :], smap[0:1, :].rearrange("p (j e) -> p j e", e=8)[:, :, 0:7], AX.X, ALU.add))
            step(v.tensor_copy(slot_expert[0:1, :], smap_sum[0:1, :]))
            step(v.tensor_copy(tiles_done[0:1, :], cnt[0:1, a, :]))
            v.engine_nop().then_inc(S["plan_ready"], 1)
            v.memset(code[:, :, :], 0.0).then_inc(S["code_c"], 1)
            for i in range(CODE):
                v.wait_ge(S["code_c"], i + 1)
                ahead = CODE - 2 - i
                lo, hi = max(0, -ahead), SLOTS - max(0, ahead)
                if i == 0:
                    v.tensor_copy(code[:, 0, lo:hi], smap_sum[:, lo + ahead:hi + ahead]).then_inc(S["code_c"], 1)
                else:
                    v.scalar_tensor_tensor(code[:, i, lo:hi], code[:, i - 1, lo:hi], float(EXPERTS), smap_sum[:, lo + ahead:hi + ahead],
                                           ALU.mult, ALU.add).then_inc(S["code_c"], 1)
            v.tensor_scalar(code[:, CODE - 1, 0:1], code[:, CODE - 2, 0:1], float(EXPERTS), None, ALU.mult).then_inc(S["code_c"], 1)
            v.wait_ge(S["code_c"], CODE + 2)
            v.tensor_copy(slot_code[:, :], code[:, CODE - 1, :]).then_inc(S["code_c"], 1)

            v.wait_ge(S["scattered"], 16 * 2 * GROUPS)
            v.wait_ge(S["hi_stored"], 16 * PIECES)
            v.wait_ge(S["lo_stored"], 16 * PIECES)
            v.wait_ge(S["resid_stored"], 16 * GROUPS)
            v.memset(hid[0:2, 0, 0:128], 1.0).then_inc(S["ones_ready"], 1)
            v.wait_ge(S["ones_ready"], 1)
            v.tensor_copy(ones2[:, :], hid[0:2, 0, 0:128]).then_inc(S["ones_ready"], 1)
            v.wait_ge(S["ones_ready"], 2)

            def split_x(j, par):
                need(v, "xs_hi", j + 1)
                need(v, "ug_ps", 2 * (j - 1) + 1)
                v.tensor_tensor(xsT[1][:, par, :, :], bank[7][:, 0:256].rearrange("p (k n) -> p k n", k=2),
                                xsT[0][:, par, :, :].bitcast(f32), ALU.subtract).then_inc(S["xs_lo"], 1)

            def gate(j, c):
                need(v, "gelu_c", 4 * j + 2 * c + 2)
                need(v, "hidT_ps", 2 * (j - 1) + c + 1)
                v.scalar_tensor_tensor(hid[:, c, :], act_g[:, c, :], 1.0, act_u[:, c, :], ALU.add, ALU.mult).then_inc(S["hid_ready"], 1)

            def split_hidden(j, par, c):
                need(v, "hid_hi", 2 * j + c + 1)
                need(v, "y_ps", j)
                v.scalar_tensor_tensor(hidT[1][:, par, 4 * c:4 * c + 4, :], bank[4 + c][:, :].rearrange("p (k n) -> p k n", k=4), 0.5,
                                       hidT[0][:, par, 4 * c:4 * c + 4, :].bitcast(f32), ALU.mult, ALU.subtract).then_inc(S["hid_lo"], 1)

            def link_of(j):
                def link(i, ins):
                    ins.then_inc(S["y_c"], 1)
                    v.wait_ge(S["y_c"], j * YC + i)
                return link
            y_mean = y_mv[:, 0:1]
            c = [y_sc[:, i:i + 1] for i in range(8)]
            seed = y_int[:, 1:2].bitcast(f32)

            def finish_first(j, buf):
                link = link_of(j)
                need(v, "y_norm_ready", j)
                need(v, "y_ps", j + 2)
                link(1, v.tensor_tensor(y_res[:, :], bank[6][:, 0:DIM], xs[:, buf, 0:DIM], ALU.add))
                link(2, v.bn_stats(y_st[:, :], y_res[:, :]))
                v.nop(nofuse=True)
                link(3, v.bn_aggr(y_mv[:, :], y_st[:, :]))
                link(4, v.tensor_scalar(c[0], y_mv[:, 1:2], 1e-12, None, ALU.add))
                link(5, v.tensor_scalar(c[1], c[0], -0.5, None, ALU.mult))
                link(6, v.tensor_scalar(y_int[:, 0:1], c[0].bitcast(i32), 1, None, ALU.logical_shift_right))
                link(7, v.tensor_scalar(y_int[:, 1:2], y_int[:, 0:1], -1.0, float(0x5f3759df), ALU.mult, ALU.add))
                link(8, v.tensor_scalar(c[2], seed, seed, c[1], ALU.mult, ALU.mult))
                link(9, v.tensor_scalar(c[3], c[2], 1.5, seed, ALU.add, ALU.mult))

            def finish_rest(j, par):
                link = link_of(j)
                link(10, v.tensor_scalar(c[4], c[3], c[3], c[1], ALU.mult, ALU.mult))
                link(11, v.tensor_scalar(c[5], c[4], 1.5, c[3], ALU.add, ALU.mult))
                link(12, v.tensor_scalar(c[6], c[5], c[5], c[1], ALU.mult, ALU.mult))
                link(13, v.tensor_scalar(c[7], c[6], 1.5, c[5], ALU.add, ALU.mult))
                need(v, "y_out_ready", j)
                v.tensor_scalar(y_norm[:, par, :], y_res[:, :], y_mean, c[7], ALU.subtract, ALU.mult).then_inc(S["y_norm_ready"], 1)

            def slot(j, buf, first, last):
                par = buf % 2
                second = isinstance(j, int) and j == 1
                if not first and not second:
                    finish_first(j - 2, (buf - 2) % X_BUFFERS)
                gate(j, 0)
                if not first:
                    split_hidden(j - 1, 1 - par, 1)
                if not last:
                    split_x(j + 1, 1 - par)
                if not first and not second:
                    finish_rest(j - 2, par)
                gate(j, 1)
                split_hidden(j, par, 0)

            def group(j, buf, count):
                for k in range(count):
                    slot(j + k, (buf + k) % X_BUFFERS, isinstance(j, int) and j + k == 0, isinstance(j, int) and j + k + 1 == SLOTS)

            split_x(0, 0)
            slot_groups(v, group, tail=8)
            finish_first(SLOTS - 2, (SLOTS - 2) % X_BUFFERS)
            split_hidden(SLOTS - 1, (SLOTS - 1) % 2, 1)
            finish_rest(SLOTS - 2, (SLOTS - 2) % 2)
            finish_first(SLOTS - 1, (SLOTS - 1) % X_BUFFERS)
            finish_rest(SLOTS - 1, (SLOTS - 1) % 2)

        @block.tensor
        def _(pe):
            mm, tr = pe.matmul, pe.transpose
            pe.wait_ge(S["const_loaded"], 16)
            pe.wait_ge(S["wproj_loaded"], 16)

            def phase1(s, par, pair):
                g = s - 1
                if live(g):
                    n, gp = rows_of(g), 1 - par
                    need(pe, "x_norm_ready", g + 1)
                    need(pe, "x_affT_ready", 2 * g)
                    for k in range(6):
                        ins = tr(bank[k // 3][:, (k % 3) * ROWS:(k % 3) * ROWS + n], x_norm[0:n, gp, k * 128:(k + 1) * 128], ident[0:n, 0:n])
                    ins.then_inc(S["xT_ps"], 1)
                g5 = s - 5
                if live(g5):
                    n = rows_of(g5)
                    need(pe, "x1_ready", g5 + 1)
                    need(pe, "x1T_ready", g5)
                    for k in range(2):
                        ins = tr(bank[4][:, k * ROWS:k * ROWS + n], x1[0:n, 1 - par, k * 128:(k + 1) * 128], ident[0:n, 0:n])
                    ins.then_inc(S["x1T_ps"], 1)
                g2 = s - 2
                if live(g2):
                    n = rows_of(g2)
                    need(pe, "x_affT_ready", 2 * g2 + 2)
                    need(pe, "ln2_c", 3 * (g2 - 2) + 1)
                    for k in range(6):
                        ins = mm(bank[2 + par][0:n, 0:DIM], x_affT[:, par, k, 0:n], wproj_sb[:, k, :], start=(k == 0), stop=(k == 5))
                    ins.then_inc(S["z_ps"], 1)

            sweep(pe, body=phase1, **P1)

            pe.wait_ge(S["weights_loaded"], 16 * 6)
            pe.wait_ge(S["x1T_ready"], GROUPS)

            def phase2(c, par, pair):
                def xk(k):
                    return x1T[:, k, ds(c * CHUNK, CHUNK)]
                need(pe, "lat_ready", 2 * c)
                for w in range(2):
                    for k in range(2):
                        ins = mm(bank[w][:, 0:CHUNK], wd_sb[:, k, w * LATENT:(w + 1) * LATENT], xk(k), start=(k == 0), stop=(k == 1))
                    ins.then_inc(S["lat_ps"], 1)
                for j in range(4):
                    half, q, tri = j % 2, j // 2, c * 4 + j
                    b = bank[2 + 3 * (j % 2):5 + 3 * (j % 2)]
                    cut = slice(half * 128, half * 128 + 128)
                    need(pe, "rope_c", tri * 4 - 4)
                    if q == 0:
                        for r in range(2):
                            for k in range(2):
                                mm(b[r][:, 0:CHUNK], wk_sb[:, 2 * r + k, cut], xk(k), start=(k == 0), stop=(k == 1))
                        need(pe, "lat_ready", 2 * c + 2)
                        ins = mm(b[2][:, 0:CHUNK], wk_sb[:, 4, cut], latT[:, ds(c * CHUNK, CHUNK)], start=True, stop=True)
                    else:
                        for r in range(3):
                            ins = mm(b[r][:, 0:CHUNK], wq_sb[:, r * DIM + half * 128:r * DIM + half * 128 + 128], ctq[:, par, :], start=True, stop=True)
                    ins.then_inc(S["rope_ps"], 1)

            sweep(pe, body=phase2, **P2)

            pe.wait_ge(S["rope_c"], 4 * 4 * CHUNKS)

            def phase3(s, par, pair):
                gd, gc, gb = s - 3, s - 2, s - 1

                def scores(half):
                    n, m, gp = rows_of(gb), images_of(gb), 1 - par
                    if half == 0:
                        need(pe, "keys_ready", 2 * gb + 2)
                    else:
                        need(pe, "keys_act_ready", gb + 1)
                    need(pe, "queries_ready", gb + 1)
                    need(pe, "max_c", 2 * gb)
                    for i in range(m):
                        ins = mm(bank[half][0:n, 0:HEAD_SPAN], q_pad[:, gp, half, i * ROWS:i * ROWS + n],
                                 k_blocks[:, gp, half, i * HEAD_SPAN:(i + 1) * HEAD_SPAN], start=(i == 0), stop=(i == m - 1))
                    ins.then_inc(S["scores_ps"], 1)

                def turn_round(r):
                    n = rows_of(gc)
                    need(pe, "p_wide_ready", gc + 1)
                    need(pe, "pT_act" if r % 2 == 0 else "pT_dve", 2 * gc + r // 2)
                    for h in range(ROUND):
                        head = r * ROUND + h
                        ins = tr(bank[2 + r % 2][0:n, h * n:(h + 1) * n], p_wide[0:n, par, head * n:(head + 1) * n], ident[0:n, 0:n])
                    ins.then_inc(S["pT_ps"], 1)

                def values_round(r):
                    n = rows_of(gc)
                    need(pe, "pT_act" if r % 2 == 0 else "pT_dve", 2 * gc + r // 2 + 1)
                    if r == 0:
                        need(pe, "v_ready", gc + 1)
                        need(pe, "route_c", 2 * gc)
                    for h in range(ROUND):
                        head = r * ROUND + h
                        ins = mm(bank[5][0:n, head * 17:(head + 1) * 17], pT[0:n, par, head * n:(head + 1) * n], v_one[0:n, par, head, :],
                                 start=True, stop=True)
                    ins.then_inc(S["pv_ps"], 1)

                if live(gb):
                    scores(0)
                    scores(1)
                if live(gc):
                    turn_round(0)
                    turn_round(1)
                if live(gd):
                    n, gp = rows_of(gd), 1 - par
                    need(pe, "route_c", 2 * gd + 2)
                    need(pe, "attT_ready", gd)
                    for k in range(2):
                        ins = tr(bank[6][:, k * ROWS:k * ROWS + n], att[0:n, gp, k * 128:(k + 1) * 128], ident[0:n, 0:n])
                    ins.then_inc(S["attT_ps"], 1)
                if live(gb):
                    n, gp = rows_of(gb), 1 - par
                    need(pe, "v_ready", gb)
                    mm(bank[4][0:n, 0:DIM], lat_g[:, gp, 0:n], wvo_sb[:, 0, :], start=True, stop=True).then_inc(S["v_ps"], 1)
                if live(gc):
                    turn_round(2)
                    turn_round(3)
                    values_round(0)
                    values_round(1)
                if live(gd):
                    n, gp = rows_of(gd), 1 - par
                    need(pe, "attT_ready", gd + 1)
                    need(pe, "att_c", gd)
                    for k in range(2):
                        ins = mm(bank[7][0:n, 0:DIM], attT[:, gp, k, 0:n], wvo_sb[:, 1 + k, :], start=(k == 0), stop=(k == 1))
                    ins.then_inc(S["proj_ps"], 1)
                if live(gc):
                    values_round(2)
                    values_round(3)

            sweep(pe, body=phase3, **P3)

            pe.wait_ge(S["att_c"], GROUPS)
            pe.wait_ge(S["resid_done"], GROUPS)
            for g in range(GROUPS + 1):
                if g < GROUPS:
                    n = rows_of(g)
                    need(pe, "x2_ready", g + 1)
                    need(pe, "x2T_ready", g - 1)
                    for k in range(2):
                        ins = tr(bank[g % 2][:, k * ROWS:k * ROWS + n], x2[0:n, g, k * 128:(k + 1) * 128], ident[0:n, 0:n])
                    ins.then_inc(S["x2T_ps"], 1)
                if g >= 1:
                    h = g - 1
                    n = rows_of(h)
                    need(pe, "x2T_ready", h + 1)
                    for k in range(2):
                        ins = mm(bank[2][0:n, h * EXPERTS:(h + 1) * EXPERTS], x2T[:, h % 2, k, 0:n], wr_sb[:, k, :], start=(k == 0), stop=(k == 1))
                    ins.then_inc(S["logits_ps"], 1)
            pe.wait_ge(S["route_in"], 2)
            mm(bank[3][0:ROWS, 0:NE], cst(C_BEFORE, ROWS), lg[:, 10, :], start=True, stop=True)
            mm(bank[4][0:ROWS, 0:NE], cst(C_ONES, ROWS), lg[:, 10, :], start=True, stop=True).then_inc(S["route_ps"], 1)

            pe.sem_inc(S["ug_ps"], 1)
            pe.sem_inc(S["y_ps"], 1)
            pe.wait_ge(S["plan_ready"], 1)
            pe.wait_ge(S["ones_ready"], 2)
            pe.wait_ge(S["code_c"], CODE + 3)

            def turn_x(j, buf):
                need(pe, f"xs_loaded{buf}", (j - buf) * (16 // X_BUFFERS) + 16)
                need(pe, "xs_lo", j)
                for k in range(2):
                    ins = tr(bank[7][:, k * 128:(k + 1) * 128], xs[:, buf, k * 128:(k + 1) * 128], ident)
                ins.then_inc(S["xsT_ps"], 1)

            def up(j, par, c, e, w0):
                if c == 0:
                    pe.wait_ge(S["up_loaded"], e * UP_LOADS + UP_LOADS)
                    need(pe, "xs_lo", j + 1)
                need(pe, "gelu_c", 4 * (j - 1) + 2 * c + 2)
                for t, w in enumerate((wi_hl, wg_hl)):
                    dst = bank[2 * c + t][:, :]
                    mm(dst, ones2[:, :], bias_sb[:, ds(w0 + t * FFN + c * 512, 512)], start=True, stop=False)
                    for k in range(2):
                        at = ds(w0 + k * FFN + c * 512, 512)
                        mm(dst, xsT[0][:, par, k, :], w[0][:, at], start=False, stop=False)
                        mm(dst, xsT[0][:, par, k, :], w[1][:, at], start=False, stop=False)
                        ins = mm(dst, xsT[1][:, par, k, :], w[0][:, at], start=False, stop=(k == 1))
                ins.then_inc(S["ug_ps"], 1)

            def turn_hidden(j, c):
                need(pe, "hid_ready", 2 * j + c + 1)
                need(pe, "hid_lo", 2 * (j - 1) + c + 1)
                for k in range(4):
                    ins = tr(bank[4 + c][:, k * 128:(k + 1) * 128], hid[:, c, k * 128:(k + 1) * 128], ident)
                ins.then_inc(S["hidT_ps"], 1)

            def down(j, par, e):
                w0 = buffer_of(e)
                pe.wait_ge(S["down_loaded"], e * DOWN_LOADS + DOWN_LOADS)
                need(pe, "y_c", (j - 1) * YC + 1)
                mm(bank[6][:, 0:DIM], ones2[:, :], bias_out[:, ds((e % 2) * DIM, DIM)], start=True, stop=False)
                need(pe, "hid_lo", 2 * j + 2)
                for k in range(8):
                    at = ds(w0 + k * DIM, DIM)
                    mm(bank[6][:, 0:DIM], hidT[0][:, par, k, :], wo_hl[0][:, at], start=False, stop=False)
                    mm(bank[6][:, 0:DIM], hidT[0][:, par, k, :], wo_hl[1][:, at], start=False, stop=False)
                    ins = mm(bank[6][:, 0:DIM], hidT[1][:, par, k, :], wo_hl[0][:, at], start=False, stop=(k == 7))
                ins.then_inc(S["y_ps"], 1)

            def expert_at(j):
                return pe.value_load(slot_expert[0:1, ds(j, 1)], min_val=0, max_val=EXPERTS - 1)

            def buffer_of(e):
                return (e % 2) * WSZ

            def slot(j, buf, first, last, e, e_before):
                par = buf % 2
                up(j, par, 0, e, buffer_of(e))
                if not first:
                    turn_hidden(j - 1, 1)
                if not last:
                    turn_x(j + 1, (buf + 1) % X_BUFFERS)
                up(j, par, 1, e, buffer_of(e))
                turn_hidden(j, 0)
                if not first:
                    down(j - 1, 1 - par, e_before)

            def group(j, buf, count):
                start, end = isinstance(j, int) and j == 0, isinstance(j, int) and j + count == SLOTS
                es = []
                for k in range(0, count, CODE - 1):
                    digits = pe.value_load(slot_code[0:1, ds(j + k, 1)], min_val=0, max_val=EXPERTS ** CODE - 1)
                    es = es[:k] + [digits // EXPERTS ** i % EXPERTS for i in range(CODE)]
                for k in range(count):
                    slot(j + k, (buf + k) % X_BUFFERS, start and k == 0, end and k == count - 1, es[k + 1], es[k])

            turn_x(0, 0)
            slot_groups(pe, group, tail=8)
            turn_hidden(SLOTS - 1, 1)
            down(SLOTS - 1, (SLOTS - 1) % 2, expert_at(SLOTS - 1))


def kernel(**inputs):
    import numpy as np
    import concourse.bacc as bacc
    from concourse.bass_utils import run_bass_kernel_spmd as run

    x = {k: np.asarray(a) for k, a in inputs.items()}
    P = 16
    side = 96 // P
    patches = x["x"].reshape(IMAGES, 3, side, P, side, P).transpose(0, 2, 4, 3, 5, 1).reshape(IMAGES * PATCHES, PATCH_DIM)

    cols, width = constant_columns()
    consts = np.zeros((128, width), np.float32)
    p = np.arange(128)[:, None]

    def put(which, a):
        lo, hi = cols[which]
        consts[:, lo:hi] = np.broadcast_to(a, (128, hi - lo))
    put(C_IDENT, np.eye(128))
    put(C_BEFORE, p < np.arange(ROWS)[None])
    put(C_ONES, 1.0)
    put(C_HEAD, p // HEAD_DIM == np.arange(8)[None])
    put(C_IMAGE, p // TOKENS == np.arange(3)[None])
    put(C_PATCH, np.concatenate([p % TOKENS != 0, p % TOKENS == 0], 1))
    put(C_RANK, np.tile(EXPERTS - np.arange(EXPERTS), GROUPS)[None])
    put(C_VALID, p + ROWS * np.arange(GROUPS)[None] < ALL_TOKENS)
    put(C_THRESH, np.tile(SLOT * np.arange(19), EXPERTS)[None])
    put(C_SLOTNO, np.repeat(np.arange(SLOTS), 8)[None])
    put(C_NOT_IMAGE, np.where(p // TOKENS == np.arange(3)[None], 0.0, -1e30))
    put(C_TOKEN, p + ROWS * np.arange(GROUPS)[None])
    put(C_PAD, p + ALL_TOKENS)
    half = DIM // 2
    theta = (np.float32(10000.0) ** (np.float32(-2.0) * np.arange(half, dtype=np.float32))).astype(np.float32) / np.float32(half)
    angle = (np.arange(TOKENS, dtype=np.float32)[:, None] * theta[None, :].astype(np.float32)).astype(np.float32)
    sign = np.tile(np.array([-1.0, 1.0], np.float32), half)[:, None]
    rope = np.stack([np.repeat(np.cos(angle).T, 2, axis=0), np.repeat(np.sin(angle).T, 2, axis=0) * sign]).astype(np.float32)

    def partner(a):
        return a.reshape(*a.shape[:-1], half, 2)[..., ::-1].reshape(a.shape)

    def by_partition(w):
        return w.reshape(EXPERTS, -1, 128, w.shape[-1]).transpose(0, 2, 1, 3).reshape(EXPERTS, 128, PIECE)

    def columns(a):
        return a.reshape(-1, 128).T
    a = {k[len("L0_attn_"):]: t for k, t in x.items() if k.startswith("L0_attn_")}
    arrays = {
        "patches": patches,
        "consts": consts,
        "w_proj": x["L0_tok_W_proj"],
        "rows_pack": np.concatenate([x["L0_tok_ln2_g"], x["L0_tok_ln2_b"], x["L0_tok_cls_token"].reshape(-1), x["L0_tok_b_proj"],
                                     a["Wu_v_b"], a["Wo_b"], x["L0_ffn_br"]]),
        "pos": x["L0_tok_pos_emb"][0],
        "wd": np.concatenate([a["Wd_q_w"], a["Wd_kv_w"]], 1),
        "wq": np.concatenate([a["Wq_r_w"], partner(a["Wq_r_w"]), a["Wu_q_w"]], 1),
        "wk": np.concatenate([a["Wk_r_w"], partner(a["Wk_r_w"]), a["Wu_k_w"]], 0),
        "wv_o": np.concatenate([a["Wu_v_w"], a["Wo_w"]], 0),
        "cols_pack": np.concatenate([columns(a["Wd_q_b"]), columns(a["Wd_kv_b"]),
                                     columns(a["Wk_r_b"]), columns(partner(a["Wk_r_b"])), columns(a["Wu_k_b"]),
                                     columns(a["Wq_r_b"]), columns(partner(a["Wq_r_b"])), columns(a["Wu_q_b"]),
                                     columns(x["L0_tok_ln1_g"]), columns(x["L0_tok_ln1_b"])], 1),
        "rope": rope,
        "w_router": x["L0_ffn_Wr"],
        "expert_weights": np.stack([by_partition(x["L0_ffn_Wi"]), by_partition(x["L0_ffn_Wg"]), by_partition(x["L0_ffn_Wo"])],
                                   1).reshape(PIECES * 128, PIECE),
        "expert_bias": np.concatenate([x[k].reshape(-1) for k in ("L0_ffn_bi", "L0_ffn_bg", "L0_ffn_bo")]).reshape(128, BIAS_COLS),
        "expert_rows": np.concatenate([x["L0_ffn_gamma"], x["L0_ffn_beta"]], 1),
    }
    arrays = {k: np.ascontiguousarray(t) for k, t in arrays.items()}
    f32 = mybir.dt.float32
    nc = bacc.Bacc("TRN2", target_bir_lowering=False, num_devices=1)
    args = {k: nc.dram_tensor(k, t.shape, f32, kind="ExternalInput").ap() for k, t in arrays.items()}
    args["out"] = nc.dram_tensor("out", (ALL_TOKENS + 128, DIM), f32, kind="ExternalOutput").ap()
    args["slots_in"] = nc.dram_tensor("slots_in", (SLOTS * SLOT, ROW), f32, kind="Internal").ap()
    for part in ("weight_hi", "weight_lo"):
        args[part] = nc.dram_tensor(part, (PIECES * 128, PIECE), f32, kind="Internal").ap()
    args["bias_parts"] = nc.dram_tensor("bias_parts", (2, 128 * BIAS_COLS), f32, kind="Internal").ap()
    build(nc, **args)
    r = run(nc, [arrays], core_ids=[0])
    return r.results[0]["out"][:ALL_TOKENS].reshape(IMAGES, TOKENS, DIM)
```

```python
import concourse.bass as bass
from concourse import mybir
from contextlib import ExitStack

IMAGES, PATCHES, TOKENS, DIM = 64, 36, 37, 256
PATCH_DIM = 768
ALL_TOKENS = IMAGES * TOKENS
PER_GROUP = 3
GROUPS = -(-IMAGES // PER_GROUP)
ROWS = PER_GROUP * TOKENS
HEADS, HEAD_DIM = 16, 16
LATENT = 128
EXPERTS, TOP, FFN = 8, 2, 1024
SLOT = 128
X_BUFFERS = 8
CODE = 5
SLOTS = (ALL_TOKENS * TOP + EXPERTS * (SLOT - 1) + EXPERTS - TOP) // SLOT
CHUNKS = 8
CHUNK = ALL_TOKENS // CHUNKS
CHUNK_IMAGES = CHUNK // TOKENS
SCORE_SCALE = float(1.0 / (HEADS + 2 * LATENT) ** 0.5)
HEAD_SPAN = TOKENS * (HEADS // 2)
ROUND = 4
PIECE = 2 * FFN
PIECES = 3 * EXPERTS
PIECES_EARLY = 12
UP_BUFFERS = 3
U_BIAS_UP, U_BIAS_GATE, UP_COLS = 4 * PIECE, 4 * PIECE + FFN, 4 * PIECE + 2 * FFN
DOWN_BUFFERS = 2
D_BIAS, D_GAMMA, D_BETA, DOWN_COLS = (2 * PIECE + i * DIM for i in range(4))
BIAS_COLS = EXPERTS * (FFN + DIM) // 128
C_IDENT, C_BEFORE, C_ONES, C_HEAD, C_IMAGE, C_PATCH, C_RANK, C_VALID, C_THRESH, C_SLOTNO, C_NOT_IMAGE, C_TOKEN, C_PAD, C_ROW = range(14)


def constant_columns():
    widths = [128, ROWS, ROWS, 8, 3, 2, GROUPS * 8, GROUPS, 8 * 19, SLOTS * 8, 3, GROUPS, 1, 128]
    start, out = 0, []
    for w in widths:
        out.append((start, start + w))
        start += w
    return out, start


def images_of(g):
    return IMAGES - PER_GROUP * (GROUPS - 1) if isinstance(g, int) and g == GROUPS - 1 else PER_GROUP


def build(nc, patches, consts, w_proj, rows_pack, pos, wd, wq, wk, wv_o, cols_pack, rope, w_router,
          expert_weights, expert_bias, expert_rows, out, x2_rows, bias_parts, weight_hi, weight_lo):
    f32, f32r, i32 = mybir.dt.float32, mybir.dt.float32r, mybir.dt.int32
    ALU, ACT, AX = mybir.AluOpType, mybir.ActivationFunctionType, mybir.AxisListType
    ds = bass.ds
    cols, const_width = constant_columns()

    whole = ExitStack()
    with whole:
        def sb(name, shape, dt=f32, ctx=whole):
            return ctx.enter_context(nc.sbuf_tensor(name, shape, dt))

        def pb(name, shape, ctx, dt=f32):
            return ctx.enter_context(nc.psum_tensor(name, shape, dt))

        def sem(name):
            return whole.enter_context(nc.semaphore(name))

        const = sb("const", [128, const_width])

        def cst(which, p=128):
            a, b = cols[which]
            return const[0:p, a:b]

        ident = cst(C_IDENT)
        slot_token = sb("slot_token", [128, SLOTS], i32)
        slot_weight = sb("slot_weight", [128, SLOTS])
        slot_expert = sb("slot_expert", [1, SLOTS], i32)
        tiles_done = sb("tiles_done", [1, EXPERTS], i32)
        slot_code = sb("slot_code", [1, SLOTS], i32)

        early = ExitStack()
        def eb(name, shape, dt=f32):
            return sb(name, shape, dt, early)
        resid = eb("resid", [ROWS, GROUPS * DIM])
        x1T = eb("x1T", [128, 2, ALL_TOKENS])
        qT = eb("qT", [128, 2, ALL_TOKENS])
        kT = eb("kT", [128, 2, ALL_TOKENS])
        latT = eb("latT", [128, ALL_TOKENS])
        wd_sb = eb("wd_sb", [128, 2, 2 * LATENT])
        wq_sb = eb("wq_sb", [128, 3 * DIM])
        wk_sb = eb("wk_sb", [128, 5, DIM])
        wvo_sb = eb("wvo_sb", [128, 3, DIM])
        wr_sb = eb("wr_sb", [128, 2, EXPERTS])
        colb = eb("colb", [128, 26])
        rope_sb = eb("rope_sb", [128, 2, 2, TOKENS])
        rowb = eb("rowb", [ROWS, 6 * DIM + EXPERTS])
        ln2_g, ln2_b, cls_row, b_proj, b_v, b_o = (rowb[:, i * DIM:(i + 1) * DIM] for i in range(6))
        b_router = rowb[:, 6 * DIM:6 * DIM + EXPERTS]
        pos_sb = eb("pos_sb", [ROWS, DIM])
        ln4_stats = eb("ln4_stats", [ROWS, GROUPS, 6])
        raw_piece = eb("raw_piece", [128, PIECE])
        no_rows = eb("no_rows", [128, DIM])
        splitting = ExitStack()
        hi_piece = sb("hi_piece", [128, PIECE], f32r, splitting)
        lo_piece = sb("lo_piece", [128, PIECE], f32r, splitting)

        one = ExitStack()
        def ob(name, shape, dt=f32):
            return sb(name, shape, dt, one)
        wproj_sb = ob("wproj_sb", [128, 6, DIM])
        bias_raw = ob("bias_raw", [128, BIAS_COLS])
        bias_hl = ob("bias_hl", [128, 2, BIAS_COLS], f32r)
        x_in = ob("x_in", [ROWS, 2, PATCH_DIM])
        x_norm = ob("x_norm", [ROWS, 2, PATCH_DIM])
        x_affT = ob("x_affT", [128, 2, 6, ROWS])
        z_sb = ob("z_sb", [ROWS, 2, DIM])
        z_norm = ob("z_norm", [ROWS, 2, DIM])
        x1 = ob("x1", [ROWS, 2, DIM])
        add_rows = ob("add_rows", [ROWS, DIM])
        mul_rows = ob("mul_rows", [ROWS, DIM])
        tmp_rows = ob("tmp_rows", [ROWS, DIM])
        ln1_st = ob("ln1_st", [ROWS, 2, 2, 6])
        ln2_st = ob("ln2_st", [ROWS, 2, 6])
        ln3_st = ob("ln3_st", [ROWS, 2, 6])
        ln_mv = ob("ln_mv", [ROWS, 2, 3, 2])
        ln_ve = ob("ln_ve", [ROWS, 2, 3])
        ln_sd = ob("ln_sd", [ROWS, 2, 3])
        ln_r0 = ob("ln_r0", [ROWS, 2, 3])
        ln_t = ob("ln_t", [ROWS, 2, 3, 3])
        ln_rs = ob("ln_rs", [ROWS, 2, 3])
        one.close()
        two = ExitStack()
        ctq = sb("ctq", [128, 2, CHUNK], f32, two)
        rot = sb("rot", [128, 2, 3, CHUNK], f32, two)
        two.close()
        three = ExitStack()
        def tb(name, shape, dt=f32):
            return sb(name, shape, dt, three)
        k_blocks = tb("k_blocks", [128, 2, 2, PER_GROUP * HEAD_SPAN])
        q_pad = tb("q_pad", [128, 2, 2, PER_GROUP * (ROWS + TOKENS)])
        lat_g = tb("lat_g", [128, 2, ROWS])
        shifted = tb("shifted", [ROWS, 2, HEADS * TOKENS])
        p_wide = tb("p_wide", [ROWS, 2, HEADS * ROWS])
        pT = tb("pT", [ROWS, 2, HEADS * ROWS])
        v_one = tb("v_one", [ROWS, 2, HEADS, HEAD_DIM + 1])
        top = tb("top", [ROWS, 2, HEADS])
        inv_sum = tb("inv_sum", [ROWS, 2, HEADS])
        att = tb("att", [ROWS, 2, DIM])
        attT = tb("attT", [128, 2, 2, ROWS])
        att_b = tb("att_b", [ROWS, 2, DIM])
        three.close()
        splitting.close()
        four = ExitStack()
        def fb(name, shape, dt=f32):
            return sb(name, shape, dt, four)
        CHOICES = TOP * GROUPS
        PER_TURN, AT_BUFFERS = 4, 3
        TURNS = CHOICES // PER_TURN
        fb("kept_free", [128, 384])
        at_row = fb("at_row", [ROWS, AT_BUFFERS, PER_TURN, 128], f32r)
        in_slot = fb("in_slot", [ROWS, CHOICES, SLOTS])
        slot_values = fb("slot_values", [ROWS, CHOICES, 3, SLOTS], f32r)
        x2T = fb("x2T", [128, 2, 4 * ROWS])
        x2 = fb("x2", [ROWS, GROUPS, DIM])
        mv4 = fb("mv4", [ROWS, GROUPS, 2])
        sc4 = fb("sc4", [ROWS, 8, GROUPS])
        NE = GROUPS * EXPERTS
        lg = fb("lg", [ROWS, 13, NE])
        RUN_PAD = 16 * EXPERTS
        running = fb("running", [ROWS, 2, RUN_PAD + NE])
        small = fb("small", [ROWS, 9, TOP, GROUPS])
        row_int = fb("row_int", [ROWS, 2, TOP, GROUPS], i32)
        cnt = fb("cnt", [ROWS, 5, 4 + EXPERTS])
        over = fb("over", [ROWS, EXPERTS * 19])
        smap = fb("smap", [1, SLOTS * 8])
        smap_sum = fb("smap_sum", [1, SLOTS])
        code = fb("code", [1, CODE, SLOTS])
        weight_hl = fb("weight_hl", [ROWS, 2, CHOICES], f32r)
        table_parts = fb("table_parts", [128, 3, SLOTS])
        four.close()
        early.close()
        late = ExitStack()
        def lb(name, shape, dt=f32):
            return sb(name, shape, dt, late)
        down_sb = lb("down_sb", [128, DOWN_BUFFERS * DOWN_COLS], f32r)
        up_sb = lb("up_sb", [128, UP_BUFFERS * UP_COLS], f32r)
        ones2 = lb("ones2", [2, 128], f32r)
        xs = lb("xs", [128, X_BUFFERS, DIM])
        xsT = [lb(f"xsT_{p}", [128, 2, 2, 128], f32r) for p in ("hi", "lo")]
        gate_sb = lb("gate_sb", [128, 2, 512])
        hid = lb("hid", [128, 2, 512])
        hidT = [lb(f"hidT_{p}", [128, 2, 8, 128], f32r) for p in ("hi", "lo")]
        y_norm = lb("y_norm", [128, 2, DIM])
        y_out = lb("y_out", [128, 2, DIM])
        x_token = lb("x_token", [128, X_BUFFERS, 1], i32)
        y_st = lb("y_st", [128, 6])
        y_mv = lb("y_mv", [128, 2])
        y_sc = lb("y_sc", [128, 12])
        y_int = lb("y_int", [128, 2], i32)
        late.close()
        bank = [pb(f"bank{i}", [128, 512], whole) for i in range(8)]

        S = {n: sem(n) for n in (
            "const_loaded wproj_loaded rows_loaded weights_loaded piece_loaded piece_hi piece_lo hi_stored lo_stored zeroed x_loaded0 x_loaded1 setup_done setup_c "
            "ln1_c ln2_c ln3_c ln_c std_ready x_norm_ready xT_ps x_affT_ready z_ps z_norm_ready resid_c "
            "x1_ready x1T_ps x1T_ready "
            "lat_ps lat_ready rope_ps rope_c "
            "attn_zero keys_ready keys_act_ready queries_ready scores_ps v_ps v_ready max_c p_wide_ready "
            "pT_ps pT_act pT_dve pv_ps heads_c att_c attT_ps attT_ready proj_ps resid_done "
            "ln4_c x2_ready x2T_ps x2T_ready logits_ps sd4_ready route_c totals_ps earlier_ps route_in exp4_ready "
            "bias_loaded bias_c bias_stored pad_stored resid_stored "
            "x2_stored rank_c in_slot_c weights_in tokens_in at_row_c slots_ps slot_table_c plan_ready code_c token_c "
            "up_loaded down_loaded rows5_loaded ones_ready added "
            "" + " ".join(f"xs_loaded{i}" for i in range(X_BUFFERS)) + " xsT_ps xs_hi xs_lo ug_ps gate_in_ready gelu_c hid_ready hidT_ps hid_hi hid_lo y_ps y_c y_norm_ready y_scaled_c y_out_ready ").split()}

        block = whole.enter_context(nc.Block())

        def need(eng, name, n):
            if isinstance(n, int) and n <= 0:
                return
            eng.wait_ge(S[name], n)

        def need_first(eng, name, n):
            if isinstance(n, int) and n <= 0:
                return
            eng.wait_ge(S[name], n)
            eng.nop(nofuse=True)

        def sweep(eng, head, tail, total, body):
            for s in range(min(head, total)):
                body(s, s % 2, s // 2)
            if tail > head:
                with eng.Fori(head // 2, tail // 2) as half:
                    body(half * 2, 0, half)
                    body(half * 2 + 1, 1, half)
            for s in range(tail, total):
                body(s, s % 2, s // 2)

        def slot_groups(eng, group, tail):
            group(0, 0, 4)
            with eng.Fori(0, (SLOTS - 4 - tail) // X_BUFFERS) as turn:
                group(turn * X_BUFFERS + 4, 4, X_BUFFERS)
            if tail:
                group(SLOTS - tail, 4, tail)

        def experts_from(eng, j, count):
            es = []
            for k in range(0, count, CODE - 1):
                digits = eng.value_load(slot_code[0:1, ds(j + k, 1)], min_val=0, max_val=EXPERTS ** CODE - 1)
                es = es[:k] + [digits // EXPERTS ** i % EXPERTS for i in range(CODE)]
            return es

        def live(g):
            return not isinstance(g, int) or 0 <= g < GROUPS

        def rows_of(g):
            return images_of(g) * TOKENS

        P1 = dict(head=6, tail=20, total=GROUPS + 5)
        P3 = dict(head=4, tail=20, total=GROUPS + 3)
        P2 = dict(head=2, tail=8, total=CHUNKS)
        UP_LOADS, DOWN_LOADS = 16 * 6, 16 * 3
        YC = 13

        def x_loaded_after(g, pair):
            return pair * (16 * PER_GROUP) + 16 * images_of(g)

        @block.sync
        def _(sp):
            def load_x(g, par):
                need(sp, "x_norm_ready", g - 1)
                for i in range(images_of(g)):
                    sp.dma_start(x_in[TOKENS * i + 1:TOKENS * (i + 1), par, :],
                                 patches[ds((g * PER_GROUP + i) * PATCHES, PATCHES), :]).then_inc(S[f"x_loaded{par}"], 16)

            sp.wait_ge(S["setup_done"], 1)
            load_x(0, 0)
            sp.dma_start(const[:, :], consts).then_inc(S["const_loaded"], 16)
            load_x(1, 1)
            sp.dma_start(rowb[:, :], rows_pack.partition_broadcast(ROWS)).then_inc(S["rows_loaded"], 16)
            for i in range(PER_GROUP):
                sp.dma_start(pos_sb[TOKENS * i:TOKENS * (i + 1), :], pos).then_inc(S["rows_loaded"], 16)
            sp.dma_start(colb[:, :], cols_pack).then_inc(S["rows_loaded"], 16)
            sp.dma_start(wproj_sb[:, :, :], w_proj.rearrange("(k p) n -> p k n", p=128)).then_inc(S["wproj_loaded"], 16)
            sp.dma_start(wd_sb[:, :, :], wd.rearrange("(k p) n -> p k n", p=128)).then_inc(S["weights_loaded"], 16)
            sp.dma_start(wq_sb[:, :], wq).then_inc(S["weights_loaded"], 16)
            sp.dma_start(wk_sb[:, :, :], wk.rearrange("(k p) n -> p k n", p=128)).then_inc(S["weights_loaded"], 16)
            sp.dma_start(wvo_sb[:, :, :], wv_o.rearrange("(k p) n -> p k n", p=128)).then_inc(S["weights_loaded"], 16)
            sp.dma_start(wr_sb[:, :, :], w_router.rearrange("(k p) n -> p k n", p=128)).then_inc(S["weights_loaded"], 16)
            sp.dma_start(rope_sb[:, :, :, :], rope.rearrange("t (k p) n -> p t k n", p=128)).then_inc(S["weights_loaded"], 16)

            sp.dma_start(bias_raw[:, :], expert_bias).then_inc(S["bias_loaded"], 16)

            def out_high(q):
                need(sp, "piece_hi", q + 1)
                sp.dma_start(weight_hi[ds(q * 128, 128), :], hi_piece[:, :].bitcast(f32)).then_inc(S["hi_stored"], 16)

            def out_low(q):
                need(sp, "piece_lo", q + 1)
                sp.dma_start(weight_lo[ds(q * 128, 128), :], lo_piece[:, :].bitcast(f32)).then_inc(S["lo_stored"], 16)

            def piece_in(q):
                need(sp, "piece_lo", q)
                sp.dma_start(raw_piece[:, :], expert_weights[ds(q * 128, 128), :]).then_inc(S["piece_loaded"], 16)

            def within(pair, lo, hi):
                return not isinstance(pair, int) or lo <= pair < hi

            def phase1(s, par, pair):
                if not (isinstance(s, int) and (s < 2 or s >= GROUPS)):
                    load_x(s, par)
                if isinstance(s, int) and s == 4:
                    sp.wait_ge(S["bias_c"], 2)
                    sp.dma_start(bias_parts.rearrange("t (p n) -> p t n", n=BIAS_COLS), bias_hl[:, :, :].bitcast(f32)).then_inc(S["bias_stored"], 16)
                if par == 1:
                    if within(pair, 1, PIECES_EARLY + 1):
                        out_high(pair - 1)
                    if within(pair, 0, PIECES_EARLY):
                        piece_in(pair)
                    if within(pair, 1, PIECES_EARLY + 1):
                        out_low(pair - 1)
            sweep(sp, body=phase1, **P1)
            sp.wait_ge(S["zeroed"], 1)
            sp.dma_start(out[ALL_TOKENS:ALL_TOKENS + 128, :], no_rows[:, :]).then_inc(S["pad_stored"], 16)
            sp.dma_start(x2_rows[ALL_TOKENS:ALL_TOKENS + 128, :], no_rows[:, :]).then_inc(S["pad_stored"], 16)
            sp.wait_ge(S["bias_stored"], 16)

            def phase3(s, par, pair):
                if par == 0:
                    q, late = PIECES_EARLY + pair, PIECES - PIECES_EARLY
                    if within(pair, 1, late + 1):
                        out_high(q - 1)
                    if within(pair, 0, late):
                        piece_in(q)
                    if within(pair, 1, late + 1):
                        out_low(q - 1)
                g = s - 3
                if live(g):
                    n = rows_of(g)
                    need(sp, "resid_done", g + 1)
                    sp.dma_start(out[ds(g * ROWS, n), :], resid[0:n, ds(g * DIM, DIM)]).then_inc(S["resid_stored"], 16)
            sweep(sp, body=phase3, **P3)
            sp.wait_ge(S["hi_stored"], 16 * PIECES)
            sp.wait_ge(S["lo_stored"], 16 * PIECES)
            sp.wait_ge(S["resid_stored"], 16 * GROUPS)
            sp.wait_ge(S["x2_ready"], GROUPS)
            full, rest = ROWS * (GROUPS - 1), rows_of(GROUPS - 1)
            sp.dma_start(x2_rows[0:full, :].rearrange("(g p) d -> p g d", p=ROWS), x2[:, 0:GROUPS - 1, :]).then_inc(S["x2_stored"], 16)
            sp.dma_start(x2_rows[full:full + rest, :], x2[0:rest, GROUPS - 1, :]).then_inc(S["x2_stored"], 16)
            sp.wait_ge(S["pad_stored"], 32)

            bias_up = bias_parts[:, 0:EXPERTS * FFN].rearrange("t (e n) -> t e n", e=EXPERTS)
            bias_down = bias_parts[:, EXPERTS * FFN:].rearrange("t (e n) -> t e n", e=EXPERTS)
            def slots_done(e):
                return sp.value_load(tiles_done[0:1, e:e + 1], min_val=0, max_val=SLOTS)

            def load_up(e):
                need(sp, "up_loaded", UP_LOADS * e)
                again = e >= UP_BUFFERS
                if again:
                    done = slots_done(e - UP_BUFFERS)
                    sp.wait_ge(S["ug_ps"], done * 2 + 1)
                base = (e % UP_BUFFERS) * UP_COLS

                def to(at, width, partitions=128):
                    return up_sb[0:partitions, base + at:base + at + width].bitcast(f32)
                for i, (which, src) in enumerate(((0, weight_hi), (0, weight_lo), (1, weight_hi), (1, weight_lo))):
                    q = 3 * e + which
                    sp.dma_start(to(i * PIECE, PIECE), src[q * 128:(q + 1) * 128, :]).then_inc(S["up_loaded"], 16)
                sp.dma_start(to(U_BIAS_UP, FFN, 2), bias_up[:, e, :]).then_inc(S["up_loaded"], 16)
                if again:
                    sp.wait_ge(S["gate_in_ready"], done * 2 + 1)
                sp.dma_start(to(U_BIAS_GATE, FFN), expert_rows[e, 2 * DIM:].partition_broadcast(128)).then_inc(S["up_loaded"], 16)

            def load_down(e):
                need(sp, "down_loaded", DOWN_LOADS * e)
                need(sp, "rows5_loaded", 16 * e)
                again = e >= DOWN_BUFFERS
                if again:
                    done = slots_done(e - DOWN_BUFFERS)
                    sp.wait_ge(S["y_ps"], done + 1)
                base = (e % DOWN_BUFFERS) * DOWN_COLS
                q = 3 * e + 2

                def to(at, width, partitions=128):
                    return down_sb[0:partitions, base + at:base + at + width].bitcast(f32)
                for i, src in enumerate((weight_hi, weight_lo)):
                    sp.dma_start(to(i * PIECE, PIECE), src[q * 128:(q + 1) * 128, :]).then_inc(S["down_loaded"], 16)
                sp.dma_start(to(D_BIAS, DIM, 2), bias_down[:, e, :]).then_inc(S["down_loaded"], 16)
                if again:
                    sp.wait_ge(S["y_out_ready"], done + 1)
                sp.dma_start(to(D_GAMMA, 2 * DIM), expert_rows[e, 0:2 * DIM].partition_broadcast(128)).then_inc(S["rows5_loaded"], 16)

            load_up(0)
            load_down(0)
            sp.wait_ge(S["route_in"], 1)
            load_up(1)
            load_down(1)
            sp.wait_ge(S["plan_ready"], 1)
            sp.wait_ge(S["code_c"], CODE + 3)
            sp.wait_ge(S["x2_stored"], 32)
            load_up(2)
            for e in range(DOWN_BUFFERS, EXPERTS):
                if e + 1 < EXPERTS:
                    load_up(e + 1)
                load_down(e)

        @block.gpsimd
        def _(pool):
            pool.memset(no_rows[:, :], 0.0).then_inc(S["zeroed"], 1)
            pool.wait_ge(S["bias_loaded"], 16)
            pool.tensor_copy(bias_hl[:, 0, :], bias_raw[:, :]).then_inc(S["bias_c"], 1)
            pool.wait_ge(S["bias_c"], 1)
            pool.tensor_tensor(bias_hl[:, 1, :], bias_raw[:, :], bias_hl[:, 0, :].bitcast(f32), ALU.subtract).then_inc(S["bias_c"], 1)

            def split_piece(pair, base, limit):
                if isinstance(pair, int) and base + pair >= limit:
                    return
                q = base + pair
                need_first(pool, "lo_stored", q * 16)
                need_first(pool, "piece_hi", q + 1)
                pool.tensor_tensor(lo_piece[:, :], raw_piece[:, :], hi_piece[:, :].bitcast(f32), ALU.subtract).then_inc(S["piece_lo"], 1)

            def phase1(s, par, pair):
                g = s - 3
                if live(g):
                    n = rows_of(g)
                    here = resid[0:n, ds(g * DIM, DIM)]
                    need_first(pool, "z_norm_ready", g + 1)
                    pool.tensor_tensor(here, z_norm[0:n, 1 - par, :], mul_rows[0:n, :], ALU.mult).then_inc(S["resid_c"], 1)
                    need_first(pool, "resid_c", 2 * g + 1)
                    pool.tensor_tensor(here, here, add_rows[0:n, :], ALU.add).then_inc(S["resid_c"], 1)
                if par == 1:
                    split_piece(pair, 0, PIECES_EARLY)

            pool.wait_ge(S["rows_loaded"], 16 * (2 + PER_GROUP))
            pool.wait_ge(S["setup_c"], 4)
            sweep(pool, body=phase1, **P1)

            pool.wait_ge(S["rope_c"], 4 * 4 * CHUNKS)
            pool.wait_ge(S["lat_ready"], 2 * CHUNKS)

            def phase3(s, par, pair):
                if live(s):
                    m = images_of(s)
                    need_first(pool, "scores_ps", 2 * (s - 1))
                    k_src = kT[:, 0, ds(s * ROWS, m * TOKENS)].rearrange("p (i t) -> p i t", t=TOKENS)
                    pool.tensor_tensor(
                        k_blocks[:, par, 0, 0:m * HEAD_SPAN].rearrange("p (i h t) -> p i h t", i=m, h=8),
                        k_src.unsqueeze(2).broadcast_to([128, m, 8, TOKENS]),
                        cst(C_HEAD).unsqueeze(1).unsqueeze(3).broadcast_to([128, m, 8, TOKENS]), ALU.mult).then_inc(S["keys_ready"], 1)
                    need_first(pool, "v_ps", s - 1)
                    pool.tensor_copy(lat_g[:, par, 0:m * TOKENS], latT[:, ds(s * ROWS, m * TOKENS)]).then_inc(S["keys_ready"], 1)
                if par == 1:
                    split_piece(pair, PIECES_EARLY, PIECES)

            sweep(pool, body=phase3, **P3)

            pool.wait_ge(S["in_slot_c"], 1)
            pool.tensor_tensor(slot_values[:, :, 2, :], in_slot[:, :, :],
                               weight_hl[:, 1, :].bitcast(f32).unsqueeze(2).broadcast_to([ROWS, CHOICES, SLOTS]), ALU.mult).then_inc(S["weights_in"], 1)
            pool.wait_ge(S["plan_ready"], 1)
            pool.wait_ge(S["x2_stored"], 32)
            pool.wait_ge(S["pad_stored"], 32)

            pool.wait_ge(S["resid_stored"], 16 * GROUPS)
            pool.sem_inc(S["y_out_ready"], 1)

            def gather(j, buf):
                pool.tensor_copy(x_token[:, buf, :], slot_token[:, ds(j, 1)]).then_inc(S["token_c"], 1)
                need_first(pool, "token_c", j + 1)
                pool.indirect_dma_start(out=xs[:, buf, :], out_offset=None, in_=x2_rows,
                                        in_offset=bass.IndirectOffsetOnAxis(ap=x_token[:, buf, :], axis=0)).then_inc(S[f"xs_loaded{buf}"], 16)

            def add_slot(j, buf):
                par = buf % 2
                e = pool.value_load(slot_expert[0:1, ds(j, 1)], min_val=0, max_val=EXPERTS - 1)
                base = e % DOWN_BUFFERS * DOWN_COLS
                y = y_norm[:, par, :]
                if not (isinstance(j, int) and j + 4 >= SLOTS):
                    need_first(pool, "added", 16 * (j - 3))
                    gather(j + 4, (buf + 4) % X_BUFFERS)
                need_first(pool, "rows5_loaded", e * 16 + 16)
                need_first(pool, "y_norm_ready", j + 1)
                pool.tensor_tensor(y, y, down_sb[:, ds(base + D_GAMMA, DIM)].bitcast(f32), ALU.mult).then_inc(S["y_scaled_c"], 1)
                need_first(pool, "y_scaled_c", 2 * j + 1)
                pool.tensor_tensor(y, y, down_sb[:, ds(base + D_BETA, DIM)].bitcast(f32), ALU.add).then_inc(S["y_scaled_c"], 1)
                need_first(pool, "y_scaled_c", 2 * j + 2)
                need_first(pool, "added", 16 * j)
                pool.tensor_tensor(y_out[:, par, :], y, slot_weight[:, ds(j, 1)].broadcast_to([128, DIM]),
                                   ALU.mult).then_inc(S["y_out_ready"], 1)
                need_first(pool, "y_out_ready", j + 2)
                pool.indirect_dma_start(out=out, out_offset=bass.IndirectOffsetOnAxis(ap=x_token[:, buf, :], axis=0),
                                        in_=y_out[:, par, :], in_offset=None, compute_op=ALU.add).then_inc(S["added"], 16)

            def group(j, buf, count):
                for k in range(count):
                    add_slot(j + k, (buf + k) % X_BUFFERS)
            for j in range(4):
                gather(j, j)
            slot_groups(pool, group, tail=8)
            pool.wait_ge(S["added"], 16 * SLOTS)

        @block.scalar
        def _(act):
            A = act.activation

            def phase1(s, par, pair):
                if isinstance(s, int) and s == 1:
                    act.wait_ge(S["rows_loaded"], 16 * (2 + PER_GROUP))
                g = s - 1
                if live(g):
                    n, gp = rows_of(g), 1 - par
                    need(act, "xT_ps", g + 1)
                    need(act, "z_ps", g - 1)
                    for k in range(6):
                        ins = A(x_affT[:, gp, k, 0:n], bank[k // 3][:, (k % 3) * ROWS:(k % 3) * ROWS + n], ACT.Identity,
                                scale=colb[:, 14 + k:15 + k], bias=colb[:, 20 + k:21 + k])
                        if k % 3 == 2:
                            ins.then_inc(S["x_affT_ready"], 1)
                need(act, "ln_c", 6 * s + 1)
                A(ln_sd[:, par, :], ln_ve[:, par, :], ACT.Sqrt).then_inc(S["std_ready"], 1)
                g = s - 5
                if live(g):
                    n = rows_of(g)
                    need(act, "x1T_ps", g + 1)
                    A(x1T[:, :, ds(g * ROWS, n)], bank[4][:, 0:2 * ROWS].rearrange("p (k n) -> p k n", k=2)[:, :, 0:n],
                      ACT.Copy).then_inc(S["x1T_ready"], 1)

            sweep(act, body=phase1, **P1)

            def phase2(c, par, pair):
                need(act, "rope_ps", 4 * (c - 1))
                need(act, "lat_ps", 2 * c + 1)
                A(ctq[:, par, :], bank[0][:, 0:CHUNK], ACT.Identity, bias=colb[:, 0:1]).then_inc(S["lat_ready"], 1)
                need(act, "lat_ps", 2 * c + 2)
                A(latT[:, ds(c * CHUNK, CHUNK)], bank[1][:, 0:CHUNK], ACT.Identity, bias=colb[:, 1:2]).then_inc(S["lat_ready"], 1)

            sweep(act, body=phase2, **P2)

            act.wait_ge(S["rope_c"], 4 * 4 * CHUNKS)
            act.wait_ge(S["attn_zero"], 2)

            def copy_round(g, gp, r):
                n = rows_of(g)
                b = bank[2 + r % 2]
                need(act, "pT_ps", 4 * g + r + 1)
                need(act, "pv_ps", 4 * (g - 1))
                A(pT[0:n, gp, r * ROUND * n:(r + 1) * ROUND * n], b[0:n, 0:ROUND * n], ACT.Copy).then_inc(S["pT_act"], 1)

            def phase3(s, par, pair):
                if live(s - 2):
                    copy_round(s - 2, par, 0)
                g = s - 3
                if live(g):
                    n, gp = rows_of(g), 1 - par
                    need(act, "attT_ps", g + 1)
                    need(act, "proj_ps", g - 1)
                    A(attT[:, gp, :, 0:n], bank[6][:, 0:2 * ROWS].rearrange("p (k n) -> p k n", k=2)[:, :, 0:n], ACT.Copy).then_inc(S["attT_ready"], 1)
                if live(s - 2):
                    copy_round(s - 2, par, 2)
                g = s - 1
                if live(g):
                    n, gp = rows_of(g), 1 - par
                    need(act, "max_c", 2 * g + 2)
                    need(act, "pT_ps", 4 * (g - 1))
                    m = images_of(g)
                    wide = p_wide[0:n, gp, 0:HEADS * n].rearrange("p (h i t) -> p h i t", h=HEADS, i=m)
                    for i in range(m):
                        ins = A(wide[:, :, i, :], shifted[0:n, gp, :].rearrange("p (h t) -> p h t", t=TOKENS), ACT.Exp,
                                scale=SCORE_SCALE, bias=cst(C_NOT_IMAGE, n)[:, i:i + 1])
                    ins.then_inc(S["p_wide_ready"], 1)
                if live(s):
                    m = images_of(s)
                    need(act, "scores_ps", 2 * (s - 1))
                    A(q_pad[:, par, :, :].rearrange("p h (i w) -> p h i w", i=PER_GROUP)[:, :, 0:m, 0:TOKENS],
                      qT[:, :, ds(s * ROWS, m * TOKENS)].rearrange("p h (i t) -> p h i t", t=TOKENS), ACT.Copy).then_inc(S["queries_ready"], 1)
                    k_src = kT[:, 1, ds(s * ROWS, m * TOKENS)].rearrange("p (i t) -> p i t", t=TOKENS)
                    blocks = k_blocks[:, par, 1, 0:m * HEAD_SPAN].rearrange("p (i h t) -> p i h t", i=m, h=8)
                    for h in range(8):
                        ins = A(blocks[:, :, h, :], k_src, ACT.Copy, scale=cst(C_HEAD)[:, h:h + 1])
                    ins.then_inc(S["keys_act_ready"], 1)

            sweep(act, body=phase3, **P3)

            act.wait_ge(S["ln4_c"], GROUPS + 2)
            A(sc4[:, 1, :], sc4[:, 0, :], ACT.Sqrt).then_inc(S["sd4_ready"], 1)
            for pair in range(GROUPS // 2):
                need(act, "x2T_ps", pair + 1)
                need(act, "logits_ps", pair - 1)
                n = rows_of(2 * pair + 1)
                width = 2 * ROWS + n if n < ROWS else 4 * ROWS
                ins = A(x2T[:, pair % 2, 0:width], bank[pair % 2][:, 0:width], ACT.Copy)
                if n < ROWS:
                    ins = A(x2T[:, pair % 2, 3 * ROWS:3 * ROWS + n], bank[pair % 2][:, 3 * ROWS:3 * ROWS + n], ACT.Copy)
                ins.then_inc(S["x2T_ready"], 1)
            act.wait_ge(S["route_in"], 1)
            A(lg[:, 2, :], lg[:, 1, :], ACT.Exp).then_inc(S["exp4_ready"], 1)

            act.wait_ge(S["x2_stored"], 32)
            act.wait_ge(S["hi_stored"], 16 * PIECES)
            act.wait_ge(S["lo_stored"], 16 * PIECES)
            act.wait_ge(S["resid_stored"], 16 * GROUPS)
            act.wait_ge(S["plan_ready"], 1)

            def split_x(j, par):
                need(act, "xsT_ps", j + 1)
                need(act, "ug_ps", 2 * (j - 1) + 1)
                A(xsT[0][:, par, :, :], bank[7][:, 0:256].rearrange("p (k n) -> p k n", k=2), ACT.Copy).then_inc(S["xs_hi"], 1)

            def gated(j, c):
                need(act, "ug_ps", 2 * j + c + 2)
                need(act, "hidT_ps", 2 * (j - 1) + c + 1)
                A(hid[:, c, :], bank[2 * c][:, :], ACT.Gelu).then_inc(S["gelu_c"], 1)
                need(act, "gate_in_ready", 2 * j + c + 2)
                A(gate_sb[:, c, :], gate_sb[:, c, :], ACT.Tanh, scale=0.5).then_inc(S["gelu_c"], 1)

            def split_hidden(j, par, c):
                need(act, "hidT_ps", 2 * j + c + 1)
                need(act, "y_ps", j)
                A(hidT[0][:, par, 4 * c:4 * c + 4, :], bank[4 + c][:, :].rearrange("p (k n) -> p k n", k=4), ACT.Copy, scale=0.5).then_inc(S["hid_hi"], 1)

            def slot(j, buf, first, last):
                par = buf % 2
                gated(j, 0)
                if not first:
                    split_hidden(j - 1, 1 - par, 1)
                if not last:
                    split_x(j + 1, 1 - par)
                gated(j, 1)
                split_hidden(j, par, 0)

            def group(j, buf, count):
                for k in range(count):
                    slot(j + k, (buf + k) % X_BUFFERS, isinstance(j, int) and j + k == 0, isinstance(j, int) and j + k + 1 == SLOTS)

            split_x(0, 0)
            slot_groups(act, group, tail=8)
            split_hidden(SLOTS - 1, (SLOTS - 1) % 2, 1)

        @block.vector
        def _(v):
            v.memset(x_in[:, :, :], 0.0).then_inc(S["setup_done"], 1)
            v.memset(ln_mv[:, :, :, :], 1.0).then_inc(S["setup_c"], 1)
            def added_rows():
                v.wait_ge(S["const_loaded"], 16)
                v.wait_ge(S["rows_loaded"], 16 * (2 + PER_GROUP))
                is_patch, is_cls = cst(C_PATCH, ROWS)[:, 0:1], cst(C_PATCH, ROWS)[:, 1:2]
                v.tensor_scalar(mul_rows[:, :], ln2_g, is_patch, None, ALU.mult).then_inc(S["setup_c"], 1)
                v.scalar_tensor_tensor(tmp_rows[:, :], ln2_b, is_patch, pos_sb[:, :], ALU.mult, ALU.add).then_inc(S["setup_c"], 1)
                v.wait_ge(S["setup_c"], 3)
                v.scalar_tensor_tensor(add_rows[:, :], cls_row, is_cls, tmp_rows[:, :], ALU.mult, ALU.add).then_inc(S["setup_c"], 1)

            def round_piece(pair, base, limit):
                if isinstance(pair, int) and base + pair >= limit:
                    return
                q = base + pair
                need_first(v, "hi_stored", q * 16)
                need_first(v, "piece_loaded", q * 16 + 16)
                v.tensor_copy(hi_piece[:, :], raw_piece[:, :]).then_inc(S["piece_hi"], 1)

            def phase1(s, par, pair):
                g1, g2, g3 = s, s - 3, s - 4
                if live(g1):
                    n = rows_of(g1)
                    need(v, f"x_loaded{par}", x_loaded_after(g1, pair))
                    for b in range(2):
                        v.bn_stats(ln1_st[0:n, par, b, :], x_in[0:n, par, b * 384:(b + 1) * 384]).then_inc(S["ln1_c"], 1)
                if live(g2):
                    n = rows_of(g2)
                    need(v, "z_ps", g2 + 1)
                    v.tensor_tensor(z_sb[0:n, par, :], bank[2 + (1 - par)][0:n, 0:DIM], b_proj[0:n, :], ALU.add).then_inc(S["ln2_c"], 1)
                if live(g1):
                    n = rows_of(g1)
                    need_first(v, "ln1_c", 3 * g1 + 2)
                    v.bn_aggr(ln_mv[0:n, par, 0, :], ln1_st[0:n, par, :, :]).then_inc(S["ln1_c"], 1)
                if live(g3):
                    n = rows_of(g3)
                    need(v, "resid_c", 2 * g3 + 2)
                    v.bn_stats(ln3_st[0:n, par, :], resid[0:n, ds(g3 * DIM, DIM)]).then_inc(S["ln3_c"], 1)
                if live(g2):
                    n = rows_of(g2)
                    need(v, "ln2_c", 3 * g2 + 1)
                    v.bn_stats(ln2_st[0:n, par, :], z_sb[0:n, par, :]).then_inc(S["ln2_c"], 1)
                if live(g3):
                    n = rows_of(g3)
                    need_first(v, "ln3_c", 2 * g3 + 1)
                    v.bn_aggr(ln_mv[0:n, par, 2, :], ln3_st[0:n, par, :]).then_inc(S["ln3_c"], 1)
                if live(g2):
                    n = rows_of(g2)
                    need_first(v, "ln2_c", 3 * g2 + 2)
                    v.bn_aggr(ln_mv[0:n, par, 1, :], ln2_st[0:n, par, :]).then_inc(S["ln2_c"], 1)
                if isinstance(s, int) and s == 0:
                    added_rows()
                if live(g1): need(v, "ln1_c", 3 * g1 + 3)
                if live(g2): need(v, "ln2_c", 3 * g2 + 3)
                if live(g3): need(v, "ln3_c", 2 * g3 + 2)
                ve, r0 = ln_ve[:, par, :], ln_r0[:, par, :]
                t = [ln_t[:, par, i, :] for i in range(3)]
                v.tensor_scalar(ve, ln_mv[:, par, :, 1], 1e-5, None, ALU.add).then_inc(S["ln_c"], 1)
                need(v, "std_ready", s + 1)
                v.reciprocal(r0, ln_sd[:, par, :]).then_inc(S["ln_c"], 1)
                need(v, "ln_c", 6 * s + 2)
                v.tensor_tensor(t[0], r0, r0, ALU.mult).then_inc(S["ln_c"], 1)
                need(v, "ln_c", 6 * s + 3)
                v.tensor_tensor(t[1], t[0], ve, ALU.mult).then_inc(S["ln_c"], 1)
                need(v, "ln_c", 6 * s + 4)
                v.tensor_scalar(t[2], t[1], -0.5, 1.5, ALU.mult, ALU.add).then_inc(S["ln_c"], 1)
                need(v, "ln_c", 6 * s + 5)
                v.tensor_tensor(ln_rs[:, par, :], r0, t[2], ALU.mult).then_inc(S["ln_c"], 1)
                need(v, "ln_c", 6 * s + 6)

                def norm(o, i, n, w, name):
                    v.tensor_scalar(o, i, ln_mv[0:n, par, w, 0:1], ln_rs[0:n, par, w:w + 1], ALU.subtract, ALU.mult).then_inc(S[name], 1)
                if live(g1):
                    n = rows_of(g1)
                    need(v, "xT_ps", g1 - 1)
                    norm(x_norm[0:n, par, :], x_in[0:n, par, :], n, 0, "x_norm_ready")
                if live(g2):
                    n = rows_of(g2)
                    need(v, "resid_c", 2 * (g2 - 1))
                    norm(z_norm[0:n, 1 - par, :], z_sb[0:n, par, :], n, 1, "z_norm_ready")
                if live(g3):
                    n = rows_of(g3)
                    need(v, "x1T_ps", g3 - 1)
                    norm(x1[0:n, par, :], resid[0:n, ds(g3 * DIM, DIM)], n, 2, "x1_ready")
                if par == 1:
                    round_piece(pair, 0, PIECES_EARLY)

            sweep(v, body=phase1, **P1)
            v.wait_ge(S["x1T_ready"], GROUPS)
            v.wait_ge(S["resid_c"], 2 * GROUPS)
            v.wait_ge(S["weights_loaded"], 16 * 6)

            def phase2(c, par, pair):
                for j in range(4):
                    half, q, tri = j % 2, j // 2, c * 4 + j
                    base = 3 * (j % 2)
                    ps = [bank[2 + base + i][:, 0:CHUNK] for i in range(3)]
                    t = [rot[:, j % 2, i, :] for i in range(3)]
                    bcol = 2 + 6 * q + half
                    table = [rope_sb[:, w, half, :].unsqueeze(1).broadcast_to([128, CHUNK_IMAGES, TOKENS]) for w in range(2)]

                    def im(x):
                        return x.rearrange("p (i t) -> p i t", t=TOKENS)
                    need(v, "rope_ps", tri + 1)
                    need(v, "rope_c", tri * 4 - 4)
                    v.scalar_tensor_tensor(im(t[0]), im(ps[0]), colb[:, bcol:bcol + 1], table[0], ALU.add, ALU.mult).then_inc(S["rope_c"], 1)
                    v.scalar_tensor_tensor(im(t[1]), im(ps[1]), colb[:, bcol + 2:bcol + 3], table[1], ALU.add, ALU.mult).then_inc(S["rope_c"], 1)
                    need(v, "rope_c", tri * 4 + 1)
                    v.scalar_tensor_tensor(t[2], ps[2], colb[:, bcol + 4:bcol + 5], t[0], ALU.add, ALU.add).then_inc(S["rope_c"], 1)
                    need(v, "rope_c", tri * 4 + 3)
                    v.tensor_tensor((qT if q else kT)[:, half, ds(c * CHUNK, CHUNK)], t[2], t[1], ALU.add).then_inc(S["rope_c"], 1)

            sweep(v, body=phase2, **P2)
            v.wait_ge(S["rope_c"], 4 * 4 * CHUNKS)
            v.wait_ge(S["rope_ps"], 4 * CHUNKS)

            v.memset(q_pad[:, :, :, :], 0.0).then_inc(S["attn_zero"], 1)
            v.memset(v_one[:, :, :, :], 1.0).then_inc(S["attn_zero"], 1)
            v.wait_ge(S["attn_zero"], 2)

            def copy_round(g, gp, r):
                n = rows_of(g)
                need(v, "pT_ps", 4 * g + r + 1)
                need(v, "pv_ps", 4 * (g - 1))
                v.tensor_copy(pT[0:n, gp, r * ROUND * n:(r + 1) * ROUND * n], bank[2 + r % 2][0:n, 0:ROUND * n]).then_inc(S["pT_dve"], 1)

            def phase3(s, par, pair):
                g = s - 1
                if live(g):
                    n, gp = rows_of(g), 1 - par
                    need(v, "scores_ps", 2 * g + 2)
                    need(v, "p_wide_ready", g - 1)
                    for half in range(2):
                        sc = bank[half][0:n, 0:HEAD_SPAN].rearrange("p (h t) -> p h t", t=TOKENS)
                        ins = v.tensor_reduce(top[0:n, gp, 8 * half:8 * half + 8], sc, AX.X, ALU.max)
                    ins.then_inc(S["max_c"], 1)
                if live(s - 2):
                    copy_round(s - 2, par, 1)
                if live(g):
                    n, gp = rows_of(g), 1 - par
                    need(v, "max_c", 2 * g + 1)
                    for half in range(2):
                        sc = bank[half][0:n, 0:HEAD_SPAN].rearrange("p (h t) -> p h t", t=TOKENS)
                        ins = v.tensor_tensor(shifted[0:n, gp, half * HEAD_SPAN:(half + 1) * HEAD_SPAN].rearrange("p (h t) -> p h t", t=TOKENS),
                                              sc, top[0:n, gp, 8 * half:8 * half + 8].unsqueeze(2).broadcast_to([n, 8, TOKENS]), ALU.subtract)
                    ins.then_inc(S["max_c"], 1)
                    need(v, "v_ps", g + 1)
                    need(v, "pv_ps", 4 * (g - 1))
                    v.tensor_tensor(v_one[0:n, gp, :, 0:HEAD_DIM], bank[4][0:n, 0:DIM].rearrange("p (h d) -> p h d", h=HEADS),
                                    b_v[0:n, :].rearrange("p (h d) -> p h d", h=HEADS), ALU.add).then_inc(S["v_ready"], 1)
                if live(s - 2):
                    copy_round(s - 2, par, 3)
                g = s - 3
                if live(g):
                    n, gp = rows_of(g), 1 - par
                    here = resid[0:n, ds(g * DIM, DIM)]
                    need(v, "proj_ps", g + 1)
                    v.tensor_tensor(att_b[0:n, gp, :], bank[7][0:n, 0:DIM], b_o[0:n, :], ALU.add).then_inc(S["att_c"], 1)
                    need(v, "att_c", 1 * (g + 1))
                    v.tensor_tensor(here, here, att_b[0:n, gp, :], ALU.add).then_inc(S["resid_done"], 1)
                    need(v, "resid_done", g + 1)
                    v.bn_stats(ln4_stats[0:n, ds(g, 1), :], here).then_inc(S["ln4_c"], 1)
                g = s - 2
                if live(g):
                    n, gp = rows_of(g), par
                    pv = bank[5][0:n, 0:HEADS * 17].rearrange("p (h d) -> p h d", h=HEADS)
                    need(v, "pv_ps", 4 * g + 4)
                    need(v, "attT_ps", g - 1)
                    v.reciprocal(inv_sum[0:n, gp, :].unsqueeze(2), pv[:, :, 16:17]).then_inc(S["heads_c"], 1)
                    need(v, "heads_c", 2 * g + 1)
                    v.tensor_tensor(att[0:n, gp, :].rearrange("p (h d) -> p h d", h=HEADS), pv[:, :, 0:16],
                                    inv_sum[0:n, gp, :].unsqueeze(2).broadcast_to([n, HEADS, HEAD_DIM]), ALU.mult).then_inc(S["heads_c"], 1)
                if par == 1:
                    round_piece(pair, PIECES_EARLY, PIECES)

            sweep(v, body=phase3, **P3)
            v.wait_ge(S["ln4_c"], GROUPS)
            v.wait_ge(S["pT_act"], 2 * GROUPS)
            v.wait_ge(S["attT_ready"], GROUPS)
            v.wait_ge(S["proj_ps"], GROUPS)

            count = [0]

            def step(ins):
                count[0] += 1
                ins.then_inc(S["route_c"], 1)
                v.wait_ge(S["route_c"], count[0])

            step(v.memset(mv4[:, :, :], 1.0))
            for g in range(GROUPS):
                n = rows_of(g)
                ins = v.bn_aggr(mv4[0:n, g, :], ln4_stats[0:n, g, :])
            ins.then_inc(S["ln4_c"], 1)
            v.wait_ge(S["ln4_c"], GROUPS + 1)
            v.tensor_scalar(sc4[:, 0, :], mv4[:, :, 1], 1e-5, None, ALU.add).then_inc(S["ln4_c"], 1)
            v.wait_ge(S["sd4_ready"], 1)
            step(v.reciprocal(sc4[:, 2, :], sc4[:, 1, :]))
            step(v.tensor_tensor(sc4[:, 3, :], sc4[:, 2, :], sc4[:, 2, :], ALU.mult))
            step(v.tensor_tensor(sc4[:, 4, :], sc4[:, 3, :], sc4[:, 0, :], ALU.mult))
            step(v.tensor_scalar(sc4[:, 5, :], sc4[:, 4, :], -0.5, 1.5, ALU.mult, ALU.add))
            step(v.tensor_tensor(sc4[:, 6, :], sc4[:, 2, :], sc4[:, 5, :], ALU.mult))
            for g in range(GROUPS):
                n = rows_of(g)
                v.tensor_scalar(x2[0:n, g, :], resid[0:n, g * DIM:(g + 1) * DIM], mv4[0:n, g, 0:1], sc4[0:n, 6, g:g + 1],
                                ALU.subtract, ALU.mult).then_inc(S["x2_ready"], 1)
            def L(i, n=ROWS):
                return lg[0:n, i, :].rearrange("p (g e) -> p g e", e=EXPERTS)

            def per_token(x):
                return x.unsqueeze(2).broadcast_to([ROWS, GROUPS, EXPERTS])
            sm = [small[:, 0, 0, :], small[:, 0, 1, :], small[:, 1, 0, :], small[:, 1, 1, :], small[:, 2, 0, :], small[:, 2, 1, :],
                  small[:, 3, 0, :], small[:, 3, 1, :]]
            choice_weight, valid_weight, choice_pos, choice_slot, choice_at = (small[:, i, :, :] for i in (5, 6, 4, 7, 8))
            v.memset(running[:, :, 0:RUN_PAD], 0.0).then_inc(S["rank_c"], 1)
            v.memset(cnt[:, :, 0:4], 0.0).then_inc(S["rank_c"], 1)
            v.wait_ge(S["rank_c"], 2)
            step(v.memset(lg[:, 0, :], 0.0))
            v.wait_ge(S["logits_ps"], GROUPS // 2)
            full = (GROUPS - 1) * EXPERTS
            rest = rows_of(GROUPS - 1)
            step(v.tensor_tensor(lg[:, 0, 0:full].rearrange("p (g e) -> p g e", e=EXPERTS),
                                 bank[2][0:ROWS, 0:full].rearrange("p (g e) -> p g e", e=EXPERTS),
                                 b_router.unsqueeze(1).broadcast_to([ROWS, GROUPS - 1, EXPERTS]), ALU.add))
            step(v.tensor_tensor(lg[0:rest, 0, full:], bank[2][0:rest, full:full + EXPERTS], b_router[0:rest, :], ALU.add))
            step(v.tensor_reduce(sm[0], L(0), AX.X, ALU.max))
            v.tensor_tensor(L(1), L(0), per_token(sm[0]), ALU.subtract).then_inc(S["route_in"], 1)
            v.wait_ge(S["exp4_ready"], 1)
            step(v.tensor_reduce(sm[1], L(2), AX.X, ALU.add))
            step(v.reciprocal(sm[2], sm[1]))
            step(v.tensor_tensor(L(3), L(2), per_token(sm[2]), ALU.mult))
            rank = cst(C_RANK, ROWS).rearrange("p (g e) -> p g e", e=EXPERTS)

            def pick(src, best, sel, a, b):
                step(v.tensor_reduce(best, src, AX.X, ALU.max))
                step(v.tensor_tensor(L(a), src, per_token(best), ALU.is_equal))
                step(v.tensor_tensor(L(b), L(a), rank, ALU.mult))
                step(v.tensor_reduce(sm[3], L(b), AX.X, ALU.max))
                step(v.tensor_tensor(sel, L(b), per_token(sm[3]), ALU.is_equal))
            pick(L(3), sm[4], L(6), 4, 5)
            step(v.scalar_tensor_tensor(L(7), L(6), -2.0, L(3), ALU.mult, ALU.add))
            pick(L(7), sm[5], L(8), 4, 5)
            step(v.tensor_tensor(L(9), L(6), L(8), ALU.add))
            v.tensor_tensor(L(10), L(9), per_token(cst(C_VALID, ROWS)), ALU.mult).then_inc(S["route_in"], 1)
            step(v.tensor_tensor(sm[6], sm[4], sm[5], ALU.add))
            step(v.reciprocal(sm[7], sm[6]))
            v.tensor_tensor(choice_weight[:, 0, :], sm[4], sm[7], ALU.mult)
            step(v.tensor_tensor(choice_weight[:, 1, :], sm[5], sm[7], ALU.mult))
            step(v.tensor_tensor(valid_weight, choice_weight, cst(C_VALID, ROWS).unsqueeze(1).broadcast_to([ROWS, TOP, GROUPS]), ALU.mult))
            flat = "p c g -> p (c g)"
            step(v.tensor_copy(weight_hl[:, 0, :], valid_weight.rearrange(flat)))
            step(v.tensor_tensor(weight_hl[:, 1, :], valid_weight.rearrange(flat), weight_hl[:, 0, :].bitcast(f32), ALU.subtract))
            v.wait_ge(S["totals_ps"], 1)
            step(v.tensor_copy(running[:, 0, RUN_PAD:], bank[4][0:ROWS, 0:NE]))
            src, shift = 0, 1
            while shift < GROUPS:
                w = RUN_PAD - shift * EXPERTS
                step(v.tensor_tensor(running[:, 1 - src, RUN_PAD:], running[:, src, RUN_PAD:], running[:, src, w:w + NE], ALU.add))
                src, shift = 1 - src, shift * 2
            v.wait_ge(S["earlier_ps"], 1)
            w = RUN_PAD - EXPERTS
            step(v.tensor_tensor(lg[:, 11, :], bank[3][0:ROWS, 0:NE], running[:, src, w:w + NE], ALU.add))
            total = running[:, src, RUN_PAD + NE - EXPERTS:]
            over_v = over[:, :].rearrange("p (e t) -> p e t", e=EXPERTS)
            step(v.tensor_tensor(over_v, total.unsqueeze(2).broadcast_to([ROWS, EXPERTS, 19]),
                                 cst(C_THRESH, ROWS).rearrange("p (e t) -> p e t", e=EXPERTS), ALU.is_gt))
            step(v.tensor_reduce(cnt[:, 0, 4:], over_v, AX.X, ALU.add))
            a = 0
            for shift in (1, 2, 4):
                step(v.tensor_tensor(cnt[:, a + 1, 4:], cnt[:, a, 4:], cnt[:, a, 4 - shift:4 - shift + EXPERTS], ALU.add))
                a += 1
            tiles = cnt[:, a, 4:]
            step(v.tensor_scalar(cnt[:, 4, 4:], cnt[:, a, 3:3 + EXPERTS], float(SLOT), None, ALU.mult))
            step(v.tensor_tensor(L(12), L(11), cnt[:, 4, 4:].unsqueeze(1).broadcast_to([ROWS, GROUPS, EXPERTS]), ALU.add))
            v.tensor_tensor(L(4), L(12), L(6), ALU.mult)
            step(v.tensor_tensor(L(5), L(12), L(8), ALU.mult))
            v.tensor_reduce(choice_pos[:, 0, :], L(4), AX.X, ALU.add)
            step(v.tensor_reduce(choice_pos[:, 1, :], L(5), AX.X, ALU.add))
            step(v.tensor_copy(row_int[:, 0, :, :], choice_pos))
            step(v.tensor_scalar(row_int[:, 1, :, :], row_int[:, 0, :, :], 7, None, ALU.logical_shift_right))
            step(v.tensor_copy(choice_slot, row_int[:, 1, :, :]))
            v.scalar_tensor_tensor(choice_at, choice_slot, -float(SLOT), choice_pos, ALU.mult, ALU.add).then_inc(S["rank_c"], 1)
            v.wait_ge(S["rank_c"], 3)
            v.wait_ge(S["hi_stored"], 16 * PIECES)
            v.wait_ge(S["lo_stored"], 16 * PIECES)
            v.tensor_tensor(in_slot[:, :, :], cst(C_SLOTNO, ROWS).rearrange("p (j e) -> p e j", e=8)[:, 0:1, :].broadcast_to([ROWS, CHOICES, SLOTS]),
                            choice_slot.rearrange(flat).unsqueeze(2).broadcast_to([ROWS, CHOICES, SLOTS]), ALU.is_equal).then_inc(S["in_slot_c"], 1)
            v.wait_ge(S["in_slot_c"], 1)
            v.tensor_tensor(slot_values[:, :, 0, :].rearrange("p (c g) j -> p c g j", c=TOP), in_slot[:, :, :].rearrange("p (c g) j -> p c g j", c=TOP),
                            cst(C_TOKEN, ROWS).unsqueeze(1).unsqueeze(3).broadcast_to([ROWS, TOP, GROUPS, SLOTS]), ALU.mult).then_inc(S["tokens_in"], 1)
            v.tensor_tensor(slot_values[:, :, 1, :], in_slot[:, :, :],
                            weight_hl[:, 0, :].bitcast(f32).unsqueeze(2).broadcast_to([ROWS, CHOICES, SLOTS]), ALU.mult).then_inc(S["tokens_in"], 1)
            for turn in range(TURNS):
                need(v, "slots_ps", turn - AT_BUFFERS + 1)
                v.tensor_tensor(at_row[:, turn % AT_BUFFERS, :, :], cst(C_ROW, ROWS).unsqueeze(1).broadcast_to([ROWS, PER_TURN, 128]),
                                choice_at.rearrange(flat)[:, turn * PER_TURN:(turn + 1) * PER_TURN].unsqueeze(2).broadcast_to([ROWS, PER_TURN, 128]),
                                ALU.is_equal).then_inc(S["at_row_c"], 1)
            step(v.tensor_tensor(smap[0:1, :].rearrange("p (j e) -> p j e", e=8),
                                 cst(C_SLOTNO, 1).rearrange("p (j e) -> p j e", e=8),
                                 tiles[0:1, :].unsqueeze(1).broadcast_to([1, SLOTS, 8]), ALU.is_ge))
            step(v.tensor_reduce(smap_sum[0:1, :], smap[0:1, :].rearrange("p (j e) -> p j e", e=8)[:, :, 0:7], AX.X, ALU.add))
            step(v.tensor_copy(slot_expert[0:1, :], smap_sum[0:1, :]))
            step(v.tensor_copy(tiles_done[0:1, :], tiles[0:1, :]))
            v.wait_ge(S["slots_ps"], TURNS)
            v.tensor_copy(table_parts[:, 2, :], bank[5][:, SLOTS:2 * SLOTS]).then_inc(S["slot_table_c"], 1)
            v.tensor_scalar(table_parts[:, 0, :], bank[5][:, 0:SLOTS], 0.0, cst(C_PAD), ALU.is_equal, ALU.mult).then_inc(S["slot_table_c"], 1)
            v.wait_ge(S["slot_table_c"], 2)
            v.scalar_tensor_tensor(table_parts[:, 1, :], bank[5][:, 0:SLOTS], -1.0, table_parts[:, 0, :], ALU.add, ALU.add).then_inc(S["slot_table_c"], 1)
            v.tensor_tensor(slot_weight[:, :], bank[5][:, 2 * SLOTS:3 * SLOTS], table_parts[:, 2, :], ALU.add).then_inc(S["slot_table_c"], 1)
            v.wait_ge(S["slot_table_c"], 4)
            v.tensor_copy(slot_token[:, :], table_parts[:, 1, :]).then_inc(S["slot_table_c"], 1)
            v.wait_ge(S["slot_table_c"], 5)
            v.engine_nop().then_inc(S["plan_ready"], 1)
            v.memset(code[:, :, :], 0.0).then_inc(S["code_c"], 1)
            for i in range(CODE):
                v.wait_ge(S["code_c"], i + 1)
                ahead = CODE - 2 - i
                lo, hi = max(0, -ahead), SLOTS - max(0, ahead)
                if i == 0:
                    v.tensor_copy(code[:, 0, lo:hi], smap_sum[:, lo + ahead:hi + ahead]).then_inc(S["code_c"], 1)
                else:
                    v.scalar_tensor_tensor(code[:, i, lo:hi], code[:, i - 1, lo:hi], float(EXPERTS), smap_sum[:, lo + ahead:hi + ahead],
                                           ALU.mult, ALU.add).then_inc(S["code_c"], 1)
            v.tensor_scalar(code[:, CODE - 1, 0:1], code[:, CODE - 2, 0:1], float(EXPERTS), None, ALU.mult).then_inc(S["code_c"], 1)
            v.wait_ge(S["code_c"], CODE + 2)
            v.tensor_copy(slot_code[:, :], code[:, CODE - 1, :]).then_inc(S["code_c"], 1)

            v.wait_ge(S["x2_stored"], 32)
            v.wait_ge(S["code_c"], CODE + 3)
            v.wait_ge(S["hi_stored"], 16 * PIECES)
            v.wait_ge(S["lo_stored"], 16 * PIECES)
            v.wait_ge(S["resid_stored"], 16 * GROUPS)
            v.memset(hid[0:2, 0, 0:128], 1.0).then_inc(S["ones_ready"], 1)
            v.wait_ge(S["ones_ready"], 1)
            v.tensor_copy(ones2[:, :], hid[0:2, 0, 0:128]).then_inc(S["ones_ready"], 1)
            v.wait_ge(S["ones_ready"], 2)
            v.sem_inc(S["gate_in_ready"], 1)

            def split_x(j, par):
                need(v, "xs_hi", j + 1)
                need(v, "ug_ps", 2 * (j - 1) + 1)
                v.tensor_tensor(xsT[1][:, par, :, :], bank[7][:, 0:256].rearrange("p (k n) -> p k n", k=2),
                                xsT[0][:, par, :, :].bitcast(f32), ALU.subtract).then_inc(S["xs_lo"], 1)

            def gate_bias_added(j, c, e):
                need(v, "ug_ps", 2 * j + c + 2)
                need(v, "hid_ready", 2 * (j - 1) + c + 1)
                v.tensor_tensor(gate_sb[:, c, :], bank[2 * c + 1][:, :],
                                up_sb[:, ds(e % UP_BUFFERS * UP_COLS + U_BIAS_GATE + c * 512, 512)].bitcast(f32), ALU.add).then_inc(
                    S["gate_in_ready"], 1)

            def gate(j, c):
                need(v, "gelu_c", 4 * j + 2 * c + 2)
                v.scalar_tensor_tensor(hid[:, c, :], gate_sb[:, c, :], 1.0, hid[:, c, :], ALU.add, ALU.mult).then_inc(S["hid_ready"], 1)

            def split_hidden(j, par, c):
                need(v, "hid_hi", 2 * j + c + 1)
                need(v, "y_ps", j)
                v.scalar_tensor_tensor(hidT[1][:, par, 4 * c:4 * c + 4, :], bank[4 + c][:, :].rearrange("p (k n) -> p k n", k=4), 0.5,
                                       hidT[0][:, par, 4 * c:4 * c + 4, :].bitcast(f32), ALU.mult, ALU.subtract).then_inc(S["hid_lo"], 1)

            def link_of(j):
                def link(i, ins):
                    ins.then_inc(S["y_c"], 1)
                    v.wait_ge(S["y_c"], j * YC + i)
                return link
            y_mean = y_mv[:, 0:1]
            c = [y_sc[:, i:i + 1] for i in range(8)]
            seed = y_int[:, 1:2].bitcast(f32)

            def finish_first(j, par, buf):
                link = link_of(j)
                need(v, "y_norm_ready", j)
                need(v, "y_out_ready", j)
                need(v, "y_ps", j + 2)
                link(1, v.tensor_tensor(y_norm[:, par, :], bank[6][:, 0:DIM], xs[:, buf, 0:DIM], ALU.add))
                link(2, v.bn_stats(y_st[:, :], y_norm[:, par, :]))
                v.nop(nofuse=True)
                link(3, v.bn_aggr(y_mv[:, :], y_st[:, :]))
                link(4, v.tensor_scalar(c[0], y_mv[:, 1:2], 1e-12, None, ALU.add))
                link(5, v.tensor_scalar(c[1], c[0], -0.5, None, ALU.mult))
                link(6, v.tensor_scalar(y_int[:, 0:1], c[0].bitcast(i32), 1, None, ALU.logical_shift_right))
                link(7, v.tensor_scalar(y_int[:, 1:2], y_int[:, 0:1], -1.0, float(0x5f3759df), ALU.mult, ALU.add))
                link(8, v.tensor_scalar(c[2], seed, seed, c[1], ALU.mult, ALU.mult))
                link(9, v.tensor_scalar(c[3], c[2], 1.5, seed, ALU.add, ALU.mult))

            def finish_newton(j):
                link = link_of(j)
                link(10, v.tensor_scalar(c[4], c[3], c[3], c[1], ALU.mult, ALU.mult))
                link(11, v.tensor_scalar(c[5], c[4], 1.5, c[3], ALU.add, ALU.mult))
                link(12, v.tensor_scalar(c[6], c[5], c[5], c[1], ALU.mult, ALU.mult))
                link(13, v.tensor_scalar(c[7], c[6], 1.5, c[5], ALU.add, ALU.mult))

            def finish_norm(j, par):
                v.tensor_scalar(y_norm[:, par, :], y_norm[:, par, :], y_mean, c[7], ALU.subtract, ALU.mult).then_inc(S["y_norm_ready"], 1)

            def slot(j, buf, first, last, e):
                par = buf % 2
                second = isinstance(j, int) and j == 1
                if not first and not second:
                    finish_first(j - 2, par, (buf - 2) % X_BUFFERS)
                gate_bias_added(j, 0, e)
                if not first and not second:
                    finish_newton(j - 2)
                gate(j, 0)
                if not first:
                    split_hidden(j - 1, 1 - par, 1)
                if not last:
                    split_x(j + 1, 1 - par)
                if not first and not second:
                    finish_norm(j - 2, par)
                gate_bias_added(j, 1, e)
                gate(j, 1)
                split_hidden(j, par, 0)

            def group(j, buf, count):
                es = experts_from(v, j, count)
                for k in range(count):
                    slot(j + k, (buf + k) % X_BUFFERS, isinstance(j, int) and j + k == 0, isinstance(j, int) and j + k + 1 == SLOTS, es[k + 1])

            split_x(0, 0)
            slot_groups(v, group, tail=8)
            finish_first(SLOTS - 2, (SLOTS - 2) % 2, (SLOTS - 2) % X_BUFFERS)
            split_hidden(SLOTS - 1, (SLOTS - 1) % 2, 1)
            finish_newton(SLOTS - 2)
            finish_norm(SLOTS - 2, (SLOTS - 2) % 2)
            finish_first(SLOTS - 1, (SLOTS - 1) % 2, (SLOTS - 1) % X_BUFFERS)
            finish_newton(SLOTS - 1)
            finish_norm(SLOTS - 1, (SLOTS - 1) % 2)

        @block.tensor
        def _(pe):
            mm, tr = pe.matmul, pe.transpose
            pe.wait_ge(S["const_loaded"], 16)
            pe.wait_ge(S["wproj_loaded"], 16)

            def phase1(s, par, pair):
                g = s - 1
                if live(g):
                    n, gp = rows_of(g), 1 - par
                    need(pe, "x_norm_ready", g + 1)
                    need(pe, "x_affT_ready", 2 * g)
                    for k in range(6):
                        ins = tr(bank[k // 3][:, (k % 3) * ROWS:(k % 3) * ROWS + n], x_norm[0:n, gp, k * 128:(k + 1) * 128], ident[0:n, 0:n])
                    ins.then_inc(S["xT_ps"], 1)
                g5 = s - 5
                if live(g5):
                    n = rows_of(g5)
                    need(pe, "x1_ready", g5 + 1)
                    need(pe, "x1T_ready", g5)
                    for k in range(2):
                        ins = tr(bank[4][:, k * ROWS:k * ROWS + n], x1[0:n, 1 - par, k * 128:(k + 1) * 128], ident[0:n, 0:n])
                    ins.then_inc(S["x1T_ps"], 1)
                g2 = s - 2
                if live(g2):
                    n = rows_of(g2)
                    need(pe, "x_affT_ready", 2 * g2 + 2)
                    need(pe, "ln2_c", 3 * (g2 - 2) + 1)
                    for k in range(6):
                        ins = mm(bank[2 + par][0:n, 0:DIM], x_affT[:, par, k, 0:n], wproj_sb[:, k, :], start=(k == 0), stop=(k == 5))
                    ins.then_inc(S["z_ps"], 1)

            sweep(pe, body=phase1, **P1)

            pe.wait_ge(S["weights_loaded"], 16 * 6)
            pe.wait_ge(S["x1T_ready"], GROUPS)

            def phase2(c, par, pair):
                def xk(k):
                    return x1T[:, k, ds(c * CHUNK, CHUNK)]
                need(pe, "lat_ready", 2 * c)
                for w in range(2):
                    for k in range(2):
                        ins = mm(bank[w][:, 0:CHUNK], wd_sb[:, k, w * LATENT:(w + 1) * LATENT], xk(k), start=(k == 0), stop=(k == 1))
                    ins.then_inc(S["lat_ps"], 1)
                for j in range(4):
                    half, q, tri = j % 2, j // 2, c * 4 + j
                    b = bank[2 + 3 * (j % 2):5 + 3 * (j % 2)]
                    cut = slice(half * 128, half * 128 + 128)
                    need(pe, "rope_c", tri * 4 - 4)
                    if q == 0:
                        for r in range(2):
                            for k in range(2):
                                mm(b[r][:, 0:CHUNK], wk_sb[:, 2 * r + k, cut], xk(k), start=(k == 0), stop=(k == 1))
                        need(pe, "lat_ready", 2 * c + 2)
                        ins = mm(b[2][:, 0:CHUNK], wk_sb[:, 4, cut], latT[:, ds(c * CHUNK, CHUNK)], start=True, stop=True)
                    else:
                        for r in range(3):
                            ins = mm(b[r][:, 0:CHUNK], wq_sb[:, r * DIM + half * 128:r * DIM + half * 128 + 128], ctq[:, par, :], start=True, stop=True)
                    ins.then_inc(S["rope_ps"], 1)

            sweep(pe, body=phase2, **P2)

            pe.wait_ge(S["rope_c"], 4 * 4 * CHUNKS)

            def phase3(s, par, pair):
                gd, gc, gb = s - 3, s - 2, s - 1

                def scores(half):
                    n, m, gp = rows_of(gb), images_of(gb), 1 - par
                    if half == 0:
                        need(pe, "keys_ready", 2 * gb + 2)
                    else:
                        need(pe, "keys_act_ready", gb + 1)
                    need(pe, "queries_ready", gb + 1)
                    need(pe, "max_c", 2 * gb)
                    for i in range(m):
                        ins = mm(bank[half][0:n, 0:HEAD_SPAN], q_pad[:, gp, half, i * ROWS:i * ROWS + n],
                                 k_blocks[:, gp, half, i * HEAD_SPAN:(i + 1) * HEAD_SPAN], start=(i == 0), stop=(i == m - 1))
                    ins.then_inc(S["scores_ps"], 1)

                def turn_round(r):
                    n = rows_of(gc)
                    need(pe, "p_wide_ready", gc + 1)
                    need(pe, "pT_act" if r % 2 == 0 else "pT_dve", 2 * gc + r // 2)
                    for h in range(ROUND):
                        head = r * ROUND + h
                        ins = tr(bank[2 + r % 2][0:n, h * n:(h + 1) * n], p_wide[0:n, par, head * n:(head + 1) * n], ident[0:n, 0:n])
                    ins.then_inc(S["pT_ps"], 1)

                def values_round(r):
                    n = rows_of(gc)
                    need(pe, "pT_act" if r % 2 == 0 else "pT_dve", 2 * gc + r // 2 + 1)
                    if r == 0:
                        need(pe, "v_ready", gc + 1)
                        need(pe, "heads_c", 2 * gc)
                    for h in range(ROUND):
                        head = r * ROUND + h
                        ins = mm(bank[5][0:n, head * 17:(head + 1) * 17], pT[0:n, par, head * n:(head + 1) * n], v_one[0:n, par, head, :],
                                 start=True, stop=True)
                    ins.then_inc(S["pv_ps"], 1)

                if live(gb):
                    scores(0)
                    scores(1)
                if live(gc):
                    turn_round(0)
                    turn_round(1)
                if live(gd):
                    n, gp = rows_of(gd), 1 - par
                    need(pe, "heads_c", 2 * gd + 2)
                    need(pe, "attT_ready", gd)
                    for k in range(2):
                        ins = tr(bank[6][:, k * ROWS:k * ROWS + n], att[0:n, gp, k * 128:(k + 1) * 128], ident[0:n, 0:n])
                    ins.then_inc(S["attT_ps"], 1)
                if live(gb):
                    n, gp = rows_of(gb), 1 - par
                    need(pe, "v_ready", gb)
                    mm(bank[4][0:n, 0:DIM], lat_g[:, gp, 0:n], wvo_sb[:, 0, :], start=True, stop=True).then_inc(S["v_ps"], 1)
                if live(gc):
                    turn_round(2)
                    turn_round(3)
                    values_round(0)
                    values_round(1)
                if live(gd):
                    n, gp = rows_of(gd), 1 - par
                    need(pe, "attT_ready", gd + 1)
                    need(pe, "att_c", gd)
                    for k in range(2):
                        ins = mm(bank[7][0:n, 0:DIM], attT[:, gp, k, 0:n], wvo_sb[:, 1 + k, :], start=(k == 0), stop=(k == 1))
                    ins.then_inc(S["proj_ps"], 1)
                if live(gc):
                    values_round(2)
                    values_round(3)

            sweep(pe, body=phase3, **P3)

            pe.wait_ge(S["att_c"], GROUPS)
            pe.wait_ge(S["resid_done"], GROUPS)
            PAIRS = GROUPS // 2
            for pair in range(PAIRS + 1):
                if pair < PAIRS:
                    need(pe, "x2_ready", 2 * pair + 2)
                    need(pe, "x2T_ready", pair - 1)
                    for i in range(2):
                        g = 2 * pair + i
                        n = rows_of(g)
                        for k in range(2):
                            at = (2 * i + k) * ROWS
                            ins = tr(bank[pair % 2][:, at:at + n], x2[0:n, g, k * 128:(k + 1) * 128], ident[0:n, 0:n])
                    ins.then_inc(S["x2T_ps"], 1)
                if pair >= 1:
                    need(pe, "x2T_ready", pair)
                    for i in range(2):
                        g = 2 * (pair - 1) + i
                        n = rows_of(g)
                        for k in range(2):
                            at = (2 * i + k) * ROWS
                            ins = mm(bank[2][0:n, g * EXPERTS:(g + 1) * EXPERTS], x2T[:, (pair - 1) % 2, at:at + n], wr_sb[:, k, :],
                                     start=(k == 0), stop=(k == 1))
                    ins.then_inc(S["logits_ps"], 1)
            pe.wait_ge(S["route_in"], 2)
            mm(bank[4][0:ROWS, 0:NE], cst(C_ONES, ROWS), lg[:, 10, :], start=True, stop=True).then_inc(S["totals_ps"], 1)
            mm(bank[3][0:ROWS, 0:NE], cst(C_BEFORE, ROWS), lg[:, 10, :], start=True, stop=True).then_inc(S["earlier_ps"], 1)
            pe.wait_ge(S["tokens_in"], 2)
            pe.wait_ge(S["weights_in"], 1)
            for turn in range(TURNS):
                pe.wait_ge(S["at_row_c"], turn + 1)
                for i in range(PER_TURN):
                    choice = turn * PER_TURN + i
                    ins = mm(bank[5][:, 0:3 * SLOTS], at_row[:, turn % AT_BUFFERS, i, :], slot_values[:, choice, :, :].rearrange("p t j -> p (t j)"),
                             start=(choice == 0), stop=(choice == CHOICES - 1))
                ins.then_inc(S["slots_ps"], 1)

            pe.sem_inc(S["ug_ps"], 1)
            pe.sem_inc(S["y_ps"], 1)
            pe.wait_ge(S["ones_ready"], 2)
            pe.wait_ge(S["code_c"], CODE + 3)

            def turn_x(j, buf):
                need(pe, f"xs_loaded{buf}", (j - buf) * (16 // X_BUFFERS) + 16)
                need(pe, "xs_lo", j)
                for k in range(2):
                    ins = tr(bank[7][:, k * 128:(k + 1) * 128], xs[:, buf, k * 128:(k + 1) * 128], ident)
                ins.then_inc(S["xsT_ps"], 1)

            def up_weight(e, which, half, at, width):
                return up_sb[:, ds(e % UP_BUFFERS * UP_COLS + (2 * which + half) * PIECE + at, width)]

            def down_weight(e, half, at, width):
                return down_sb[:, ds(e % DOWN_BUFFERS * DOWN_COLS + half * PIECE + at, width)]

            def up(j, par, c, e):
                if c == 0:
                    pe.wait_ge(S["up_loaded"], e * UP_LOADS + UP_LOADS)
                    need(pe, "xs_lo", j + 1)
                need(pe, "gelu_c", 4 * (j - 1) + 2 * c + 2)
                for t in range(2):
                    dst = bank[2 * c + t][:, :]
                    if t == 0:
                        mm(dst, ones2[:, :], up_sb[0:2, ds(e % UP_BUFFERS * UP_COLS + U_BIAS_UP + c * 512, 512)], start=True, stop=False)
                    for k in range(2):
                        at = k * FFN + c * 512
                        mm(dst, xsT[0][:, par, k, :], up_weight(e, t, 0, at, 512), start=(t == 1 and k == 0), stop=False)
                        mm(dst, xsT[0][:, par, k, :], up_weight(e, t, 1, at, 512), start=False, stop=False)
                        ins = mm(dst, xsT[1][:, par, k, :], up_weight(e, t, 0, at, 512), start=False, stop=(k == 1))
                ins.then_inc(S["ug_ps"], 1)

            def turn_hidden(j, c):
                need(pe, "hid_ready", 2 * j + c + 1)
                need(pe, "hid_lo", 2 * (j - 1) + c + 1)
                for k in range(4):
                    ins = tr(bank[4 + c][:, k * 128:(k + 1) * 128], hid[:, c, k * 128:(k + 1) * 128], ident)
                ins.then_inc(S["hidT_ps"], 1)

            def down(j, par, e):
                pe.wait_ge(S["down_loaded"], e * DOWN_LOADS + DOWN_LOADS)
                need(pe, "y_c", (j - 1) * YC + 1)
                y_bank = bank[6][:, 0:DIM]
                mm(y_bank, ones2[:, :], down_sb[0:2, ds(e % DOWN_BUFFERS * DOWN_COLS + D_BIAS, DIM)], start=True, stop=False)
                need(pe, "hid_lo", 2 * j + 2)
                for k in range(8):
                    mm(y_bank, hidT[0][:, par, k, :], down_weight(e, 0, k * DIM, DIM), start=False, stop=False)
                    mm(y_bank, hidT[0][:, par, k, :], down_weight(e, 1, k * DIM, DIM), start=False, stop=False)
                    ins = mm(y_bank, hidT[1][:, par, k, :], down_weight(e, 0, k * DIM, DIM), start=False, stop=(k == 7))
                ins.then_inc(S["y_ps"], 1)

            def expert_at(j):
                return pe.value_load(slot_expert[0:1, ds(j, 1)], min_val=0, max_val=EXPERTS - 1)

            def slot(j, buf, first, last, e, e_before):
                par = buf % 2
                up(j, par, 0, e)
                if not first:
                    turn_hidden(j - 1, 1)
                if not last:
                    turn_x(j + 1, (buf + 1) % X_BUFFERS)
                up(j, par, 1, e)
                turn_hidden(j, 0)
                if not first:
                    down(j - 1, 1 - par, e_before)

            def group(j, buf, count):
                start, end = isinstance(j, int) and j == 0, isinstance(j, int) and j + count == SLOTS
                es = experts_from(pe, j, count)
                for k in range(count):
                    slot(j + k, (buf + k) % X_BUFFERS, start and k == 0, end and k == count - 1, es[k + 1], es[k])

            turn_x(0, 0)
            slot_groups(pe, group, tail=8)
            turn_hidden(SLOTS - 1, 1)
            down(SLOTS - 1, (SLOTS - 1) % 2, expert_at(SLOTS - 1))


def kernel(**inputs):
    import numpy as np
    import concourse.bacc as bacc
    from concourse.bass_utils import run_bass_kernel_spmd as run

    x = {k: np.asarray(a) for k, a in inputs.items()}
    P = 16
    side = 96 // P
    patches = x["x"].reshape(IMAGES, 3, side, P, side, P).transpose(0, 2, 4, 3, 5, 1).reshape(IMAGES * PATCHES, PATCH_DIM)

    cols, width = constant_columns()
    consts = np.zeros((128, width), np.float32)
    p = np.arange(128)[:, None]

    def put(which, a):
        lo, hi = cols[which]
        consts[:, lo:hi] = np.broadcast_to(a, (128, hi - lo))
    put(C_IDENT, np.eye(128))
    put(C_BEFORE, p < np.arange(ROWS)[None])
    put(C_ONES, 1.0)
    put(C_HEAD, p // HEAD_DIM == np.arange(8)[None])
    put(C_IMAGE, p // TOKENS == np.arange(3)[None])
    put(C_PATCH, np.concatenate([p % TOKENS != 0, p % TOKENS == 0], 1))
    put(C_RANK, np.tile(EXPERTS - np.arange(EXPERTS), GROUPS)[None])
    put(C_VALID, p + ROWS * np.arange(GROUPS)[None] < ALL_TOKENS)
    put(C_THRESH, np.tile(np.where(np.arange(19) == 0, -1, SLOT * np.arange(19)), EXPERTS)[None])
    put(C_SLOTNO, np.repeat(np.arange(SLOTS), 8)[None])
    put(C_NOT_IMAGE, np.where(p // TOKENS == np.arange(3)[None], 0.0, -1e30))
    number = p + ROWS * np.arange(GROUPS)[None]
    put(C_TOKEN, np.where(number < ALL_TOKENS, number + 1, 0))
    put(C_PAD, p + ALL_TOKENS + 1)
    put(C_ROW, np.arange(128)[None])
    half = DIM // 2
    theta = (np.float32(10000.0) ** (np.float32(-2.0) * np.arange(half, dtype=np.float32))).astype(np.float32) / np.float32(half)
    angle = (np.arange(TOKENS, dtype=np.float32)[:, None] * theta[None, :].astype(np.float32)).astype(np.float32)
    sign = np.tile(np.array([-1.0, 1.0], np.float32), half)[:, None]
    rope = np.stack([np.repeat(np.cos(angle).T, 2, axis=0), np.repeat(np.sin(angle).T, 2, axis=0) * sign]).astype(np.float32)

    def partner(a):
        return a.reshape(*a.shape[:-1], half, 2)[..., ::-1].reshape(a.shape)

    def by_partition(w):
        return w.reshape(EXPERTS, -1, 128, w.shape[-1]).transpose(0, 2, 1, 3).reshape(EXPERTS, 128, PIECE)

    def columns(a):
        return a.reshape(-1, 128).T
    a = {k[len("L0_attn_"):]: t for k, t in x.items() if k.startswith("L0_attn_")}
    arrays = {
        "patches": patches,
        "consts": consts,
        "w_proj": x["L0_tok_W_proj"],
        "rows_pack": np.concatenate([x["L0_tok_ln2_g"], x["L0_tok_ln2_b"], x["L0_tok_cls_token"].reshape(-1), x["L0_tok_b_proj"],
                                     a["Wu_v_b"], a["Wo_b"], x["L0_ffn_br"]]),
        "pos": x["L0_tok_pos_emb"][0],
        "wd": np.concatenate([a["Wd_q_w"], a["Wd_kv_w"]], 1),
        "wq": np.concatenate([a["Wq_r_w"], partner(a["Wq_r_w"]), a["Wu_q_w"]], 1),
        "wk": np.concatenate([a["Wk_r_w"], partner(a["Wk_r_w"]), a["Wu_k_w"]], 0),
        "wv_o": np.concatenate([a["Wu_v_w"], a["Wo_w"]], 0),
        "cols_pack": np.concatenate([columns(a["Wd_q_b"]), columns(a["Wd_kv_b"]),
                                     columns(a["Wk_r_b"]), columns(partner(a["Wk_r_b"])), columns(a["Wu_k_b"]),
                                     columns(a["Wq_r_b"]), columns(partner(a["Wq_r_b"])), columns(a["Wu_q_b"]),
                                     columns(x["L0_tok_ln1_g"]), columns(x["L0_tok_ln1_b"])], 1),
        "rope": rope,
        "w_router": x["L0_ffn_Wr"],
        "expert_weights": np.stack([by_partition(x["L0_ffn_Wi"]), by_partition(x["L0_ffn_Wg"]), by_partition(x["L0_ffn_Wo"])],
                                   1).reshape(PIECES * 128, PIECE),
        "expert_bias": np.concatenate([x[k].reshape(-1) for k in ("L0_ffn_bi", "L0_ffn_bo")]).reshape(128, BIAS_COLS),
        "expert_rows": np.concatenate([x["L0_ffn_gamma"], x["L0_ffn_beta"], x["L0_ffn_bg"]], 1),
    }
    arrays = {k: np.ascontiguousarray(t) for k, t in arrays.items()}
    f32 = mybir.dt.float32
    nc = bacc.Bacc("TRN2", target_bir_lowering=False, num_devices=1)
    args = {k: nc.dram_tensor(k, t.shape, f32, kind="ExternalInput").ap() for k, t in arrays.items()}
    args["out"] = nc.dram_tensor("out", (ALL_TOKENS + 128, DIM), f32, kind="ExternalOutput").ap()
    args["x2_rows"] = nc.dram_tensor("x2_rows", (ALL_TOKENS + 128, DIM), f32, kind="Internal").ap()
    for part in ("weight_hi", "weight_lo"):
        args[part] = nc.dram_tensor(part, (PIECES * 128, PIECE), f32, kind="Internal").ap()
    args["bias_parts"] = nc.dram_tensor("bias_parts", (2, 128 * BIAS_COLS), f32, kind="Internal").ap()
    build(nc, **args)
    r = run(nc, [arrays], core_ids=[0])
    return r.results[0]["out"][:ALL_TOKENS].reshape(IMAGES, TOKENS, DIM)
```
